# Optimizing a Trainium2 kernel written in Bass

```python
import numpy as np
import jax
import jax.numpy as jnp

def _softmax(x, axis=-1):
    return jax.nn.softmax(x, axis=axis)

def _gelu(x):
    return jax.nn.gelu(x, approximate=True)

def _silu(x):
    return jax.nn.silu(x)

def _sigmoid(x):
    return jax.nn.sigmoid(x)

def _layernorm(x, axis=-1, eps=1e-05):
    m = jnp.mean(x, axis=axis, keepdims=True)
    v = jnp.var(x, axis=axis, keepdims=True)
    return (x - m) / jnp.sqrt(v + eps)

def _scatter_add(tgt, idx, src, axis=0):
    return tgt.at[idx].add(src)

def _segment_sum(src, seg, n):
    return jax.ops.segment_sum(src, seg, n)
kernel_name = 'mk_seq_postln_d2_jaxref_r8_15b184'

def setup_inputs(seed: int=0):
    np.random.seed(seed)
    _w = jnp.asarray

    def _L0_attn_setup():
        import jax, jax.numpy as jnp
        import numpy as np
        B, T, D, H = (1, 512, 128, 16)
        DK = D // H
        SCALE = 1.0 / float(np.sqrt(DK))
        NEG = -1000000000.0
        key = jax.random.key(seed)
        k1, k2, k3 = jax.random.split(key, 3)
        x = jax.random.normal(k1, (B, T, D), dtype=jnp.float32)
        Wqkv = jax.random.normal(k2, (3 * D, D), dtype=jnp.float32) * 0.02
        Wout = jax.random.normal(k3, (D, D), dtype=jnp.float32) * 0.02
        return {'x': x, 'Wqkv': Wqkv, 'Wout': Wout}
    _L0_attn_in = _L0_attn_setup()

    def _L0_ffn_setup():
        import jax, jax.numpy as jnp
        import numpy as np
        B, S, D, F, E, K = (2, 256, 128, 256, 8, 2)
        key = jax.random.key(seed)
        ks = jax.random.split(key, 5)
        scale = 0.02
        return {'x': jax.random.normal(ks[0], (B, S, D), dtype=jnp.float32), 'Wg': jax.random.normal(ks[1], (E, D), dtype=jnp.float32) * scale, 'W1': jax.random.normal(ks[2], (E, F, D), dtype=jnp.float32) * scale, 'W2': jax.random.normal(ks[3], (E, F, D), dtype=jnp.float32) * scale, 'W3': jax.random.normal(ks[4], (E, D, F), dtype=jnp.float32) * scale}
    _L0_ffn_in = _L0_ffn_setup()

    def _L1_attn_setup():
        import jax, jax.numpy as jnp
        import numpy as np
        DIM = 128
        NUM_HEADS = 16
        HEAD_DIM = DIM // NUM_HEADS

        def _rope_tables(seq_len, dim, dtype):
            inv_freq = 1.0 / 10000.0 ** (jnp.arange(0, dim, 2, dtype=jnp.float32) / dim)
            t = jnp.arange(seq_len, dtype=jnp.float32)
            freqs = jnp.outer(t, inv_freq)
            return (jnp.cos(freqs).astype(dtype), jnp.sin(freqs).astype(dtype))

        def _apply_rope(x, cos_emb, sin_emb):
            x1 = x[..., 0::2]
            x2 = x[..., 1::2]
            return jnp.concatenate((x1 * cos_emb - x2 * sin_emb, x1 * sin_emb + x2 * cos_emb), axis=-1)
        key = jax.random.key(seed)
        k_x, k_qkv, k_out, k_b = jax.random.split(key, 4)
        B, S, D = (2, 256, DIM)
        x = jax.random.normal(k_x, (B, S, D), dtype=jnp.float32)
        w_qkv = jax.random.normal(k_qkv, (3 * D, D), dtype=jnp.float32) * (1.0 / np.sqrt(D))
        w_out = jax.random.normal(k_out, (D, D), dtype=jnp.float32) * (1.0 / np.sqrt(D))
        b_out = jax.random.normal(k_b, (D,), dtype=jnp.float32) * 0.01
        return {'x': x, 'w_qkv': w_qkv, 'w_out': w_out, 'b_out': b_out}
    _L1_attn_in = _L1_attn_setup()

    def _L1_ffn_setup():
        import jax, jax.numpy as jnp
        import numpy as np
        key = jax.random.key(seed)
        ks = jax.random.split(key, 6)
        B, L, D, E = (4, 256, 128, 4)
        H = 4 * D
        x = jax.random.normal(ks[0], (B, L, D), dtype=jnp.float32)
        rW1 = jax.random.normal(ks[1], (D, 2 * D), dtype=jnp.float32) * (2.0 / D) ** 0.5
        rb1 = jnp.zeros((2 * D,), dtype=jnp.float32)
        rW2 = jax.random.normal(ks[2], (2 * D, E), dtype=jnp.float32) * (2.0 / (2 * D)) ** 0.5
        rb2 = jnp.zeros((E,), dtype=jnp.float32)
        We1 = jax.random.normal(ks[3], (E, D, H), dtype=jnp.float32) * (2.0 / D) ** 0.5
        be1 = jnp.zeros((E, H), dtype=jnp.float32)
        We2 = jax.random.normal(ks[4], (E, H, D), dtype=jnp.float32) * (2.0 / H) ** 0.5
        be2 = jnp.zeros((E, D), dtype=jnp.float32)
        return {'x': x, 'rW1': rW1, 'rb1': rb1, 'rW2': rW2, 'rb2': rb2, 'We1': We1, 'be1': be1, 'We2': We2, 'be2': be2}
    _L1_ffn_in = _L1_ffn_setup()
    _d = {'L0_attn_x': _L0_attn_in['x'], 'L0_attn_Wqkv': _L0_attn_in['Wqkv'], 'L0_attn_Wout': _L0_attn_in['Wout'], 'L0_ffn_Wg': _L0_ffn_in['Wg'], 'L0_ffn_W1': _L0_ffn_in['W1'], 'L0_ffn_W2': _L0_ffn_in['W2'], 'L0_ffn_W3': _L0_ffn_in['W3'], 'L1_attn_w_qkv': _L1_attn_in['w_qkv'], 'L1_attn_w_out': _L1_attn_in['w_out'], 'L1_attn_b_out': _L1_attn_in['b_out'], 'L1_ffn_rW1': _L1_ffn_in['rW1'], 'L1_ffn_rb1': _L1_ffn_in['rb1'], 'L1_ffn_rW2': _L1_ffn_in['rW2'], 'L1_ffn_rb2': _L1_ffn_in['rb2'], 'L1_ffn_We1': _L1_ffn_in['We1'], 'L1_ffn_be1': _L1_ffn_in['be1'], 'L1_ffn_We2': _L1_ffn_in['We2'], 'L1_ffn_be2': _L1_ffn_in['be2']}
    _x0 = _d['L0_attn_x']
    _d['L0_attn_x'] = jax.random.normal(jax.random.fold_in(jax.random.key(seed), 1), (4, 1024, 128), dtype=_x0.dtype)
    del _x0
    return _d

def reference(L0_attn_x, L0_attn_Wqkv, L0_attn_Wout, L0_ffn_Wg, L0_ffn_W1, L0_ffn_W2, L0_ffn_W3, L1_attn_w_qkv, L1_attn_w_out, L1_attn_b_out, L1_ffn_rW1, L1_ffn_rb1, L1_ffn_rW2, L1_ffn_rb2, L1_ffn_We1, L1_ffn_be1, L1_ffn_We2, L1_ffn_be2):

    def _L0_attn_ref(x, Wqkv, Wout):
        import jax, jax.numpy as jnp
        import numpy as np
        B, T, D, H = (1, 512, 128, 16)
        DK = D // H
        SCALE = 1.0 / float(np.sqrt(DK))
        NEG = -1000000000.0
        b, t, d = x.shape
        qkv = jnp.einsum('btd,ed->bte', x, Wqkv)
        qkv = qkv.reshape(b, t, 3, H, DK).transpose(2, 0, 3, 1, 4)
        q, k, v = (qkv[0], qkv[1], qkv[2])
        scores = jnp.einsum('bhtd,bhsd->bhts', q, k) * SCALE
        scores = jnp.clip(scores, -10.0, 10.0)
        mask = jnp.triu(jnp.full((t, t), NEG, dtype=scores.dtype), k=1)
        scores = scores + mask[None, None, :, :]
        attn = jax.nn.softmax(scores, axis=-1)
        out = jnp.einsum('bhts,bhsd->bhtd', attn, v)
        out = out.transpose(0, 2, 1, 3).reshape(b, t, d)
        return jnp.einsum('btd,ed->bte', out, Wout)

    def _L0_ffn_ref(x, Wg, W1, W2, W3):
        import jax, jax.numpy as jnp
        import numpy as np
        B, S, D, F, E, K = (2, 256, 128, 256, 8, 2)
        k = K
        scores = jnp.einsum('bsd,ed->bse', x, Wg)
        topk_scores, topk_idx = jax.lax.top_k(scores, k)
        topk_probs = jax.nn.softmax(topk_scores, axis=-1)
        h1 = jnp.einsum('bsd,efd->bsef', x, W1)
        h2 = jnp.einsum('bsd,efd->bsef', x, W2)
        hidden = jax.nn.silu(h1) * h2
        expert_out = jnp.einsum('bsef,edf->bsed', hidden, W3)
        onehot = jax.nn.one_hot(topk_idx, scores.shape[-1], dtype=x.dtype)
        gating = jnp.einsum('bsk,bske->bse', topk_probs, onehot)
        return jnp.einsum('bse,bsed->bsd', gating, expert_out)

    def _L1_attn_ref(x, w_qkv, w_out, b_out):
        import jax, jax.numpy as jnp
        import numpy as np
        DIM = 128
        NUM_HEADS = 16
        HEAD_DIM = DIM // NUM_HEADS

        def _rope_tables(seq_len, dim, dtype):
            inv_freq = 1.0 / 10000.0 ** (jnp.arange(0, dim, 2, dtype=jnp.float32) / dim)
            t = jnp.arange(seq_len, dtype=jnp.float32)
            freqs = jnp.outer(t, inv_freq)
            return (jnp.cos(freqs).astype(dtype), jnp.sin(freqs).astype(dtype))

        def _apply_rope(x, cos_emb, sin_emb):
            x1 = x[..., 0::2]
            x2 = x[..., 1::2]
            return jnp.concatenate((x1 * cos_emb - x2 * sin_emb, x1 * sin_emb + x2 * cos_emb), axis=-1)
        B, S, D = x.shape
        H, hd = (NUM_HEADS, HEAD_DIM)
        qkv = jnp.einsum('bsd,ed->bse', x, w_qkv)
        q, k, v = jnp.split(qkv, 3, axis=-1)
        q, k, v = (t.reshape(B, S, H, hd).transpose(0, 2, 1, 3) for t in (q, k, v))
        cos_emb, sin_emb = _rope_tables(S, hd, x.dtype)
        q = _apply_rope(q, cos_emb, sin_emb)
        k = _apply_rope(k, cos_emb, sin_emb)
        scores = jnp.einsum('bhqd,bhkd->bhqk', q, k) / jnp.sqrt(jnp.asarray(hd, x.dtype))
        attn = jax.nn.softmax(scores, axis=-1)
        out = jnp.einsum('bhqk,bhkd->bhqd', attn, v)
        out = out.transpose(0, 2, 1, 3).reshape(B, S, D)
        return jnp.einsum('bsd,ed->bse', out, w_out) + b_out

    def _L1_ffn_ref(x, rW1, rb1, rW2, rb2, We1, be1, We2, be2):
        import jax, jax.numpy as jnp
        import numpy as np
        E = We1.shape[0]
        top_k = min(2, E)
        rh = jax.nn.gelu(x @ rW1 + rb1, approximate=False)
        router_logits = rh @ rW2 + rb2
        router_probs = jax.nn.softmax(router_logits, axis=-1)
        expert_weights, expert_indices = jax.lax.top_k(router_probs, top_k)
        one_hot = jax.nn.one_hot(expert_indices, E, dtype=x.dtype)
        token_mask = one_hot.sum(axis=2)
        combine_w = (one_hot * expert_weights[..., None]).sum(axis=2)
        out = jnp.zeros_like(x)
        for e in range(E):
            xi = x * token_mask[..., e:e + 1]
            h = jax.nn.gelu(xi @ We1[e] + be1[e], approximate=False)
            yo = h @ We2[e] + be2[e]
            out = out + yo * combine_w[..., e:e + 1]
        return out
    x = L0_attn_x
    x = _layernorm(x + _L0_attn_ref(x, L0_attn_Wqkv, L0_attn_Wout), axis=-1)
    x = _layernorm(x + _L0_ffn_ref(x, L0_ffn_Wg, L0_ffn_W1, L0_ffn_W2, L0_ffn_W3), axis=-1)
    x = _layernorm(x + _L1_attn_ref(x, L1_attn_w_qkv, L1_attn_w_out, L1_attn_b_out), axis=-1)
    x = _layernorm(x + _L1_ffn_ref(x, L1_ffn_rW1, L1_ffn_rb1, L1_ffn_rW2, L1_ffn_rb2, L1_ffn_We1, L1_ffn_be1, L1_ffn_We2, L1_ffn_be2), axis=-1)
    return x

_drawn_inputs = setup_inputs


def setup_inputs(seed=0):
    import zlib

    import numpy as np

    out = dict(_drawn_inputs(seed))
    spreads = {'L1_ffn_rb1': (0.0, 0.1),
     'L1_ffn_rb2': (0.0, 0.1),
     'L1_ffn_be1': (0.0, 0.1),
     'L1_ffn_be2': (0.0, 0.1)}
    factors = {'L0_attn_Wqkv': 2.831, 'L0_attn_Wout': 3.474, 'L0_ffn_Wg': 2.697, 'L0_ffn_W1': 2.708}
    for name, (base, spread) in spreads.items():
        noise = np.random.default_rng([zlib.crc32(name.encode()), seed]).standard_normal(out[name].shape)
        drawn = base * np.exp(spread * noise) if base else spread * noise
        out[name] = jnp.asarray(drawn.astype(out[name].dtype))
    for name, factor in factors.items():
        out[name] = (out[name] * factor).astype(out[name].dtype)
    return out
```

```python
from contextlib import ExitStack

import numpy as np

import concourse.bass as bass
from concourse import mybir

ALU = mybir.AluOpType
ACT = mybir.ActivationFunctionType
AXX = mybir.AxisListType.X
F32 = mybir.dt.float32
F32R = mybir.dt.float32r
U32 = mybir.dt.uint32

P = 128
B, T, D, H = 4, 1024, 128, 16
DK = D // H
NTOK = B * T
CH = 512
TPC = CH // P
CPB = T // CH
KT = T // P
NT = NTOK // P
HG = 4
G = H // HG
NG = B * G
SLOT = 32
E0, F0 = 8, 256
E1, F1 = 4, 512
NH = E0 * F0 // P
assert NH == E1 * F1 // P
SCALE = float(DK) ** -0.5
CLIP = 10.0
EPS = 1e-5
NS = 2


def steps_of(causal):
    out = []
    for qc in range(CPB):
        for kt in range(KT if not causal else (qc + 1) * TPC):
            for hp in range(HG // 2):
                q0 = max(qc * CH, kt * P) if causal else qc * CH
                out.append([qc, kt, hp, q0, (qc + 1) * CH - q0, False])
        out[-1][5] = True
    return out


class Layer:

    def __init__(self, n, sem):
        self.n = n
        self.causal = n == 0
        self.steps = steps_of(self.causal)
        self.S = len(self.steps)
        self.last = [s for s, x in enumerate(self.steps) if x[5]]
        self.k_rows = 4 * DK if self.causal else 3 * DK + 2
        first1 = self.last[0] + 1
        self.norm_prev, self.proj_prev = 2, 5
        self.norm_0, self.proj_0 = first1 + 2, first1 + 5
        self.turn = [] if self.causal else [27, 28]
        self.jobs0 = 2 + len(self.turn)
        self.jobs = 4 + len(self.turn)
        self.max_jobs = 0 if self.causal else KT * HG * 2
        self.stacks_loaded = [sem(f"l{n}_stacks_loaded{p}") for p in range(2)]
        self.aug_loaded = [sem(f"l{n}_aug_loaded{p}") for p in range(2)]
        self.v_staged = sem(f"l{n}_v_staged")
        self.scores_ready = sem(f"l{n}_scores_ready")
        self.exp_done = sem(f"l{n}_exp_done")
        self.clip_done = sem(f"l{n}_clip_done")
        self.pv_done = sem(f"l{n}_pv_done")
        self.o_free = sem(f"l{n}_o_free")
        self.o_saved = sem(f"l{n}_o_saved")
        self.on_ready = sem(f"l{n}_on_ready")
        self.spare_ready = sem(f"l{n}_spare_ready")
        self.spare_free = sem(f"l{n}_spare_free")
        self.smax_ready = sem(f"l{n}_smax_ready")
        self.smax_free = sem(f"l{n}_smax_free")
        self.negmax_ready = sem(f"l{n}_negmax_ready")
        self.turned = sem(f"l{n}_turned")
        self.chain = sem(f"l{n}_chain")

    def spare_base(self, i):
        return self.jobs0 + len(self.turn) + self.jobs * (i - 1)

    def max_jobs_at(self, s):
        if self.causal or s < 4:
            return range(0)
        return range(min(3 * (s - 4), self.max_jobs), min(3 * (s - 3), self.max_jobs))


class Chain:

    def __init__(self, eng, sem):
        self.eng, self.sem, self.base, self.n = eng, sem, 0, 0

    def at(self, base):
        self.base, self.n = base, 0

    def link(self, ins, apart=None):
        self.n += 1
        ins.then_inc(self.sem, 1)
        self.eng.wait_ge(self.sem, self.base + self.n)
        if apart is not None:
            self.eng.sem_inc(apart, 1)


def build_program(nc, d, out):
    with ExitStack() as ctx:
        def sb(name, shape, dt=F32):
            return ctx.enter_context(nc.sbuf_tensor(name, shape, dt))

        def sem(name):
            return ctx.enter_context(nc.semaphore(name))

        bank = [ctx.enter_context(nc.psum_tensor(f"bank{i}", [P, CH], F32)) for i in range(4)]
        score = [ctx.enter_context(nc.psum_tensor(f"score{i}", [P, 2, CH], F32)) for i in range(NS)]
        hbank = [score[0][:, 0, :], score[0][:, 1, :], score[1][:, 0, :], score[1][:, 1, :]]

        ident = sb("ident", [P, P])
        den_pick = sb("den_pick", [P, P])
        tri = sb("tri", [P, P])
        expert_row = sb("expert_row", [E0, E0, P])
        iota8 = sb("iota8", [P, E0])
        w_qkv0 = sb("w_qkv0", [P, 3, P])
        w_qkv1 = sb("w_qkv1", [P, 5, P])
        w_o = [sb(f"w_o{n}", [P, G, P]) for n in range(2)]
        rope_a = sb("rope_a", [P, T])
        rope_b = sb("rope_b", [P, T])
        b_o1 = sb("b_o1", [P, D])
        wg = sb("wg", [P, E0])
        w1 = sb("w1", [P, E0, F0])
        w2 = sb("w2", [P, E0, F0])
        w3 = sb("w3", [P, NH, P])
        rw1 = sb("rw1", [P, F0])
        rb1 = sb("rb1", [P, 2])
        rw2 = sb("rw2", [P, 2, E1])
        rb2 = sb("rb2", [P, E1])
        we1 = sb("we1", [P, E1, F1])
        be1 = sb("be1", [P, NH])
        we2 = sb("we2", [P, NH, P])
        be2 = sb("be2", [E1, D])

        x_tm = sb("x_tm", [P, NT, D])
        v_all = sb("v_all", [P, NT, D])
        k_st = [sb(f"k_st{p}", [P, T], F32R) for p in range(2)]
        q_st = [sb(f"q_st{p}", [P, T], F32R) for p in range(2)]
        v_st = [sb(f"v_st{p}", [P, KT, HG, SLOT]) for p in range(2)]
        probs = [sb(f"probs{p}", [P, 2, CH]) for p in range(NS)]
        o_sb = sb("o_sb", [P, CH])
        o_rcp = sb("o_rcp", [P, CH])
        o_n = sb("o_n", [P, CH])
        negmax_h = sb("negmax_h", [P, KT, HG, 2])
        negmax = sb("negmax", [P, KT, HG])
        negmax2 = sb("negmax2", [P, KT, 2 * HG])
        negmax_t = sb("negmax_t", [2 * HG, T], F32R)
        xs = [sb(f"xs{i}", [P, TPC, D]) for i in range(2)]
        xt = [sb(f"xt{i}", [P, CH]) for i in range(2)]
        gate_bc = sb("gate_bc", [P, E0, CH])
        act_s = [sb(f"act_s{i}", [P, CH]) for i in range(2)]
        lin_u = [sb(f"lin_u{i}", [P, CH]) for i in range(2)]
        hid = [sb(f"hid{i}", [P, CH]) for i in range(2)]
        y_sb = sb("y_sb", [P, CH])
        res = sb("res", [P, TPC, D])
        rot = [sb(f"rot{i}", [P, CH]) for i in range(4)]
        qk_hi = [sb(f"qk_hi{i}", [P, CH], F32R) for i in range(2)]
        qk_lo = [sb(f"qk_lo{i}", [P, CH], F32R) for i in range(2)]
        st6 = sb("st6", [P, TPC, 6])
        mv = sb("mv", [P, TPC, 2])
        rstd = sb("rstd", [P, TPC])
        mhalf = sb("mhalf", [P, TPC])
        sc8 = sb("sc8", [P, TPC, 8])
        mx8 = sb("mx8", [P, TPC, 8])
        ix8 = sb("ix8", [P, TPC, 8], U32)
        ixf = sb("ixf", [P, TPC, 8])
        lead = sb("lead", [P, TPC])
        e_sm = sb("e_sm", [P, TPC, E1])
        p12 = sb("p12", [P, 2, TPC])
        gts = sb("gts", [P, 2, TPC, 8])
        gate_t = sb("gate_t", [E0, CH])
        rh = sb("rh", [P, 2, CH])

        q_scr = [nc.dram_tensor(f"q_scr{n}", [B, 4, P, T], F32, kind="Internal").ap() for n in range(2)]
        k_scr = [nc.dram_tensor(f"k_scr{n}", [B, 4, P, T], F32, kind="Internal").ap() for n in range(2)]

        const_loaded = sem("const_loaded")
        w_loaded = sem("w_loaded")
        fills = sem("fills")
        apart = sem("apart")
        apart_pool = sem("apart_pool")
        ones_stored = sem("ones_stored")
        layers = [Layer(n, sem) for n in range(2)]

        class Stage:

            def __init__(self, n):
                self.x_turned = sem(f"st{n}_x_turned")
                self.xt_ready = sem(f"st{n}_xt_ready")
                self.qkv_ready = sem(f"st{n}_qkv_ready")
                self.halves_hi = sem(f"st{n}_halves_hi")
                self.halves_lo = sem(f"st{n}_halves_lo")
                self.v_saved = sem(f"st{n}_v_saved")
                self.stored = sem(f"st{n}_stored")
                self.done = sem(f"st{n}_done")
                if n == 0:
                    self.x_in = sem("st0_x_in")
                    return
                self.norm = sem(f"st{n}_norm")
                self.router_in = sem(f"st{n}_router_in")
                self.gate_pre = sem(f"st{n}_gate_pre")
                self.gate_exp = sem(f"st{n}_gate_exp")
                self.gates = sem(f"st{n}_gates")
                self.gates_turned = sem(f"st{n}_gates_turned")
                self.gate_t = sem(f"st{n}_gate_t")
                self.gbc_ready = sem(f"st{n}_gbc_ready")
                self.gbc_saved = sem(f"st{n}_gbc_saved")
                self.h_ready = sem(f"st{n}_h_ready")
                self.s_done = sem(f"st{n}_s_done")
                self.hid_ready = sem(f"st{n}_hid_ready")
                self.y_done = sem(f"st{n}_y_done")
                self.y_saved = sem(f"st{n}_y_saved")
                self.y_turned = sem(f"st{n}_y_turned")
                self.stats = sem(f"st{n}_stats")
                self.rstd = sem(f"st{n}_rstd")
                self.stats2 = sem(f"st{n}_stats2")
                self.rstd2 = sem(f"st{n}_rstd2")
                self.norm2 = sem(f"st{n}_norm2")
                self.chain = sem(f"st{n}_chain")
                self.pool_chain = sem(f"st{n}_pool_chain")
                if n == 1:
                    self.u_done = sem("st1_u_done")
                    self.x_kept = sem("st1_x_kept")
                    self.rot_done = sem("st1_rot_done")
                    self.rot_sum = sem("st1_rot_sum")
                    self.xt2_turned = sem("st1_xt2_turned")
                    self.xt2_ready = sem("st1_xt2_ready")
                else:
                    self.rh_ready = sem("st2_rh_ready")

        stages = [Stage(n) for n in range(3)]

        block = ctx.enter_context(nc.Block())

        CONSTS = [(ident, "ident"), (den_pick, "den_pick"), (tri, "tri"), (expert_row, "expert_row"),
                  (iota8, "iota8"), (w_qkv0, "w_qkv0"), (w_o[0], "w_o0"), (w_o[1], "w_o1")]
        WEIGHTS = [(w_qkv1, "w_qkv1"), (rope_a, "rope_a"), (rope_b, "rope_b"), (wg, "wg"), (w1, "w1"),
                   (w2, "w2"), (w3, "w3"), (rw1, "rw1"), (rb1, "rb1"), (rw2, "rw2"), (we1, "we1"),
                   (be1, "be1"), (we2, "we2"), (be2, "be2")]
        ALL_CONSTS = 16 * (len(CONSTS) + 1)
        ALL_W = 16 * (len(WEIGHTS) + 2)
        x_tiles = d["x"].rearrange("(t p) c -> p t c", p=P)
        out_tiles = out.rearrange("(t p) c -> p t c", p=P)

        def bg(i):
            return i // G, i % G

        def pe_max_job(pe, L, i, p, m):
            qt, j, half = m // (HG * 2), m // 2 % HG, m % 2
            pe.wait_ge(L.smax_free, i * L.max_jobs + m + 1)
            r = slice(SLOT * j, SLOT * j + 3 * DK)
            nc.tensor.matmul(bank[1 + m % 2][:, :], q_st[p][r, qt * P:(qt + 1) * P],
                             k_st[p][r, half * CH:(half + 1) * CH],
                             start=True, stop=True).then_inc(L.smax_ready, 1)

        def pe_turn(pe, L, i, half, job):
            if half == 0:
                pe.wait_ge(L.negmax_ready, i + 1)
            pe.wait_ge(L.spare_free, job + 1)
            for t in range(TPC):
                last = nc.tensor.transpose(bank[3][0:2 * HG, t * P:(t + 1) * P],
                                           negmax2[:, half * TPC + t, :], ident[:, :])
            last.then_inc(L.spare_ready, 1)

        def pe_norm(pe, L, chunk, job):
            pe.wait_ge(L.o_saved, chunk + 1)
            pe.wait_ge(L.spare_free, job + 1)
            nc.tensor.matmul(bank[3][:, :], den_pick[:, :], o_sb[:, :], start=True,
                             stop=True).then_inc(L.spare_ready, 1)

        def pe_proj(pe, L, chunk, job, g):
            pe.wait_ge(L.on_ready, chunk + 1)
            pe.wait_ge(L.spare_free, job + 1)
            for t in range(TPC):
                last = nc.tensor.matmul(bank[3][:, t * P:(t + 1) * P], o_n[:, t * P:(t + 1) * P],
                                        w_o[L.n][:, g, :], start=True, stop=True)
            last.then_inc(L.spare_ready, 1)

        def pe_scores(pe, L, i, p, s):
            qc, kt, hp, q0, w, _ = L.steps[s]
            pe.wait_ge(L.exp_done, i * L.S + s + 1)
            for a in range(2):
                j = 2 * hp + a
                r = slice(SLOT * j, SLOT * j + L.k_rows)
                last = nc.tensor.matmul(score[s % NS][:, a, 0:w], k_st[p][r, kt * P:(kt + 1) * P],
                                        q_st[p][r, q0:q0 + w], start=True, stop=True)
            last.then_inc(L.scores_ready, 1)

        def pe_round(pe, L, i, p, prev, nxt):
            b, g = bg(i)
            if L.causal:
                pe.wait_ge(L.stacks_loaded[p], 16 * 2 * HG * (i // 2 + 1))
            else:
                pe.wait_ge(L.aug_loaded[p], 16 * 2 * (i // 2 + 1))
            pe.wait_ge(L.v_staged, i + 1)
            job = 0 if prev else None
            base = L.spare_base(i) if prev else len(L.turn)
            pe_scores(pe, L, i, p, 0)
            for s, (qc, kt, hp, q0, w, last_step) in enumerate(L.steps):
                if s + 1 < L.S:
                    pe_scores(pe, L, i, p, s + 1)
                if L.causal:
                    pe.wait_ge(L.clip_done, i * L.S + s + 1)
                else:
                    pe.wait_ge(L.exp_done, NS + i * L.S + s + 1)
                if kt == 0 and hp == 0:
                    pe.wait_ge(L.o_free, CPB * i + qc + 1)
                for a in range(2):
                    j = 2 * hp + a
                    last = nc.tensor.matmul(bank[0][SLOT * j:SLOT * (j + 1), q0 - qc * CH:q0 - qc * CH + w],
                                            v_st[p][:, kt, j, :], probs[s % NS][:, a, 0:w],
                                            start=(kt == 0), stop=(s + 2 > L.last[qc]))
                last.then_inc(L.pv_done, 1)
                if nxt:
                    if s == 4 and not L.causal:
                        pe.wait_ge(L.stacks_loaded[1 - p], 16 * 2 * HG * ((i + 1) // 2 + 1))
                    for m in L.max_jobs_at(s):
                        pe_max_job(pe, L, i + 1, 1 - p, m)
                n0 = 2 if prev else 0
                if prev and s == L.norm_prev:
                    pe_norm(pe, L, CPB * i - 1, base)
                if prev and s == L.proj_prev:
                    pe_proj(pe, L, CPB * i - 1, base + 1, (i - 1) % G)
                if s == L.norm_0:
                    pe_norm(pe, L, CPB * i, base + n0)
                if s == L.proj_0:
                    pe_proj(pe, L, CPB * i, base + n0 + 1, g)
                if nxt and s in L.turn:
                    h = L.turn.index(s)
                    pe_turn(pe, L, i + 1, h, base + n0 + 2 + h)

        def pe_attention(pe, L):
            pe.wait_ge(L.stacks_loaded[0], 16 * 2 * HG)
            if not L.causal:
                for m in range(L.max_jobs):
                    pe_max_job(pe, L, 0, 0, m)
                for h in range(2):
                    pe_turn(pe, L, 0, h, h)
            pe_round(pe, L, 0, 0, False, True)
            with pe.Fori(0, NG // 2 - 1) as u:
                pe_round(pe, L, 2 * u + 1, 1, True, True)
                pe_round(pe, L, 2 * u + 2, 0, True, True)
            pe_round(pe, L, NG - 1, 1, True, False)
            end = L.spare_base(NG - 1) + 4
            pe_norm(pe, L, CPB * NG - 1, end)
            pe_proj(pe, L, CPB * NG - 1, end + 1, G - 1)

        def act_exp(act, L, i, s):
            w = L.steps[s][4]
            act.wait_ge(L.scores_ready, i * L.S + s + 1)
            act.wait_ge(L.pv_done, i * L.S + s + 1)
            nc.scalar.activation(probs[s % NS][:, :, 0:w], score[s % NS][:, :, 0:w], ACT.Exp,
                                 scale=SCALE).then_inc(L.exp_done, 1)

        def act_turn(act, L, half, job):
            act.wait_ge(L.spare_ready, job + 1)
            nc.scalar.activation(negmax_t[:, half * CH:(half + 1) * CH], bank[3][0:2 * HG, :],
                                 ACT.Copy).then_inc(L.spare_free, 1)

        def act_round(act, L, i, p, prev, nxt):
            base = (L.spare_base(i) + 4) if prev else len(L.turn) + 2
            act_exp(act, L, i, 0)
            for s in range(L.S):
                if s + 1 < L.S:
                    act_exp(act, L, i, s + 1)
                if nxt and s in L.turn:
                    h = L.turn.index(s)
                    if h == 0:
                        act.wait_ge(L.aug_loaded[p], 32 * (i // 2 + 1))
                    act_turn(act, L, h, base + h)

        def act_attention(act, L):
            if not L.causal:
                act_turn(act, L, 0, 0)
                act_turn(act, L, 1, 1)
            act_round(act, L, 0, 0, False, True)
            with act.Fori(0, NG // 2 - 1) as u:
                act_round(act, L, 2 * u + 1, 1, True, True)
                act_round(act, L, 2 * u + 2, 0, True, True)
            act_round(act, L, NG - 1, 1, True, False)

        def dve_clip(dve, L, i, s):
            qc, kt, hp, q0, w, _ = L.steps[s]
            dve.wait_ge(L.exp_done, NS + i * L.S + s + 1)
            e = probs[s % NS]
            diagonal = q0 == kt * P
            ins = nc.vector.tensor_scalar(e[:, :, 0:w], e[:, :, 0:w], float(np.exp(-CLIP)),
                                          float(np.exp(CLIP)), ALU.max, ALU.min)
            if diagonal:
                dve_chain[0].link(ins)
                ins = nc.vector.tensor_tensor(e[:, :, 0:P], e[:, :, 0:P],
                                              tri[:, None, :].broadcast_to([P, 2, P]), ALU.mult)
            ins.then_inc(L.clip_done, 1)

        dve_chain = [None]

        def dve_norm(dve, L, chunk, job):
            dve.wait_ge(L.spare_ready, job + 1)
            dve_chain[0].link(nc.vector.reciprocal(o_rcp[:, :], bank[3][:, :]))
            dve.sem_inc(L.spare_free, 1)
            dve.wait_ge(L.o_saved, chunk + 1)
            nc.vector.tensor_tensor(o_n[:, :], o_sb[:, :], o_rcp[:, :], ALU.mult).then_inc(L.on_ready, 1)

        def dve_proj(dve, L, job, tile):
            dve.wait_ge(L.spare_ready, job + 1)
            xv = x_tm[:, bass.ds(tile, TPC), :]
            nc.vector.tensor_tensor(xv, xv, bank[3][:, :].rearrange("p (t c) -> p t c", c=D),
                                    ALU.add).then_inc(L.spare_free, 1)

        def dve_max_job(dve, L, i, m):
            qt, j, half = m // (HG * 2), m // 2 % HG, m % 2
            dve.wait_ge(L.smax_ready, i * L.max_jobs + m + 1)
            nc.vector.tensor_reduce(negmax_h[:, qt, j, half:half + 1], bank[1 + m % 2][:, :], AXX, ALU.max,
                                    negate=True).then_inc(L.smax_free, 1)

        def dve_negmax(dve, L, i):
            dve.wait_ge(L.smax_free, NS + (i + 1) * L.max_jobs)
            c = dve_chain[0]
            c.link(nc.vector.tensor_tensor(negmax[:, :, :], negmax_h[:, :, :, 0], negmax_h[:, :, :, 1], ALU.min))
            c.link(nc.vector.tensor_copy(negmax2[:, :, 0:HG].bitcast(F32R), negmax[:, :, :]))
            nc.vector.tensor_tensor(negmax2[:, :, HG:2 * HG].bitcast(F32R), negmax[:, :, :],
                                    negmax2[:, :, 0:HG], ALU.subtract).then_inc(L.negmax_ready, 1)

        def links(L, prev, nxt):
            n = (1 if prev else 0) + 1 + (2 if nxt and not L.causal else 0)
            return n + (sum(x[3] == x[1] * P for x in L.steps) if L.causal else 0)

        def dve_round(dve, L, i, prev, nxt):
            b, g = bg(i)
            base = L.spare_base(i) if prev else len(L.turn)
            n0 = 2 if prev else 0
            if L.causal:
                dve_clip(dve, L, i, 0)
            for s, (qc, kt, hp, q0, w, last_step) in enumerate(L.steps):
                if L.causal and s + 1 < L.S:
                    dve_clip(dve, L, i, s + 1)
                if last_step:
                    dve.wait_ge(L.pv_done, NS + i * L.S + s + 1)
                    if qc == 1 or prev:
                        dve.wait_ge(L.on_ready, CPB * i + qc)
                    nc.vector.tensor_copy(o_sb[:, :], bank[0][:, :]).then_inc(L.o_saved, 1)
                    dve.wait_ge(L.o_saved, CPB * i + qc + 1)
                    dve.sem_inc(L.o_free, 1)
                if nxt:
                    for m in L.max_jobs_at(s):
                        dve_max_job(dve, L, i + 1, m)
                    if not L.causal and s == 26:
                        dve_negmax(dve, L, i + 1)
                if prev and s == L.norm_prev:
                    dve_norm(dve, L, CPB * i - 1, base)
                if prev and s == L.proj_prev:
                    dve_proj(dve, L, base + 1, ((i - 1) // G) * KT + TPC)
                if s == L.norm_0:
                    dve_norm(dve, L, CPB * i, base + n0)
                if s == L.proj_0:
                    dve_proj(dve, L, base + n0 + 1, b * KT)

        def dve_attention(dve, L):
            c = dve_chain[0] = Chain(dve, L.chain)
            total = 0
            if not L.causal:
                for m in range(L.max_jobs):
                    dve_max_job(dve, L, 0, m)
                dve_negmax(dve, L, 0)
                total = 2
            c.at(total)
            dve_round(dve, L, 0, False, True)
            total += links(L, False, True)
            assert c.base + c.n == total
            per = links(L, True, True)
            with dve.Fori(0, NG // 2 - 1) as u:
                for k in range(2):
                    c.at(total + (2 * u + k) * per)
                    dve_round(dve, L, 2 * u + 1 + k, True, True)
                    assert c.n == per
            total += (NG - 2) * per
            c.at(total)
            dve_round(dve, L, NG - 1, True, False)
            end = L.spare_base(NG - 1) + 4
            dve_norm(dve, L, CPB * NG - 1, end)
            dve_proj(dve, L, end + 1, (B - 1) * KT + TPC)

        def sp_load_stacks(sp, L, i, p):
            b, g = bg(i)
            for scr, st, terms in ((k_scr, k_st, 4), (q_scr, q_st, 4 if L.causal else 3)):
                for j in range(HG):
                    src = scr[L.n][bass.ds(b, 1), 0:terms, bass.ds(g * HG * DK + j * DK, DK), :]
                    sp.dma_start(st[p][SLOT * j:SLOT * j + terms * DK, :].bitcast(F32),
                                 src.rearrange("b t c n -> (b t) c n")).then_inc(L.stacks_loaded[p], 16)

        def sp_load_aug(sp, L, i, p):
            sp.wait_ge(L.spare_free, 1 + (len(L.turn) if isinstance(i, int) and i == 0
                                          else L.spare_base(i)))
            for k in range(2):
                r = 3 * DK + k
                sp.dma_start(q_st[p][r:r + SLOT * (HG - 1) + 1:SLOT, :].bitcast(F32),
                             negmax_t[k * HG:(k + 1) * HG, :].bitcast(F32)).then_inc(L.aug_loaded[p], 16)

        def sp_attention(sp, L):
            sp_load_stacks(sp, L, 0, 0)
            if not L.causal:
                sp_load_aug(sp, L, 0, 0)
            sp_load_stacks(sp, L, 1, 1)
            if not L.causal:
                sp_load_aug(sp, L, 1, 1)
            with sp.Fori(0, NG // 2 - 1) as u:
                for k in range(2):
                    i = 2 * u + 2 + k
                    sp.wait_ge(L.pv_done, NS + (i - 1) * L.S)
                    sp_load_stacks(sp, L, i, k)
                    if not L.causal:
                        sp_load_aug(sp, L, i, k)

        def pool_attention(pool, L):
            for i in range(2):
                nc.gpsimd.tensor_copy(v_st[i][:, :, :, 0:DK],
                                      v_all[:, 0:KT, i * HG * DK:(i + 1) * HG * DK].rearrange(
                                          "p t (j c) -> p t j c", c=DK)).then_inc(L.v_staged, 1)
            with pool.Fori(0, NG // 2 - 1) as u:
                for k in range(2):
                    i = 2 * u + 2 + k
                    pool.wait_ge(L.pv_done, NS + (i - 1) * L.S)
                    b, g = bg(i)
                    nc.gpsimd.tensor_copy(v_st[k][:, :, :, 0:DK],
                                          v_all[:, bass.ds(b * KT, KT), bass.ds(g * HG * DK, HG * DK)].rearrange(
                                              "p t (j c) -> p t j c", c=DK)).then_inc(L.v_staged, 1)

        def pe_turn_tiles(dst, src):
            for t in range(TPC):
                last = nc.tensor.transpose(dst[:, t * P:(t + 1) * P], src[:, t, :], ident[:, :])
            return last

        def pe_qkv(pe, st, c, w, x, rope):
            n = 4 if rope else 2
            for a in range(n):
                last = nc.tensor.matmul(hbank[a], w[:, a, :], x[:, :], start=True, stop=True)
            for t in range(TPC):
                last = nc.tensor.matmul(bank[0][:, t * P:(t + 1) * P], x[:, t * P:(t + 1) * P], w[:, n, :],
                                        start=True, stop=True)
            last.then_inc(st.qkv_ready, 1)

        def sp_store_halves(sp, st, n, c, b, hh):
            sp.wait_ge(st.halves_lo, 2 * (c + 1))
            sp.wait_ge(st.halves_hi, 2 * (c + 1))
            for a, scr, order in ((0, q_scr, "hhll" if n == 0 else "hhl"), (1, k_scr, "hlhl" if n == 0 else "hlh")):
                for t, what in enumerate(order):
                    src = qk_hi[a] if what == "h" else qk_lo[a]
                    dst = scr[n][bass.ds(b, 1), t, :, hh * CH:(hh + 1) * CH].rearrange("b c n -> (b c) n")
                    sp.dma_start(dst, src[:, :].bitcast(F32)).then_inc(st.stored, 16)
        STORES = [8 * 16, 6 * 16]

        def dve_layernorm(dve, c_, x, o, pool_wait, pool_sig, val):
            for t in range(TPC):
                ins = nc.vector.bn_stats(st6[:, t, :], x[:, t, :])
            c_.link(ins, apart)
            for t in range(TPC):
                ins = nc.vector.bn_aggr(mv[:, t, :], st6[:, t, :])
            ins.then_inc(pool_wait, 1)
            dve.wait_ge(pool_wait, val)
            dve.wait_ge(pool_sig, val)
            for t in range(TPC):
                ins = nc.vector.tensor_scalar(o[:, t, :], x[:, t, :], mv[:, t, 0:1], rstd[:, t:t + 1],
                                              ALU.subtract, ALU.mult)
            return ins

        def pool_rstd(pool, pc, wait, sig, val):
            pool.wait_ge(wait, val)
            pool.sem_inc(apart_pool, 1)
            pc.link(nc.gpsimd.tensor_scalar(rstd[:, :], mv[:, :, 1], EPS, None, ALU.add))
            nc.gpsimd.tensor_tensor(rstd[:, :], rstd[:, :], mhalf[:, :], ALU.pow).then_inc(sig, 1)

        HPC = NH

        def pe_ffn_h(pe, st, c, n, layer):
            pe.wait_ge(st.s_done, c * HPC + n + 1)
            if layer == 0:
                pe.wait_ge(st.u_done, c * HPC + n + 1)
                e, f = n // 2, n % 2
                nc.tensor.matmul(hbank[n % 2], w1[:, e, f * P:(f + 1) * P], xt[0][:, :], start=True, stop=True)
                last = nc.tensor.matmul(hbank[2 + n % 2], w2[:, e, f * P:(f + 1) * P], xt[0][:, :],
                                        start=True, stop=True)
            else:
                e, f = n // 4, n % 4
                last = nc.tensor.matmul(hbank[n % 2], we1[:, e, f * P:(f + 1) * P], xt[0][:, :],
                                        start=True, stop=True)
            last.then_inc(st.h_ready, 1)

        def pe_ffn(pe, st, c, layer):
            w = w3 if layer == 0 else we2
            pe_ffn_h(pe, st, c, 0, layer)
            for n in range(HPC):
                if n + 1 < HPC:
                    pe_ffn_h(pe, st, c, n + 1, layer)
                pe.wait_ge(st.hid_ready, c * HPC + n + 1)
                nc.tensor.matmul(bank[0][:, :], w[:, n, :], hid[n % 2][:, :], start=(n == 0),
                                 stop=(layer == 0 and n == HPC - 1)).then_inc(st.y_done, 1)
            if layer == 1:
                nc.tensor.matmul(bank[0][:, :], be2[:, :], gate_t[0:E1, :], start=False,
                                 stop=True).then_inc(st.y_done, 1)
        YPC = [HPC, HPC + 1]

        def experts(layer):
            return E0 if layer == 0 else E1

        def pe_end_stage(pe, st, c, layer, hh):
            pe.wait_ge(st.norm, c + 1)
            pe.wait_ge(st.done, c + 1)
            pe_turn_tiles(bank[3], xs[0]).then_inc(st.x_turned, 1)
            pe.wait_ge(st.xt_ready, c + 1)
            if layer == 0:
                for t in range(TPC):
                    last = nc.tensor.matmul(bank[1][:, t * 8:t * 8 + 8], xt[0][:, t * P:(t + 1) * P], wg[:, :],
                                            start=True, stop=True)
                last.then_inc(st.router_in, 1)
            else:
                for f in range(2):
                    last = nc.tensor.matmul(hbank[f], rw1[:, f * P:(f + 1) * P], xt[0][:, :], start=True, stop=True)
                last.then_inc(st.h_ready, 1)
                pe.wait_ge(st.rh_ready, c + 1)
                for t in range(TPC):
                    for f in range(2):
                        last = nc.tensor.matmul(bank[1][:, t * E1:(t + 1) * E1], rh[:, f, t * P:(t + 1) * P],
                                                rw2[:, f, :], start=(f == 0), stop=(f == 1))
                last.then_inc(st.router_in, 1)
            pe.wait_ge(st.gates, c + 1)
            for t in range(TPC):
                last = nc.tensor.transpose(bank[2][0:8, t * P:(t + 1) * P], gts[:, 0, t, :], ident[:, :])
            last.then_inc(st.gates_turned, 1)
            pe.wait_ge(st.gate_t, c + 1)
            n_e = experts(layer)
            for e in range(n_e):
                pe.wait_ge(st.gbc_saved, c * n_e + e + 1)
                nc.tensor.matmul(bank[1 + e % 2][:, :], expert_row[:, e, :], gate_t[:, :], start=True,
                                 stop=True).then_inc(st.gbc_ready, 1)
            pe_ffn(pe, st, c, layer)
            pe.wait_ge(st.y_saved, c + 1)
            for t in range(TPC):
                last = nc.tensor.transpose(bank[3][:, t * P:(t + 1) * P], y_sb[:, t * P:(t + 1) * P], ident[:, :])
            last.then_inc(st.y_turned, 1)
            if layer == 0:
                pe.wait_ge(st.norm2, c + 1)
                pe_turn_tiles(bank[3], xs[1]).then_inc(st.xt2_turned, 1)
                pe.wait_ge(st.xt2_ready, c + 1)
                pe_qkv(pe, st, c, w_qkv1, xt[1], True)

        def act_end_stage(act, st, c, layer, hh):
            act.wait_ge(st.x_turned, c + 1)
            nc.scalar.activation(xt[0][:, :], bank[3][:, :], ACT.Copy).then_inc(st.xt_ready, 1)
            if layer == 1:
                act.wait_ge(st.h_ready, c * (HPC + 1) + 1)
                for f in range(2):
                    last = nc.scalar.activation(rh[:, f, :], hbank[f], ACT.Gelu, bias=rb1[:, f:f + 1])
                last.then_inc(st.rh_ready, 1)
            act.wait_ge(st.gate_pre, c + 1)
            if layer == 0:
                nc.scalar.activation(p12[:, 1, :], lead[:, :], ACT.Exp).then_inc(st.gate_exp, 1)
            else:
                nc.scalar.activation(e_sm[:, :, :], sc8[:, :, 0:E1], ACT.Exp).then_inc(st.gate_exp, 1)
            act.wait_ge(st.gates_turned, c + 1)
            nc.scalar.activation(gate_t[:, :], bank[2][0:8, :], ACT.Copy).then_inc(st.gate_t, 1)
            n_e = experts(layer)
            for e in range(n_e):
                act.wait_ge(st.gbc_ready, c * n_e + e + 1)
                nc.scalar.activation(gate_bc[:, e, :], bank[1 + e % 2][:, :], ACT.Copy).then_inc(st.gbc_saved, 1)
            for n in range(HPC):
                act.wait_ge(st.h_ready, (c * HPC + n + 1) if layer == 0 else (c * (HPC + 1) + n + 2))
                if n >= 2:
                    act.wait_ge(st.hid_ready, c * HPC + n - 1)
                if layer == 0:
                    nc.scalar.activation(act_s[n % 2][:, :], hbank[n % 2], ACT.Silu).then_inc(st.s_done, 1)
                else:
                    nc.scalar.activation(act_s[n % 2][:, :], hbank[n % 2], ACT.Gelu,
                                         bias=be1[:, n:n + 1]).then_inc(st.s_done, 1)
            act.wait_ge(st.y_done, (c + 1) * YPC[layer])
            nc.scalar.activation(y_sb[:, :], bank[0][:, :], ACT.Copy).then_inc(st.y_saved, 1)
            if layer == 0:
                act.wait_ge(st.xt2_turned, c + 1)
                nc.scalar.activation(xt[1][:, :], bank[3][:, :], ACT.Copy).then_inc(st.xt2_ready, 1)
                for a in range(2):
                    act.wait_ge(st.rot_sum, 2 * c + a + 1)
                    nc.scalar.activation(qk_hi[a][:, :], rot[2 * a][:, :], ACT.Copy).then_inc(st.halves_hi, 1)

        LINKS = [12, 14]

        def dve_gates(dve, ch, st, c, layer):
            dve.wait_ge(st.router_in, c + 1)
            if layer == 0:
                ch.link(nc.vector.tensor_copy(sc8[:, :, :], bank[1][:, 0:TPC * 8].rearrange("p (t e) -> p t e", e=8)), apart)
            else:
                lg = bank[1][:, 0:TPC * E1].rearrange("p (t e) -> p t e", e=E1)
                ch.link(nc.vector.tensor_tensor(sc8[:, :, 0:E1], lg, rb2[:, None, :].broadcast_to([P, TPC, E1]), ALU.add))
                ch.link(nc.vector.tensor_reduce(lead[:, :], sc8[:, :, 0:E1], AXX, ALU.max))
                nc.vector.tensor_tensor(sc8[:, :, 0:E1], sc8[:, :, 0:E1],
                                        lead[:, :, None].broadcast_to([P, TPC, E1]),
                                        ALU.subtract).then_inc(st.gate_pre, 1)
                dve.wait_ge(st.gate_exp, c + 1)
                ch.link(nc.vector.tensor_reduce(lead[:, :], e_sm[:, :, :], AXX, ALU.add))
                ch.link(nc.vector.reciprocal(lead[:, :], lead[:, :]))
                ch.link(nc.vector.tensor_tensor(sc8[:, :, 0:E1], e_sm[:, :, :],
                                                lead[:, :, None].broadcast_to([P, TPC, E1]), ALU.mult), apart)
            for t in range(TPC):
                ins = nc.vector.max(mx8[:, t, :], sc8[:, t, :])
            ch.link(ins, apart)
            for t in range(TPC):
                ins = nc.vector.max_index(ix8[:, t, :], mx8[:, t, :], sc8[:, t, :])
            ch.link(ins)
            ch.link(nc.vector.tensor_copy(ixf[:, :, :], ix8[:, :, :]))
            if layer == 0:
                nc.vector.tensor_tensor(lead[:, :], mx8[:, :, 1], mx8[:, :, 0], ALU.subtract).then_inc(st.gate_pre, 1)
                dve.wait_ge(st.gate_exp, c + 1)
                ch.link(nc.vector.tensor_scalar(p12[:, 0, :], p12[:, 1, :], 1.0, None, ALU.add))
                ch.link(nc.vector.reciprocal(p12[:, 0, :], p12[:, 0, :]))
                ch.link(nc.vector.tensor_tensor(p12[:, 1, :], p12[:, 1, :], p12[:, 0, :], ALU.mult))
            else:
                ch.link(nc.vector.tensor_copy(p12[:, :, :], mx8[:, :, 0:2].rearrange("p t k -> p k t")))
            for t in range(TPC):
                for k in range(2):
                    ins = nc.vector.tensor_scalar(gts[:, k, t, :], iota8[:, :], ixf[:, t, k:k + 1],
                                                  p12[:, k, t:t + 1], ALU.is_equal, ALU.mult)
            ch.link(ins)
            nc.vector.tensor_tensor(gts[:, 0, :, :], gts[:, 0, :, :], gts[:, 1, :, :], ALU.add).then_inc(st.gates, 1)

        def dve_rope_halves(dve, st, c, hh):
            dve.wait_ge(st.qkv_ready, c + 1)
            for a in range(2):
                nc.vector.tensor_tensor(rot[2 * a][:, :], hbank[2 * a], rope_a[:, hh * CH:(hh + 1) * CH], ALU.mult)
                nc.vector.tensor_tensor(rot[2 * a + 1][:, :], hbank[2 * a + 1], rope_b[:, hh * CH:(hh + 1) * CH],
                                        ALU.mult).then_inc(st.rot_done, 1)

        def dve_end_stage(dve, st, c, layer, hh, tile):
            ch = dve_chain[0]
            dve.wait_ge(st.done, c + 1)
            xv = x_tm[:, bass.ds(tile, TPC), :]
            dve.sem_inc(apart, 1)
            if layer == 1:
                ch.link(nc.vector.tensor_tensor(res[:, :, :], xv, b_o1[:, None, :].broadcast_to([P, TPC, D]), ALU.add))
            else:
                ch.link(nc.vector.tensor_copy(res[:, :, :], xv))
            dve_layernorm(dve, ch, res, xs[0], st.stats, st.rstd, c + 1).then_inc(st.norm, 1)
            dve_gates(dve, ch, st, c, layer)
            n_e = experts(layer)
            dve.wait_ge(st.gbc_saved, NS + (c + 1) * n_e)
            for n in range(HPC):
                e = n * n_e // HPC
                dve.wait_ge(st.s_done, NS + c * HPC + n + 1)
                if n >= 2:
                    dve.wait_ge(st.y_done, c * YPC[layer] + n - 1)
                if layer == 0:
                    nc.vector.tensor_tensor(lin_u[n % 2][:, :], hbank[2 + n % 2], gate_bc[:, e, :],
                                            ALU.mult).then_inc(st.u_done, 1)
                    dve.wait_ge(st.u_done, NS + c * HPC + n + 1)
                    nc.vector.tensor_tensor(hid[n % 2][:, :], act_s[n % 2][:, :], lin_u[n % 2][:, :],
                                            ALU.mult).then_inc(st.hid_ready, 1)
                else:
                    nc.vector.tensor_tensor(hid[n % 2][:, :], act_s[n % 2][:, :], gate_bc[:, e, :],
                                            ALU.mult).then_inc(st.hid_ready, 1)
            dve.wait_ge(st.y_turned, c + 1)
            ch.link(nc.vector.tensor_tensor(res[:, :, :], xs[0][:, :, :],
                                            bank[3][:, :].rearrange("p (t c) -> p t c", c=D), ALU.add))
            dve_layernorm(dve, ch, res, xs[1], st.stats2, st.rstd2, c + 1).then_inc(st.norm2, 1)
            if layer == 0:
                dve.wait_ge(st.norm2, c + 1)
                dve.sem_inc(apart, 1)
                nc.vector.tensor_copy(xv, xs[1][:, :, :]).then_inc(st.x_kept, 1)
                dve_rope_halves(dve, st, c, hh)
                nc.vector.tensor_copy(v_all[:, bass.ds(tile, TPC), :],
                                      bank[0][:, :].rearrange("p (t c) -> p t c", c=D)).then_inc(st.v_saved, 1)
                for a in range(2):
                    dve.wait_ge(st.halves_hi, 2 * c + a + 1)
                    nc.vector.tensor_tensor(qk_lo[a][:, :], rot[2 * a][:, :], qk_hi[a][:, :].bitcast(F32),
                                            ALU.subtract).then_inc(st.halves_lo, 1)

        def pool_end_stage(pool, pc, st, c, layer):
            pool_rstd(pool, pc, st.stats, st.rstd, c + 1)
            pool_rstd(pool, pc, st.stats2, st.rstd2, c + 1)
            if layer == 0:
                for a in range(2):
                    pool.wait_ge(st.rot_done, 2 * c + a + 1)
                    nc.gpsimd.tensor_tensor(rot[2 * a][:, :], rot[2 * a][:, :], rot[2 * a + 1][:, :],
                                            ALU.add).then_inc(st.rot_sum, 1)

        @block.sync
        def _(sp):
            for t, name in CONSTS:
                sp.dma_start(t[tuple(slice(None) for _ in t.shape)], d[name]).then_inc(const_loaded, 16)
            sp.dma_start(x_tm[:, :, :], x_tiles).then_inc(const_loaded, 16)
            for t, name in WEIGHTS:
                sp.dma_start(t[tuple(slice(None) for _ in t.shape)], d[name]).then_inc(w_loaded, 16)
            sp.dma_start(b_o1[:, :], d["b_o1"].broadcast_to([P, D])).then_inc(w_loaded, 16)
            sp.dma_start(rb2[:, :], d["rb2"].broadcast_to([P, E1])).then_inc(w_loaded, 16)
            sp.wait_ge(fills, 4)
            for b in range(B):
                for hh in range(2):
                    sp.dma_start(k_scr[1][b, 3, :, hh * CH:(hh + 1) * CH],
                                 gate_bc[:, 0, :]).then_inc(ones_stored, 16)
            sp.wait_ge(ones_stored, 16 * 2 * B)
            st = stages[0]
            with sp.Fori(0, B) as b:
                for hh in range(2):
                    c = 2 * b + hh
                    sp.wait_ge(st.x_turned, c + 1)
                    sp.dma_start(xs[0][:, :, :], x_tiles[:, bass.ds(c * TPC, TPC), :]).then_inc(st.x_in, 16)
                    sp_store_halves(sp, st, 0, c, b, hh)
            sp.wait_ge(st.stored, STORES[0] * 2 * B)
            sp_attention(sp, layers[0])
            st = stages[1]
            with sp.Fori(0, B) as b:
                for hh in range(2):
                    c = 2 * b + hh
                    sp_store_halves(sp, st, 1, c, b, hh)
                    sp.wait_ge(st.stored, STORES[1] * (c + 1))
                    sp.wait_ge(st.v_saved, c + 1)
                    sp.wait_ge(st.x_kept, c + 1)
                    sp.sem_inc(st.done, 1)
            sp_attention(sp, layers[1])
            st = stages[2]
            with sp.Fori(0, 2 * B) as c:
                sp.wait_ge(st.norm2, c + 1)
                sp.dma_start(out_tiles[:, bass.ds(c * TPC, TPC), :], xs[1][:, :, :]).then_inc(st.stored, 16)
                sp.wait_ge(st.stored, 16 * (c + 1))
                sp.sem_inc(st.done, 1)

        @block.gpsimd
        def _(pool):
            nc.gpsimd.memset(gate_bc[:, 0, :], 1.0).then_inc(fills, 1)
            for p in range(2):
                nc.gpsimd.memset(v_st[p][:, :, :, :], 1.0).then_inc(fills, 1)
            nc.gpsimd.memset(mhalf[:, :], -0.5).then_inc(fills, 1)
            pool.wait_ge(stages[0].v_saved, 2 * B)
            pool_attention(pool, layers[0])
            pc = Chain(pool, stages[1].pool_chain)
            with pool.Fori(0, 2 * B) as c:
                pc.at(2 * c)
                pool_end_stage(pool, pc, stages[1], c, 0)
            pool.wait_ge(stages[1].v_saved, 2 * B)
            pool.wait_ge(layers[0].pv_done, NS + NG * layers[0].S)
            pool_attention(pool, layers[1])
            pc = Chain(pool, stages[2].pool_chain)
            with pool.Fori(0, 2 * B) as c:
                pc.at(2 * c)
                pool_end_stage(pool, pc, stages[2], c, 1)

        @block.scalar
        def _(act):
            act.wait_ge(const_loaded, ALL_CONSTS)
            st = stages[0]
            with act.Fori(0, 2 * B) as c:
                act.wait_ge(st.x_turned, c + 2)
                nc.scalar.activation(xt[0][:, :], bank[3][:, :], ACT.Copy).then_inc(st.xt_ready, 1)
                act.wait_ge(st.qkv_ready, c + 1)
                act.wait_ge(st.done, c + 1)
                for a in range(2):
                    nc.scalar.activation(qk_hi[a][:, :], hbank[a], ACT.Copy).then_inc(st.halves_hi, 1)
            act_attention(act, layers[0])
            act.wait_ge(w_loaded, ALL_W)
            with act.Fori(0, 2 * B) as c:
                act_end_stage(act, stages[1], c, 0, 0)
            act_attention(act, layers[1])
            with act.Fori(0, 2 * B) as c:
                act_end_stage(act, stages[2], c, 1, 0)

        @block.vector
        def _(dve):
            for L in layers:
                dve.sem_inc(L.exp_done, NS)
                dve.sem_inc(L.pv_done, NS)
                dve.sem_inc(L.o_free, 1)
                dve.sem_inc(L.spare_free, 1)
                dve.sem_inc(L.smax_free, NS)
            for st in stages[1:]:
                dve.sem_inc(st.s_done, NS)
                dve.sem_inc(st.gbc_saved, NS)
                dve.sem_inc(st.done, 1)
            dve.sem_inc(stages[1].u_done, NS)
            dve.sem_inc(stages[0].x_turned, 1)
            dve.sem_inc(stages[0].done, 1)
            dve.wait_ge(const_loaded, ALL_CONSTS)
            dve.wait_ge(fills, 4)
            st = stages[0]
            with dve.Fori(0, 2 * B) as c:
                dve.wait_ge(st.qkv_ready, c + 1)
                for a in range(2):
                    dve.wait_ge(st.halves_hi, 2 * c + a + 1)
                    nc.vector.tensor_tensor(qk_lo[a][:, :], hbank[a], qk_hi[a][:, :].bitcast(F32),
                                            ALU.subtract).then_inc(st.halves_lo, 1)
                nc.vector.tensor_copy(v_all[:, bass.ds(c * TPC, TPC), :],
                                      bank[0][:, :].rearrange("p (t c) -> p t c", c=D)).then_inc(st.v_saved, 1)
                dve.wait_ge(st.stored, STORES[0] * (c + 1))
                dve.wait_ge(st.v_saved, c + 1)
                dve.sem_inc(st.done, 1)
            dve_attention(dve, layers[0])
            dve.wait_ge(w_loaded, ALL_W)
            dve.wait_ge(layers[0].spare_free, 1 + layers[0].spare_base(NG - 1) + 6)
            ch = dve_chain[0] = Chain(dve, stages[1].chain)
            with dve.Fori(0, B) as b:
                for hh in range(2):
                    c = 2 * b + hh
                    ch.at(c * LINKS[0])
                    dve_end_stage(dve, stages[1], c, 0, hh, c * TPC)
                    assert ch.n == LINKS[0], ch.n
            dve_attention(dve, layers[1])
            dve.wait_ge(layers[1].spare_free, 1 + layers[1].spare_base(NG - 1) + 6)
            ch = dve_chain[0] = Chain(dve, stages[2].chain)
            ch.link(nc.vector.memset(sc8[:, :, E1:8], -1.0))
            with dve.Fori(0, 2 * B) as c:
                ch.at(1 + c * LINKS[1])
                dve_end_stage(dve, stages[2], c, 1, 0, c * TPC)
                assert ch.n == LINKS[1], ch.n

        @block.tensor
        def _(pe):
            pe.wait_ge(const_loaded, ALL_CONSTS)
            pe.wait_ge(fills, 4)
            st = stages[0]
            with pe.Fori(0, 2 * B) as c:
                pe.wait_ge(st.x_in, 16 * (c + 1))
                pe_turn_tiles(bank[3], xs[0]).then_inc(st.x_turned, 1)
                pe.wait_ge(st.xt_ready, c + 1)
                pe.wait_ge(st.done, c + 1)
                pe_qkv(pe, st, c, w_qkv0, xt[0], False)
            pe.wait_ge(st.v_saved, 2 * B)
            pe_attention(pe, layers[0])
            pe.wait_ge(w_loaded, ALL_W)
            with pe.Fori(0, 2 * B) as c:
                pe_end_stage(pe, stages[1], c, 0, 0)
            pe.wait_ge(stages[1].done, 2 * B + 1)
            pe_attention(pe, layers[1])
            with pe.Fori(0, 2 * B) as c:
                pe_end_stage(pe, stages[2], c, 1, 0)


_IN_NAMES = ["x", "ident", "den_pick", "tri", "expert_row", "iota8", "w_qkv0", "w_qkv1", "w_o0", "w_o1", "rope_a",
             "rope_b", "b_o1", "wg", "w1", "w2", "w3", "rw1", "rb1", "rw2", "rb2", "we1", "be1", "we2", "be2"]


def _layout(i):
    f = np.float32
    a = {k: np.asarray(v) for k, v in i.items()}
    c = np.ascontiguousarray
    o = {"x": a["L0_attn_x"].reshape(NTOK, D), "ident": np.eye(P, dtype=f)}
    den = np.zeros((P, P), f)
    for j in range(HG):
        den[SLOT * j + DK, SLOT * j:SLOT * (j + 1)] = 1
    o["den_pick"] = den
    o["tri"] = np.triu(np.ones((P, P), f))
    er = np.zeros((E0, E0, P), f)
    for e in range(E0):
        er[e, e] = 1
    o["expert_row"] = er
    o["iota8"] = np.tile(np.arange(E0, dtype=f), (P, 1))
    w = a["L0_attn_Wqkv"].reshape(3, P, D)
    o["w_qkv0"] = c(w.transpose(2, 0, 1))
    w = a["L1_attn_w_qkv"].reshape(3, H, DK // 2, 2, D)
    rows = [np.concatenate([w[s, :, :, t], w[s, :, :, t]], axis=1).reshape(P, D) for s in range(2) for t in range(2)]
    rows.append(a["L1_attn_w_qkv"][2 * P:])
    o["w_qkv1"] = c(np.stack(rows).transpose(2, 0, 1))
    inv = (f(1.0) / np.power(f(10000.0), np.arange(0, DK, 2, dtype=f) / f(DK))).astype(f)
    ang = np.outer(np.arange(T, dtype=f), inv).astype(f)
    cos, sin = np.cos(ang).astype(f).T, np.sin(ang).astype(f).T
    o["rope_a"] = c(np.tile(np.concatenate([cos, sin]), (H, 1)))
    o["rope_b"] = c(np.tile(np.concatenate([-sin, cos]), (H, 1)))
    for n, name in ((0, "L0_attn_Wout"), (1, "L1_attn_w_out")):
        wo = np.zeros((HG, SLOT, G, D), f)
        wo[:, 0:DK] = a[name].reshape(D, G, HG, DK).transpose(2, 3, 1, 0)
        o[f"w_o{n}"] = wo.reshape(P, G, D)
    o["b_o1"] = a["L1_attn_b_out"].reshape(1, D)
    o["wg"] = c(a["L0_ffn_Wg"].T)
    o["w1"] = c(a["L0_ffn_W1"].transpose(2, 0, 1))
    o["w2"] = c(a["L0_ffn_W2"].transpose(2, 0, 1))
    o["w3"] = c(a["L0_ffn_W3"].transpose(2, 0, 1).reshape(F0 // P, P, E0, D).transpose(1, 2, 0, 3).reshape(P, NH, D))
    o["rw1"] = a["L1_ffn_rW1"]
    o["rb1"] = c(a["L1_ffn_rb1"].reshape(2, P).T)
    o["rw2"] = c(a["L1_ffn_rW2"].reshape(2, P, E1).transpose(1, 0, 2))
    o["rb2"] = a["L1_ffn_rb2"].reshape(1, E1)
    o["we1"] = c(a["L1_ffn_We1"].transpose(1, 0, 2))
    o["be1"] = c(a["L1_ffn_be1"].reshape(NH, P).T)
    o["we2"] = c(a["L1_ffn_We2"].reshape(NH, P, D).transpose(1, 0, 2))
    o["be2"] = a["L1_ffn_be2"]
    return {k: c(o[k]) for k in _IN_NAMES}


def kernel(**inputs):
    import concourse.bacc as _bacc
    from concourse.bass_utils import run_bass_kernel_spmd as _run

    nc = _bacc.Bacc("TRN2", target_bir_lowering=False, num_devices=1)
    arrays = {f"in_{k}": v for k, v in _layout(inputs).items()}
    aps = {k: nc.dram_tensor(f"in_{k}", arrays[f"in_{k}"].shape, F32, kind="ExternalInput").ap() for k in _IN_NAMES}
    out = nc.dram_tensor("out_dram", (NTOK, D), F32, kind="ExternalOutput").ap()
    build_program(nc, aps, out)
    r = _run(nc, [arrays], core_ids=[0])
    return np.asarray(r.results[0]["out_dram"]).reshape(B, T, D)
```

```python
from contextlib import ExitStack

import numpy as np

import concourse.bass as bass
from concourse import mybir

ALU = mybir.AluOpType
ACT = mybir.ActivationFunctionType
AXX = mybir.AxisListType.X
F32 = mybir.dt.float32
F32R = mybir.dt.float32r
U32 = mybir.dt.uint32

P = 128
B, T, D, H = 4, 1024, 128, 16
DK = D // H
NTOK = B * T
CH = 512
TPC = CH // P
CPB = T // CH
KT = T // P
NT = NTOK // P
HG = 4
G = H // HG
NG = B * G
SLOT = 32
E0, F0 = 8, 256
E1, F1 = 4, 512
NH = E0 * F0 // P
assert NH == E1 * F1 // P
SCALE = float(DK) ** -0.5
CLIP = 10.0
EPS = 1e-5
NS = 2
NP = 4
AHEAD = 3
VW = P + SLOT
LO = 16


def steps_of(causal):
    out = []
    for qc in range(CPB):
        for kt in range(KT if not causal else (qc + 1) * TPC):
            for hp in range(HG // 2):
                q0 = max(qc * CH, kt * P) if causal else qc * CH
                out.append([qc, kt, hp, q0, (qc + 1) * CH - q0, False])
        out[-1][5] = True
    return out


class Layer:

    def __init__(self, n, sem):
        self.n = n
        self.causal = n == 0
        self.steps = steps_of(self.causal)
        self.S = len(self.steps)
        self.loads = 4 * HG if self.causal else 2 * HG + 2
        assert self.S % NP == 0 and self.S % NS == 0
        self.last = [s for s, x in enumerate(self.steps) if x[5]]
        if self.causal:
            self.hi_on = ["act"] * self.S
            self.lo_on = ["pool" if s % 2 else "dve" for s in range(self.S)]
        else:
            self.hi_on = ["dve" if s > 25 and s % 2 else "act" for s in range(self.S)]
            self.lo_on = ["pool" if s <= 25 and s % 4 else "dve" for s in range(self.S)]
        self.norm_prev, self.norm_0 = 2, self.last[0] + 3
        self.max_from = 1
        self.turn = [] if self.causal else [24, 25]
        self.jobs0 = 1 + len(self.turn)
        self.jobs = 2 + len(self.turn)
        self.max_jobs = 0 if self.causal else KT * HG * 2
        self.v_used = [max(s for s, x in enumerate(self.steps) if x[1] == kt) for kt in range(KT)]
        self.stacks_loaded = [sem(f"l{n}_stacks_loaded{p}") for p in range(2)]
        self.zeroed = sem(f"l{n}_zeroed")
        self.v_staged = sem(f"l{n}_v_staged")
        self.scores_ready = sem(f"l{n}_scores_ready")
        self.exp_done = sem(f"l{n}_exp_done")
        self.act_hi = sem(f"l{n}_act_hi")
        self.dve_hi = sem(f"l{n}_dve_hi")
        self.dve_lo = sem(f"l{n}_dve_lo")
        self.pool_lo = sem(f"l{n}_pool_lo")
        self.pv_done = sem(f"l{n}_pv_done")
        self.o_free = sem(f"l{n}_o_free")
        self.o_saved = sem(f"l{n}_o_saved")
        self.spare_ready = sem(f"l{n}_spare_ready")
        self.spare_free = sem(f"l{n}_spare_free")
        self.chain = sem(f"l{n}_chain")
        self.normed = sem(f"l{n}_normed")
        if self.causal:
            self.clip_done = sem(f"l{n}_clip_done")
        else:
            self.aug_loaded = [sem(f"l{n}_aug_loaded{p}") for p in range(2)]
            self.smax_ready = sem(f"l{n}_smax_ready")
            self.smax_free = sem(f"l{n}_smax_free")
            self.negmax_ready = sem(f"l{n}_negmax_ready")

    def spare_base(self, i):
        return self.jobs0 + len(self.turn) + self.jobs * (i - 1)

    def max_jobs_at(self, s):
        if self.causal or s < self.max_from:
            return range(0)
        k = s - self.max_from
        per = self.turn[0] - self.max_from
        return range(min(self.max_jobs * k // per, self.max_jobs),
                     min(self.max_jobs * (k + 1) // per, self.max_jobs))

    def count(self, on, who, i, s):
        return i * on.count(who) + on[:s + 1].count(who)

    def around(self, i, s, prev, nxt):
        if s < 0:
            return (i - 1, s + self.S) if prev else None
        if s >= self.S:
            return (i + 1, s - self.S) if nxt else None
        return i, s


class Chain:

    def __init__(self, eng, sem):
        self.eng, self.sem, self.base, self.n = eng, sem, 0, 0

    def at(self, base):
        self.base, self.n = base, 0

    def link(self, ins, apart=None):
        self.n += 1
        ins.then_inc(self.sem, 1)
        self.eng.wait_ge(self.sem, self.base + self.n)
        if apart is not None:
            self.eng.sem_inc(apart, 1)


def build_program(nc, d, out):
    with ExitStack() as ctx:
        def sb(name, shape, dt=F32):
            return ctx.enter_context(nc.sbuf_tensor(name, shape, dt))

        def sem(name):
            return ctx.enter_context(nc.semaphore(name))

        bank = [ctx.enter_context(nc.psum_tensor(f"bank{i}", [P, CH], F32)) for i in range(4)]
        score = [ctx.enter_context(nc.psum_tensor(f"score{i}", [P, 2, CH], F32)) for i in range(NS)]
        hbank = [score[0][:, 0, :], score[0][:, 1, :], score[1][:, 0, :], score[1][:, 1, :]]

        ident = sb("ident", [P, P])
        tri = sb("tri", [P, P])
        expert_row = sb("expert_row", [2 * E0, E0, P], F32R)
        iota8 = sb("iota8", [P, E0])
        w_qkv0 = sb("w_qkv0", [P, 3, P])
        w_qkv1 = sb("w_qkv1", [P, 5, P])
        w_o = [sb(f"w_o{n}", [P, D]) for n in range(2)]
        b_o1 = sb("b_o1", [P, D])
        wg = sb("wg", [P, E0])
        w3 = sb("w3", [P, NH, P])
        rw1 = sb("rw1", [P, F0])
        rb1 = sb("rb1", [P, 2])
        rw2 = sb("rw2", [P, 2, E1])
        rb2 = sb("rb2", [P, E1])
        be1 = sb("be1", [P, NH])
        be2 = sb("be2", [2 * E0, D])

        x_tm = sb("x_tm", [P, NT, D])
        v_all = sb("v_all", [P, NT, D])
        o_tm = sb("o_tm", [P, NT, D])
        st6 = sb("st6", [P, 2, TPC, 6])
        mv = sb("mv", [P, 2, TPC, 2])
        rstd = sb("rstd", [P, 2, TPC])
        mhalf = sb("mhalf", [P, TPC])
        sc8 = sb("sc8", [P, TPC, 8])
        mx8 = sb("mx8", [P, TPC, 8])
        ix8 = sb("ix8", [P, TPC, 8], U32)
        ixf = sb("ixf", [P, TPC, 8])
        lead = sb("lead", [P, TPC])
        e_sm = sb("e_sm", [P, TPC, E1])
        p12 = sb("p12", [P, 2, TPC])
        gts = sb("gts", [P, 2, TPC, 8])
        g_halves = sb("g_halves", [P, TPC, 2 * E0])
        v_st_shape = [P, KT, HG * VW]
        with ExitStack() as overlay:
            def osb(name, shape, dt=F32):
                return overlay.enter_context(nc.sbuf_tensor(name, shape, dt))

            k_st = [osb(f"k_st{p}", [P, HG, T], F32R) for p in range(2)]
            q_st = [osb(f"q_st{p}", [P, T], F32R) for p in range(2)]
            v_st = osb("v_st", v_st_shape, F32R)
            probs = [osb(f"probs{p}", [P, 2, CH]) for p in range(NP)]
            p_hi = [osb(f"p_hi{p}", [P, 2, CH], F32R) for p in range(NP)]
            p_lo = [osb(f"p_lo{p}", [P, 2, CH], F32R) for p in range(NP)]
            o_sb = osb("o_sb", [P, CH])
            o_lo = osb("o_lo", [P, TPC, HG, DK])
            o_sum = osb("o_sum", [P, TPC, HG, DK])
            o_rcp = osb("o_rcp", [P, TPC, HG])
            negmax_h = osb("negmax_h", [P, KT, HG, 2])
            negmax = osb("negmax", [P, KT, HG])
            negmax2 = osb("negmax2", [P, KT, 2 * HG])
            negmax_t = osb("negmax_t", [2 * HG, T], F32R)
            ones_t = osb("ones_t", [HG, T])
            zeros_t = osb("zeros_t", [HG, T])
        with ExitStack() as overlay:
            xs = [osb(f"xs{i}", [P, TPC, D]) for i in range(2)]
            x_out = osb("x_out", [P, TPC, D])
            xt = [osb(f"xt{i}", [P, CH]) for i in range(2)]
            xt2 = xt[1]
            x_hi = [osb(f"x_hi{i}", [P, CH], F32R) for i in range(2)]
            x_lo = [osb(f"x_lo{i}", [P, CH], F32R) for i in range(2)]
            os_ = osb("os_", [P, TPC, D])
            ot = osb("ot", [P, CH])
            gate_bc = [osb(f"gate_bc{i}", [P, CH]) for i in range(2)]
            act_s = [osb(f"act_s{i}", [P, CH]) for i in range(2)]
            lin_u = [osb(f"lin_u{i}", [P, CH]) for i in range(2)]
            hid = [osb(f"hid{i}", [P, CH]) for i in range(2)]
            y_sb = osb("y_sb", [P, CH])
            res = [osb(f"res{i}", [P, TPC, D]) for i in range(2)]
            qk_hi = [osb(f"qk_hi{i}", [P, CH]) for i in range(4)]
            qk_lo = [osb(f"qk_lo{i}", [P, CH]) for i in range(4)]
            expert_raw = osb("expert_raw", [2 * E0, E0, P])
            gate_t = osb("gate_t", [2 * E0, CH], F32R)
            w_raw = [osb(f"w_raw{k}", [P, NH * P]) for k in range(2)]
            w_hi = [osb(f"w_hi{k}", [P, NH * P], F32R) for k in range(2)]
            w_lo = [osb(f"w_lo{k}", [P, NH * P], F32R) for k in range(2)]
            with ExitStack() as layer_only:
                rope_a = layer_only.enter_context(nc.sbuf_tensor("rope_a", [P, T], F32))
                rope_b = layer_only.enter_context(nc.sbuf_tensor("rope_b", [P, T], F32))
                rot = [layer_only.enter_context(nc.sbuf_tensor(f"rot{i}", [P, CH], F32)) for i in range(4)]
            with ExitStack() as layer_only:
                rh = layer_only.enter_context(nc.sbuf_tensor("rh", [P, 2, CH], F32))
                we2 = layer_only.enter_context(nc.sbuf_tensor("we2", [P, NH, P], F32))

        q_scr = [nc.dram_tensor(f"q_scr{n}", [B, 2 + n, P, T], F32, kind="Internal").ap() for n in range(2)]
        k_scr = [nc.dram_tensor(f"k_scr{n}", [B, 2 + n, P, T], F32, kind="Internal").ap() for n in range(2)]

        const_loaded = sem("const_loaded")
        w_loaded = sem("w_loaded")
        raw_loaded = [sem(f"raw_loaded{k}") for k in range(2)]
        we2_loaded = sem("we2_loaded")
        rows_ready = sem("rows_ready")
        w_upper = sem("w_upper")
        w_lower = sem("w_lower")
        fills = sem("fills")
        apart = sem("apart")
        v_upper = sem("v_upper")
        FILLS = 1
        apart_pool = sem("apart_pool")
        first_loaded = sem("first_loaded")
        ones_loaded = sem("ones_loaded")
        layers = [Layer(n, sem) for n in range(2)]

        class Stage:

            def __init__(self, n):
                self.x_turned = sem(f"st{n}_x_turned")
                self.xt_ready = sem(f"st{n}_xt_ready")
                self.qkv_ready = sem(f"st{n}_qkv_ready")
                self.halves_hi = sem(f"st{n}_halves_hi")
                self.halves_lo = sem(f"st{n}_halves_lo")
                self.v_saved = sem(f"st{n}_v_saved")
                self.stored = sem(f"st{n}_stored")
                self.done = sem(f"st{n}_done")
                if n == 0:
                    self.x_in = [sem(f"st0_x_in{p}") for p in range(2)]
                    self.pair_stored = [sem(f"st0_pair_stored{p}") for p in range(2)]
                    return
                self.norm = sem(f"st{n}_norm")
                self.o_in = sem(f"st{n}_o_in")
                self.o_turned = sem(f"st{n}_o_turned")
                self.ot_ready = sem(f"st{n}_ot_ready")
                self.o_proj = sem(f"st{n}_o_proj")
                self.router_in = sem(f"st{n}_router_in")
                self.gate_pre = sem(f"st{n}_gate_pre")
                self.gate_exp = sem(f"st{n}_gate_exp")
                self.gates = sem(f"st{n}_gates")
                self.gates_turned = sem(f"st{n}_gates_turned")
                self.gate_t = sem(f"st{n}_gate_t")
                self.gbc_ready = sem(f"st{n}_gbc_ready")
                self.gbc_saved = sem(f"st{n}_gbc_saved")
                self.h_ready = sem(f"st{n}_h_ready")
                self.x_upper = sem(f"st{n}_x_upper")
                self.x_lower = sem(f"st{n}_x_lower")
                self.router_h = sem(f"st{n}_router_h")
                self.s_done = sem(f"st{n}_s_done")
                self.hid_ready = sem(f"st{n}_hid_ready")
                self.y_done = sem(f"st{n}_y_done")
                self.y_saved = sem(f"st{n}_y_saved")
                self.y_turned = sem(f"st{n}_y_turned")
                self.stats = sem(f"st{n}_stats")
                self.rstd = sem(f"st{n}_rstd")
                self.stats2 = sem(f"st{n}_stats2")
                self.rstd2 = sem(f"st{n}_rstd2")
                self.norm2 = sem(f"st{n}_norm2")
                self.chain = sem(f"st{n}_chain")
                self.back_chain = sem(f"st{n}_back_chain")
                self.pool_chain = sem(f"st{n}_pool_chain")
                if n == 1:
                    self.u_done = sem("st1_u_done")
                    self.x_kept = sem("st1_x_kept")
                    self.rot_done = sem("st1_rot_done")
                    self.rot_sum = sem("st1_rot_sum")
                    self.qk_ready = sem("st1_qk_ready")
                    self.v_ready = sem("st1_v_ready")
                    self.xt2_turned = sem("st1_xt2_turned")
                    self.xt2_ready = sem("st1_xt2_ready")
                else:
                    self.rh_ready = sem("st2_rh_ready")

        stages = [Stage(n) for n in range(3)]

        block = ctx.enter_context(nc.Block())

        FIRST = [(ident, "ident"), (w_qkv0, "w_qkv0")]
        CONSTS = [(tri, "tri"), (iota8, "iota8"), (w_o[0], "w_o0"), (w_o[1], "w_o1"), (expert_raw, "expert_row")]
        WEIGHTS = [(w_qkv1, "w_qkv1"), (wg, "wg"), (w3, "w3"), (rw1, "rw1"), (rb1, "rb1"), (rw2, "rw2"),
                   (be1, "be1"), (be2, "be2")]
        ALL_CONSTS = 16 * len(CONSTS)
        ALL_W = 16 * (len(WEIGHTS) + 5)
        x_tiles = d["x"].rearrange("(t p) c -> p t c", p=P)
        out_tiles = out.rearrange("(t p) c -> p t c", p=P)

        def bg(i):
            return i // G, i % G

        def o_bank(L, qc):
            return bank[qc] if L.causal else bank[0]

        def pe_max_job(pe, L, i, p, m):
            qt, j, half = m // (HG * 2), m // 2 % HG, m % 2
            pe.wait_ge(L.smax_free, i * L.max_jobs + m + 1)
            nc.tensor.matmul(bank[1 + m % 2][:, :], q_st[p][:, qt * P:(qt + 1) * P],
                             k_st[p][:, j, half * CH:(half + 1) * CH],
                             start=True, stop=True).then_inc(L.smax_ready, 1)

        def pe_turn(pe, L, i, half, job):
            if half == 0:
                pe.wait_ge(L.negmax_ready, i + 1)
            pe.wait_ge(L.spare_free, job + 1)
            for t in range(TPC):
                last = nc.tensor.transpose(bank[3][0:2 * HG, t * P:(t + 1) * P],
                                           negmax2[:, half * TPC + t, :], ident[:, :])
            last.then_inc(L.spare_ready, 1)

        def pe_norm(pe, L, chunk, job):
            pe.wait_ge(L.o_saved, chunk + 1)
            pe.wait_ge(L.spare_free, job + 1)
            for t in range(TPC):
                last = nc.tensor.transpose(bank[3][:, t * P:(t + 1) * P], o_sb[:, t * P:(t + 1) * P], ident[:, :])
            last.then_inc(L.spare_ready, 1)

        def pe_scores(pe, L, i, p, s):
            qc, kt, hp, q0, w, _ = L.steps[s]
            pe.wait_ge(L.exp_done, i * L.S + s + 1)
            for a in range(2):
                j = 2 * hp + a
                last = nc.tensor.matmul(score[s % NS][:, a, 0:w], k_st[p][:, j, kt * P:(kt + 1) * P],
                                        q_st[p][:, q0:q0 + w], start=True, stop=True)
            last.then_inc(L.scores_ready, 1)

        def pe_loaded(pe, L, i, p):
            if L.causal:
                pe.wait_ge(L.stacks_loaded[p], 16 * L.loads * (i // 2 + 1))
            else:
                pe.wait_ge(L.aug_loaded[p], 16 * 2 * (i // 2 + 1))

        def pe_values(pe, L, i, s):
            qc, kt, hp, q0, w, last_step = L.steps[s]
            if L.hi_on[s] == "act":
                pe.wait_ge(L.act_hi, L.count(L.hi_on, "act", i, s))
            lo = L.dve_lo if L.lo_on[s] == "dve" else L.pool_lo
            pe.wait_ge(lo, L.count(L.lo_on, L.lo_on[s], i, s))
            if hp == 0 and L.steps.index([x for x in L.steps if x[1] == kt][0]) == s:
                pe.wait_ge(L.v_staged, KT * i + kt + 1)
            if kt == 0 and hp == 0:
                pe.wait_ge(L.o_free, CPB * i + qc + 1)
            for a in range(2):
                j = 2 * hp + a
                for k, half in enumerate((p_hi, p_lo)):
                    last = nc.tensor.matmul(o_bank(L, qc)[:, q0 - qc * CH:q0 - qc * CH + w],
                                            v_st[:, kt, j * P:(j + 1) * P], half[s % NP][:, a, 0:w],
                                            start=(kt == 0 and j == 0 and k == 0),
                                            stop=(last_step and a == 1 and k == 1))
            last.then_inc(L.pv_done, 1)

        def pe_round(pe, L, i, p, prev, nxt):
            base = L.spare_base(i) if prev else len(L.turn)
            n0 = 1 if prev else 0
            for s in range(L.S):
                ahead = L.around(i, s + AHEAD, prev, nxt)
                if ahead:
                    if ahead[1] == 0:
                        pe_loaded(pe, L, ahead[0], 1 - p)
                    pe_scores(pe, L, ahead[0], p if s + AHEAD < L.S else 1 - p, ahead[1])
                jobs = list(L.max_jobs_at(s)) if nxt else []
                if nxt and s == L.max_from and not L.causal:
                    pe.wait_ge(L.stacks_loaded[1 - p], 16 * L.loads * ((i + 1) // 2 + 1))
                for m in jobs[:1]:
                    pe_max_job(pe, L, i + 1, 1 - p, m)
                pe_values(pe, L, i, s)
                for m in jobs[1:]:
                    pe_max_job(pe, L, i + 1, 1 - p, m)
                if prev and s == L.norm_prev:
                    pe_norm(pe, L, CPB * i - 1, base)
                if s == L.norm_0:
                    pe_norm(pe, L, CPB * i, base + n0)
                if nxt and s in L.turn:
                    h = L.turn.index(s)
                    pe_turn(pe, L, i + 1, h, base + n0 + 1 + h)

        def pe_attention(pe, L):
            pe.wait_ge(L.stacks_loaded[0], 16 * L.loads)
            if not L.causal:
                pe.wait_ge(ones_loaded, 16 * 2 * HG)
                for m in range(L.max_jobs):
                    pe_max_job(pe, L, 0, 0, m)
                for h in range(2):
                    pe_turn(pe, L, 0, h, h)
            pe_loaded(pe, L, 0, 0)
            for s in range(AHEAD):
                pe_scores(pe, L, 0, 0, s)
            pe_round(pe, L, 0, 0, False, True)
            with pe.Fori(0, NG // 2 - 1) as u:
                pe_round(pe, L, 2 * u + 1, 1, True, True)
                pe_round(pe, L, 2 * u + 2, 0, True, True)
            pe_round(pe, L, NG - 1, 1, True, False)
            pe_norm(pe, L, CPB * NG - 1, L.spare_base(NG - 1) + 2)

        def act_exp(act, L, i, s):
            w = L.steps[s][4]
            act.wait_ge(L.scores_ready, i * L.S + s + 1)
            act.wait_ge(L.pv_done, i * L.S + s + 1)
            nc.scalar.activation(probs[s % NP][:, :, 0:w], score[s % NS][:, :, 0:w], ACT.Exp,
                                 scale=SCALE).then_inc(L.exp_done, 1)

        def wait_probs(eng, L, i, s):
            if L.causal:
                eng.wait_ge(L.clip_done, i * L.S + s + 1)
            else:
                eng.wait_ge(L.exp_done, NS + i * L.S + s + 1)

        def act_hi(act, L, i, s):
            if L.hi_on[s] != "act":
                return
            w = L.steps[s][4]
            wait_probs(act, L, i, s)
            nc.scalar.activation(p_hi[s % NP][:, :, 0:w], probs[s % NP][:, :, 0:w],
                                 ACT.Copy).then_inc(L.act_hi, 1)

        def act_turn(act, L, half, job):
            act.wait_ge(L.spare_ready, job + 1)
            nc.scalar.activation(negmax_t[:, half * CH:(half + 1) * CH], bank[3][0:2 * HG, :],
                                 ACT.Copy).then_inc(L.spare_free, 1)

        def act_round(act, L, i, p, prev, nxt):
            base = (L.spare_base(i) + 2) if prev else len(L.turn) + 1
            for s in range(L.S):
                ahead = L.around(i, s + AHEAD, prev, nxt)
                if ahead:
                    act_exp(act, L, *ahead)
                ahead = L.around(i, s + AHEAD - (1 if L.causal else 0), prev, nxt)
                if ahead:
                    act_hi(act, L, *ahead)
                if nxt and s in L.turn:
                    h = L.turn.index(s)
                    if h == 0:
                        act.wait_ge(L.aug_loaded[p], 32 * (i // 2 + 1))
                    act_turn(act, L, h, base + h)

        def act_attention(act, L):
            if not L.causal:
                act_turn(act, L, 0, 0)
                act_turn(act, L, 1, 1)
            for s in range(AHEAD):
                act_exp(act, L, 0, s)
                if not L.causal or s < AHEAD - 1:
                    act_hi(act, L, 0, s)
            act_round(act, L, 0, 0, False, True)
            with act.Fori(0, NG // 2 - 1) as u:
                act_round(act, L, 2 * u + 1, 1, True, True)
                act_round(act, L, 2 * u + 2, 0, True, True)
            act_round(act, L, NG - 1, 1, True, False)

        dve_chain = [None]

        def dve_clip(dve, L, i, s):
            qc, kt, hp, q0, w, _ = L.steps[s]
            dve.wait_ge(L.exp_done, NS + i * L.S + s + 1)
            e = probs[s % NP]
            ins = nc.vector.tensor_scalar(e[:, :, 0:w], e[:, :, 0:w], float(np.exp(-CLIP)),
                                          float(np.exp(CLIP)), ALU.max, ALU.min)
            if q0 == kt * P:
                dve_chain[0].link(ins)
                ins = nc.vector.tensor_tensor(e[:, :, 0:P], e[:, :, 0:P],
                                              tri[:, None, :].broadcast_to([P, 2, P]), ALU.mult)
            ins.then_inc(L.clip_done, 1)

        def dve_hi(dve, L, i, s):
            if L.hi_on[s] != "dve":
                return
            w = L.steps[s][4]
            wait_probs(dve, L, i, s)
            nc.vector.tensor_copy(p_hi[s % NP][:, :, 0:w], probs[s % NP][:, :, 0:w]).then_inc(L.dve_hi, 1)

        def lower_half(eng, engine, L, i, s, who, done):
            if L.lo_on[s] != who:
                return
            w = L.steps[s][4]
            hi_done = L.act_hi if L.hi_on[s] == "act" else L.dve_hi
            eng.wait_ge(hi_done, L.count(L.hi_on, L.hi_on[s], i, s))
            engine.tensor_tensor(p_lo[s % NP][:, :, 0:w], probs[s % NP][:, :, 0:w],
                                 p_hi[s % NP][:, :, 0:w].bitcast(F32), ALU.subtract).then_inc(done, 1)

        def dve_norm(dve, L, job, tile, g):
            c = dve_chain[0]
            turned = bank[3][:, :].rearrange("p (t j c) -> p t j c", t=TPC, j=HG)
            dve.wait_ge(L.spare_ready, job + 1)
            nc.vector.reciprocal(o_rcp[:, :, :], turned[:, :, :, DK])
            c.link(nc.vector.tensor_copy(o_lo[:, :, :, :], turned[:, :, :, LO:LO + DK]))
            c.link(nc.vector.tensor_tensor(o_sum[:, :, :, :], turned[:, :, :, 0:DK], o_lo[:, :, :, :], ALU.add))
            dve.sem_inc(L.spare_free, 1)
            dst = o_tm[:, bass.ds(tile, TPC), bass.ds(g * HG * DK, HG * DK)].rearrange("p t (j c) -> p t j c", c=DK)
            nc.vector.tensor_tensor(dst, o_sum[:, :, :, :],
                                    o_rcp[:, :, :, None].broadcast_to([P, TPC, HG, DK]),
                                    ALU.mult).then_inc(L.normed, 1)

        def dve_max_job(dve, L, i, m):
            qt, j, half = m // (HG * 2), m // 2 % HG, m % 2
            dve.wait_ge(L.smax_ready, i * L.max_jobs + m + 1)
            nc.vector.tensor_reduce(negmax_h[:, qt, j, half:half + 1], bank[1 + m % 2][:, :], AXX, ALU.max,
                                    negate=True).then_inc(L.smax_free, 1)

        def dve_negmax(dve, L, i):
            dve.wait_ge(L.smax_free, NS + (i + 1) * L.max_jobs)
            c = dve_chain[0]
            c.link(nc.vector.tensor_tensor(negmax[:, :, :], negmax_h[:, :, :, 0], negmax_h[:, :, :, 1], ALU.min))
            c.link(nc.vector.tensor_copy(negmax2[:, :, 0:HG].bitcast(F32R), negmax[:, :, :]))
            nc.vector.tensor_tensor(negmax2[:, :, HG:2 * HG].bitcast(F32R), negmax[:, :, :],
                                    negmax2[:, :, 0:HG], ALU.subtract).then_inc(L.negmax_ready, 1)

        def clips(L, steps):
            return sum(L.causal and L.steps[s][3] == L.steps[s][1] * P for s in steps)

        def links(L, prev, nxt):
            n = 2 * (1 + prev) + (2 if nxt and not L.causal else 0)
            return n + clips(L, range(0 if nxt else AHEAD, L.S))

        def dve_round(dve, L, i, prev, nxt):
            b, g = bg(i)
            base = L.spare_base(i) if prev else len(L.turn)
            n0 = 1 if prev else 0
            for s, (qc, kt, hp, q0, w, last_step) in enumerate(L.steps):
                if last_step:
                    dve.wait_ge(L.pv_done, NP + i * L.S + s + 1)
                    nc.vector.tensor_copy(o_sb[:, :], o_bank(L, qc)[:, :]).then_inc(L.o_saved, 1)
                    dve.wait_ge(L.o_saved, CPB * i + qc + 1)
                    dve.sem_inc(L.o_free, 1)
                ahead = L.around(i, s + AHEAD, prev, nxt)
                if ahead:
                    if L.causal:
                        dve_clip(dve, L, *ahead)
                    dve_hi(dve, L, *ahead)
                if nxt:
                    for m in list(L.max_jobs_at(s))[:1]:
                        dve_max_job(dve, L, i + 1, m)
                ahead = L.around(i, s + AHEAD - 1, prev, nxt)
                if ahead:
                    lower_half(dve, nc.vector, L, *ahead, "dve", L.dve_lo)
                if nxt:
                    for m in list(L.max_jobs_at(s))[1:]:
                        dve_max_job(dve, L, i + 1, m)
                        if m == L.max_jobs - 1:
                            dve_negmax(dve, L, i + 1)
                if prev and s == L.norm_prev:
                    pb, pg = bg(i - 1)
                    dve_norm(dve, L, base, pb * KT + TPC, pg)
                if s == L.norm_0:
                    dve_norm(dve, L, base + n0, b * KT, g)

        def dve_attention(dve, L):
            c = dve_chain[0] = Chain(dve, L.chain)
            if not L.causal:
                for m in range(L.max_jobs):
                    dve_max_job(dve, L, 0, m)
                dve_negmax(dve, L, 0)
            for s in range(AHEAD):
                if L.causal:
                    dve_clip(dve, L, 0, s)
                dve_hi(dve, L, 0, s)
                if s < AHEAD - 1:
                    lower_half(dve, nc.vector, L, 0, s, "dve", L.dve_lo)
            dve_round(dve, L, 0, False, True)
            total = c.n
            per = links(L, True, True)
            with dve.Fori(0, NG // 2 - 1) as u:
                for k in range(2):
                    c.at(total + (2 * u + k) * per)
                    dve_round(dve, L, 2 * u + 1 + k, True, True)
                    assert c.n == per
            total += (NG - 2) * per
            c.at(total)
            dve_round(dve, L, NG - 1, True, False)
            dve_norm(dve, L, L.spare_base(NG - 1) + 2, (B - 1) * KT + TPC, G - 1)

        def pool_stage_v(pool, L, i, kt):
            b, g = bg(i)
            src = v_all[:, bass.ds(b * KT + kt, 1), bass.ds(g * HG * DK, HG * DK)].rearrange(
                "p t (j c) -> p (t j) c", c=DK)
            dst = v_st[:, kt, :].rearrange("p (j c) -> p j c", c=VW)
            nc.gpsimd.tensor_copy(dst[:, :, 0:DK], src).then_inc(v_upper, 1)
            pool.wait_ge(v_upper, L.n * NG * KT + KT * i + kt + 1)
            pool.sem_inc(apart_pool, 1)
            nc.gpsimd.tensor_tensor(dst[:, :, LO:LO + DK], src, dst[:, :, 0:DK].bitcast(F32),
                                    ALU.subtract).then_inc(L.v_staged, 1)

        def pool_round(pool, L, i, prev, nxt):
            for s in range(L.S):
                ahead = L.around(i, s + AHEAD - 1, prev, nxt)
                if ahead:
                    lower_half(pool, nc.gpsimd, L, *ahead, "pool", L.pool_lo)
                if nxt:
                    for kt in range(KT):
                        if L.v_used[kt] == s - 1 or (s == L.S - 1 and L.v_used[kt] == s):
                            pool.wait_ge(L.pv_done, NP + i * L.S + L.v_used[kt] + 1)
                            pool_stage_v(pool, L, i + 1, kt)

        def pool_attention(pool, L):
            if not L.causal:
                nc.gpsimd.memset(ones_t[:, :], 1.0)
                nc.gpsimd.memset(zeros_t[:, :], 0.0)
                for p in range(2):
                    nc.gpsimd.memset(q_st[p][:, :].bitcast(F32), 0.0)
            for p in range(2):
                nc.gpsimd.memset(k_st[p][:, :, :].bitcast(F32), 0.0).then_inc(L.zeroed, 1)
            nc.gpsimd.memset(v_st[:, :, :].bitcast(F32), 0.0).then_inc(fills, 1)
            pool.wait_ge(fills, FILLS + 2 * L.n + 1)
            nc.gpsimd.memset(v_st[:, :, :].bitcast(F32).rearrange("p t (j c) -> p t j c", c=VW)[:, :, :, DK:DK + 1],
                             1.0).then_inc(fills, 1)
            pool.wait_ge(fills, FILLS + 2 * L.n + 2)
            for kt in range(KT):
                pool_stage_v(pool, L, 0, kt)
            for s in range(AHEAD - 1):
                lower_half(pool, nc.gpsimd, L, 0, s, "pool", L.pool_lo)
            pool_round(pool, L, 0, False, True)
            with pool.Fori(0, NG // 2 - 1) as u:
                pool_round(pool, L, 2 * u + 1, True, True)
                pool_round(pool, L, 2 * u + 2, True, True)
            pool_round(pool, L, NG - 1, True, False)

        def sp_load_stacks(sp, L, i, p):
            b, g = bg(i)
            for j in range(HG):
                def halves(scr, first, n):
                    return scr[L.n][bass.ds(b, 1), first:first + n, bass.ds(g * HG * DK + j * DK, DK), :].rearrange(
                        "b t c n -> (b t) c n")
                r = SLOT * j
                if L.causal:
                    for t in range(2):
                        rt = slice(r + 2 * DK * t, r + 2 * DK * (t + 1))
                        sp.dma_start(k_st[p][rt, j, :].bitcast(F32), halves(k_scr, 0, 2)).then_inc(L.stacks_loaded[p], 16)
                        sp.dma_start(q_st[p][rt, :].bitcast(F32),
                                     halves(q_scr, t, 1).broadcast_to([2, DK, T])).then_inc(L.stacks_loaded[p], 16)
                else:
                    rt = slice(r, r + 3 * DK)
                    sp.dma_start(k_st[p][rt, j, :].bitcast(F32), halves(k_scr, 0, 3)).then_inc(L.stacks_loaded[p], 16)
                    sp.dma_start(q_st[p][rt, :].bitcast(F32), halves(q_scr, 0, 3)).then_inc(L.stacks_loaded[p], 16)
            if not L.causal:
                for k in range(2):
                    sp.dma_start(aug_rows(p, k), zeros_t[:, :]).then_inc(L.stacks_loaded[p], 16)

        def aug_rows(p, k):
            r = 3 * DK + k
            return q_st[p][r:r + SLOT * (HG - 1) + 1:SLOT, :].bitcast(F32)

        def sp_load_aug(sp, L, i, p):
            sp.wait_ge(L.spare_free, 1 + (len(L.turn) if isinstance(i, int) and i == 0
                                          else L.spare_base(i)))
            for k in range(2):
                sp.dma_start(aug_rows(p, k), negmax_t[k * HG:(k + 1) * HG, :].bitcast(F32)).then_inc(L.aug_loaded[p], 16)

        def sp_attention(sp, L):
            for p in range(2):
                sp.wait_ge(L.zeroed, p + 1)
                if not L.causal:
                    for j in range(HG):
                        r = SLOT * j + 3 * DK
                        sp.dma_start(k_st[p][r:r + 2, j, :].bitcast(F32), ones_t[0:2, :]).then_inc(ones_loaded, 16)
                sp_load_stacks(sp, L, p, p)
            if L.causal:
                for t, name in WEIGHTS:
                    sp.dma_start(t[tuple(slice(None) for _ in t.shape)], d[name]).then_inc(w_loaded, 16)
                sp.dma_start(x_tm[:, :, :], x_tiles).then_inc(w_loaded, 16)
                sp.dma_start(b_o1[:, :], d["b_o1"].broadcast_to([P, D])).then_inc(w_loaded, 16)
                sp.dma_start(rb2[:, :], d["rb2"].broadcast_to([P, E1])).then_inc(w_loaded, 16)
            else:
                sp_load_aug(sp, L, 0, 0)
                sp_load_aug(sp, L, 1, 1)
            with sp.Fori(0, NG // 2 - 1) as u:
                for k in range(2):
                    i = 2 * u + 2 + k
                    sp.wait_ge(L.scores_ready, (i - 1) * L.S)
                    sp_load_stacks(sp, L, i, k)
                    if not L.causal:
                        sp_load_aug(sp, L, i, k)

        def pe_turn_tiles(dst, src):
            for t in range(TPC):
                last = nc.tensor.transpose(dst[:, t * P:(t + 1) * P], src[:, t, :], ident[:, :])
            return last

        def pe_qkv(st, w, x, par):
            for a in range(2):
                nc.tensor.matmul(hbank[2 * par + a], w[:, a, :], x[:, :], start=True, stop=True)
            for t in range(TPC):
                last = nc.tensor.matmul(bank[par][:, t * P:(t + 1) * P], x[:, t * P:(t + 1) * P], w[:, 2, :],
                                        start=True, stop=True)
            last.then_inc(st.qkv_ready, 1)

        def sp_store_halves(sp, st, n, c, b, hh):
            sp.wait_ge(st.halves_lo, 2 * (c + 1))
            sp.wait_ge(st.halves_hi, 2 * (c + 1))
            for a, scr, order in ((0, q_scr, "hhl"), (1, k_scr, "hlh")):
                for t, what in enumerate(order):
                    src = qk_hi[a] if what == "h" else qk_lo[a]
                    dst = scr[n][bass.ds(b, 1), t, :, hh * CH:(hh + 1) * CH].rearrange("b c n -> (b c) n")
                    sp.dma_start(dst, src[:, :]).then_inc(st.stored, 16)
        STORES = 6 * 16

        def sp_store_pair(sp, st, c, b, hh):
            sp.wait_ge(st.halves_lo, 2 * (c + 1))
            sp.wait_ge(st.halves_hi, 2 * (c + 1))
            for a, scr in ((0, q_scr), (1, k_scr)):
                for t, half in enumerate((qk_hi, qk_lo)):
                    dst = scr[0][bass.ds(b, 1), t, :, hh * CH:(hh + 1) * CH].rearrange("b c n -> (b c) n")
                    sp.dma_start(dst, half[2 * hh + a][:, :]).then_inc(st.pair_stored[hh], 16)
        PAIR = 4 * 16

        class Beside:
            pass

        plan = [Beside(), Beside()]
        for pl, steps in ((plan[0], (1, 2, 3, 4, 5, 6, 7, 8, 10, 11, None, 12, 13, 14)),
                          (plan[1], (1, 2, None, None, None, None, 3, 4, 6, 7, 8, 10, 12, 13))):
            (pl.y_turn, pl.norm2, pl.x2_turn, pl.q, pl.k, pl.v,
             pl.o_turn, pl.o_proj, pl.norm, pl.x_turn, pl.hidden, pl.router, pl.weigh, pl.g_turn) = steps

        SPC = NH
        n_exp = [E0, E1]

        def wait_used(eng, signal, count):
            if not isinstance(count, int) or count > 0:
                eng.wait_ge(signal, count)

        def slice_of(n):
            return slice(n * P, (n + 1) * P)

        def pe_hidden(pe, st, c, par, n, layer):
            pe.wait_ge(st.s_done, c * SPC + n + 1)
            if n == 0:
                pe.wait_ge(st.x_lower, c + 1)
            if layer == 0:
                pe.wait_ge(st.u_done, c * SPC + n + 1)
            for k in range(2 if layer == 0 else 1):
                for a, (w, x) in enumerate(((w_hi[k], x_hi[par]), (w_lo[k], x_hi[par]), (w_hi[k], x_lo[par]))):
                    last = nc.tensor.matmul(hbank[2 * k + n % 2], w[:, slice_of(n)], x[:, :], start=(a == 0),
                                            stop=(a == 2))
            last.then_inc(st.h_ready, 1)

        def pe_gate_rows(pe, st, c, e, layer):
            if e == 0:
                pe.wait_ge(st.gate_t, c + 1)
            pe.wait_ge(st.gbc_saved, c * n_exp[layer] + e + 1)
            nc.tensor.matmul(bank[1][:, :], expert_row[:, e, :], gate_t[:, :], start=True,
                             stop=True).then_inc(st.gbc_ready, 1)

        def pe_beside(pe, st, n, back, front, layer):
            pl = plan[layer]
            if back is not None:
                if n == pl.y_turn:
                    pe.wait_ge(st.y_saved, back + 2)
                    for t in range(TPC):
                        last = nc.tensor.transpose(bank[3][:, slice_of(t)], y_sb[:, slice_of(t)], ident[:, :])
                    last.then_inc(st.y_turned, 1)
                if n == pl.x2_turn:
                    pe.wait_ge(st.norm2, back + 1)
                    pe_turn_tiles(bank[2], x_out).then_inc(st.xt2_turned, 1)
                for k, at in enumerate((pl.q, pl.k)):
                    if n == at:
                        pe.wait_ge(st.xt2_ready, back + 1)
                        if k == 1:
                            pe.wait_ge(st.rot_done, 2 * back + 1)
                        for a in range(2):
                            last = nc.tensor.matmul(bank[2 + a][:, :], w_qkv1[:, 2 * k + a, :], xt2[:, :],
                                                    start=True, stop=True)
                        last.then_inc(st.qk_ready, 1)
                if n == pl.v:
                    pe.wait_ge(st.rot_done, 2 * back + 2)
                    for t in range(TPC):
                        last = nc.tensor.matmul(bank[2][:, slice_of(t)], xt2[:, slice_of(t)], w_qkv1[:, 4, :],
                                                start=True, stop=True)
                    last.then_inc(st.v_ready, 1)
            if front is not None:
                if n == pl.o_turn:
                    pe.wait_ge(st.o_in, front + 1)
                    pe_turn_tiles(bank[3], os_).then_inc(st.o_turned, 1)
                if n == pl.o_proj:
                    pe.wait_ge(st.ot_ready, front + 1)
                    if layer == 0 and back is not None:
                        pe.wait_ge(st.v_saved, back + 1)
                    for t in range(TPC):
                        last = nc.tensor.matmul(bank[2][:, slice_of(t)], ot[:, slice_of(t)], w_o[layer][:, :],
                                                start=True, stop=True)
                    last.then_inc(st.o_proj, 1)
                if n == pl.x_turn:
                    pe.wait_ge(st.norm, front + 1)
                    pe_turn_tiles(bank[3], xs_now(front_par[0])).then_inc(st.x_turned, 1)
                if n == pl.hidden:
                    pe.wait_ge(st.xt_ready, front + 1)
                    pe.wait_ge(st.x_upper, front + 1)
                    for f in range(2):
                        last = nc.tensor.matmul(bank[2 + f][:, :], rw1[:, slice_of(f)], xt[0][:, :], start=True,
                                                stop=True)
                    last.then_inc(st.router_h, 1)
                if n == pl.router:
                    if layer == 0:
                        pe.wait_ge(st.xt_ready, front + 1)
                        for t in range(TPC):
                            last = nc.tensor.matmul(bank[2][:, t * 8:t * 8 + 8], xt[0][:, slice_of(t)], wg[:, :],
                                                    start=True, stop=True)
                    else:
                        pe.wait_ge(st.rh_ready, front + 1)
                        for t in range(TPC):
                            for f in range(2):
                                last = nc.tensor.matmul(bank[2][:, t * E1:(t + 1) * E1], rh[:, f, slice_of(t)],
                                                        rw2[:, f, :], start=(f == 0), stop=(f == 1))
                    last.then_inc(st.router_in, 1)
                if n == pl.g_turn:
                    pe.wait_ge(st.gates, front + 1)
                    for t in range(TPC):
                        last = nc.tensor.transpose(bank[3][0:2 * E0, slice_of(t)], g_halves[:, t, :], ident[:, :])
                    last.then_inc(st.gates_turned, 1)
                if n == SPC - 1:
                    pe_gate_rows(pe, st, front, 0, layer)

        front_par = [0]

        def xs_now(par):
            return xs[par]

        def pe_chunk(pe, st, c, par, back, front, layer):
            per = SPC // n_exp[layer]
            w = w3 if layer == 0 else we2
            front_par[0] = 1 - par
            for n in range(SPC):
                pe_beside(pe, st, n, back, front, layer)
                e = n // per + 1
                if n % per == per - 2 and e < n_exp[layer]:
                    pe_gate_rows(pe, st, c, e, layer)
                if n + 1 < SPC:
                    pe_hidden(pe, st, c, par, n + 1, layer)
                elif front is not None:
                    pe_hidden(pe, st, front, 1 - par, 0, layer)
                if n == 0:
                    pe.wait_ge(st.y_saved, c + 1)
                    if layer == 1:
                        nc.tensor.matmul(bank[0][:, :], be2[:, :], gate_t[:, :].bitcast(F32), start=True, stop=False)
                pe.wait_ge(st.hid_ready, c * SPC + n + 1)
                nc.tensor.matmul(bank[0][:, :], w[:, n, :], hid[n % 2][:, :], start=(layer == 0 and n == 0),
                                 stop=(n == SPC - 1)).then_inc(st.y_done, 1)

        def pe_end(pe, st, layer):
            front_par[0] = 0
            pe.wait_ge(rows_ready, 1)
            for n in range(SPC):
                pe_beside(pe, st, n, None, 0, layer)
            pe.wait_ge(w_lower, 2 if layer == 0 else 3)
            if layer == 1:
                pe.wait_ge(we2_loaded, 16)
            pe_hidden(pe, st, 0, 0, 0, layer)
            pe_chunk(pe, st, 0, 0, None, 1, layer)
            with pe.Fori(0, B - 1) as u:
                pe_chunk(pe, st, 2 * u + 1, 1, 2 * u, 2 * u + 2, layer)
                pe_chunk(pe, st, 2 * u + 2, 0, 2 * u + 1, 2 * u + 3, layer)
            pe_chunk(pe, st, 2 * B - 1, 1, 2 * B - 2, None, layer)
            for n in range(SPC):
                pe_beside(pe, st, n, 2 * B - 1, None, layer)

        def act_beside(act, st, n, back, front, par, layer):
            pl = plan[layer]
            if back is not None:
                if n == pl.x2_turn:
                    act.wait_ge(st.xt2_turned, back + 1)
                    nc.scalar.activation(xt2[:, :], bank[2][:, :], ACT.Copy).then_inc(st.xt2_ready, 1)
                if layer == 0 and n in (pl.k, pl.v):
                    a = 0 if n == pl.k else 1
                    act.wait_ge(st.rot_sum, 2 * back + a + 1)
                    act.wait_ge(st.done, back + 1)
                    nc.scalar.activation(qk_hi[a][:, :].bitcast(F32R), rot[2 * a][:, :],
                                         ACT.Copy).then_inc(st.halves_hi, 1)
            if front is not None:
                if n == pl.o_turn:
                    act.wait_ge(st.o_turned, front + 1)
                    nc.scalar.activation(ot[:, :], bank[3][:, :], ACT.Copy).then_inc(st.ot_ready, 1)
                if n == pl.x_turn:
                    act.wait_ge(st.x_turned, front + 1)
                    nc.scalar.activation(xt[0][:, :], bank[3][:, :], ACT.Copy).then_inc(st.xt_ready, 1)
                    nc.scalar.activation(x_hi[par][:, :], bank[3][:, :], ACT.Copy).then_inc(st.x_upper, 1)
                if n == pl.hidden:
                    act.wait_ge(st.router_h, front + 1)
                    for f in range(2):
                        last = nc.scalar.activation(rh[:, f, :], bank[2 + f][:, :], ACT.Gelu, bias=rb1[:, f:f + 1])
                    last.then_inc(st.rh_ready, 1)
                if n == pl.router + 1:
                    act.wait_ge(st.gate_pre, front + 1)
                    if layer == 0:
                        nc.scalar.activation(p12[:, 1, :], lead[:, :], ACT.Exp).then_inc(st.gate_exp, 1)
                    else:
                        nc.scalar.activation(e_sm[:, :, :], sc8[:, :, 0:E1], ACT.Exp).then_inc(st.gate_exp, 1)
                if n == pl.g_turn:
                    act.wait_ge(st.gates_turned, front + 1)
                    nc.scalar.activation(gate_t[:, :], bank[3][0:2 * E0, :], ACT.Copy).then_inc(st.gate_t, 1)
                if n == SPC - 1:
                    act_gate_rows(act, st, front, 0, layer)

        def act_gate_rows(act, st, c, e, layer):
            act.wait_ge(st.gbc_ready, c * n_exp[layer] + e + 1)
            used = c * SPC + (e - 1) * (SPC // n_exp[layer])
            if isinstance(used, int):
                if used > 0:
                    act.wait_ge(st.hid_ready, used)
            else:
                act.wait_ge(st.hid_ready, used)
            nc.scalar.activation(gate_bc[e % 2][:, :], bank[1][:, :], ACT.Copy).then_inc(st.gbc_saved, 1)

        def act_chunk(act, st, c, par, back, front, layer):
            per = SPC // n_exp[layer]
            for n in range(SPC):
                act.wait_ge(st.h_ready, c * SPC + n + 1)
                wait_used(act, st.hid_ready, c * SPC + n - 1)
                if layer == 0:
                    nc.scalar.activation(act_s[n % 2][:, :], hbank[n % 2], ACT.Silu).then_inc(st.s_done, 1)
                else:
                    nc.scalar.activation(act_s[n % 2][:, :], hbank[n % 2], ACT.Gelu,
                                         bias=be1[:, n:n + 1]).then_inc(st.s_done, 1)
                act_beside(act, st, n, back, front, 1 - par, layer)
                e = n // per + 1
                if n % per == per - 2 and e < n_exp[layer]:
                    act_gate_rows(act, st, c, e, layer)
            act.wait_ge(st.y_done, (c + 1) * SPC)
            nc.scalar.activation(y_sb[:, :], bank[0][:, :], ACT.Copy).then_inc(st.y_saved, 1)

        def act_end(act, st, layer):
            for k in range(2 if layer == 0 else 1):
                act.wait_ge(raw_loaded[k], 16 * (layer + 1))
                nc.scalar.activation(w_hi[k][:, :], w_raw[k][:, :], ACT.Copy).then_inc(w_upper, 1)
            for n in range(SPC):
                act_beside(act, st, n, None, 0, 0, layer)
            act_chunk(act, st, 0, 0, None, 1, layer)
            with act.Fori(0, B - 1) as u:
                act_chunk(act, st, 2 * u + 1, 1, 2 * u, 2 * u + 2, layer)
                act_chunk(act, st, 2 * u + 2, 0, 2 * u + 1, 2 * u + 3, layer)
            act_chunk(act, st, 2 * B - 1, 1, 2 * B - 2, None, layer)
            for n in range(SPC):
                act_beside(act, st, n, 2 * B - 1, None, 0, layer)

        def dve_stats(c_, x, k, signal):
            for t in range(TPC):
                ins = nc.vector.bn_stats(st6[:, k, t, :], x[:, t, :])
            c_.link(ins, apart)
            for t in range(TPC):
                ins = nc.vector.bn_aggr(mv[:, k, t, :], st6[:, k, t, :])
            ins.then_inc(signal, 1)

        def dve_normalise(x, o, k):
            for t in range(TPC):
                ins = nc.vector.tensor_scalar(o[:, t, :], x[:, t, :], mv[:, k, t, 0:1], rstd[:, k, t:t + 1],
                                              ALU.subtract, ALU.mult)
            return ins

        def dve_top2(dve, ch, st, c, layer):
            dve.wait_ge(st.router_in, c + 1)
            if layer == 0:
                ch.link(nc.vector.tensor_copy(sc8[:, :, :], bank[2][:, 0:TPC * 8].rearrange("p (t e) -> p t e", e=8)),
                        apart)
                dve_best(ch)
                nc.vector.tensor_tensor(lead[:, :], mx8[:, :, 1], mx8[:, :, 0], ALU.subtract).then_inc(st.gate_pre, 1)
            else:
                lg = bank[2][:, 0:TPC * E1].rearrange("p (t e) -> p t e", e=E1)
                ch.link(nc.vector.tensor_tensor(sc8[:, :, 0:E1], lg, rb2[:, None, :].broadcast_to([P, TPC, E1]), ALU.add))
                ch.link(nc.vector.tensor_reduce(lead[:, :], sc8[:, :, 0:E1], AXX, ALU.max))
                nc.vector.tensor_tensor(sc8[:, :, 0:E1], sc8[:, :, 0:E1],
                                        lead[:, :, None].broadcast_to([P, TPC, E1]),
                                        ALU.subtract).then_inc(st.gate_pre, 1)

        def dve_best(ch):
            for t in range(TPC):
                ins = nc.vector.max(mx8[:, t, :], sc8[:, t, :])
            ch.link(ins, apart)
            for t in range(TPC):
                ins = nc.vector.max_index(ix8[:, t, :], mx8[:, t, :], sc8[:, t, :])
            ch.link(ins)
            ch.link(nc.vector.tensor_copy(ixf[:, :, :], ix8[:, :, :]))

        def dve_weigh(dve, ch, st, c, layer):
            dve.wait_ge(st.gate_exp, c + 1)
            if layer == 0:
                ch.link(nc.vector.tensor_scalar(p12[:, 0, :], p12[:, 1, :], 1.0, None, ALU.add))
                ch.link(nc.vector.reciprocal(p12[:, 0, :], p12[:, 0, :]))
                ch.link(nc.vector.tensor_tensor(p12[:, 1, :], p12[:, 1, :], p12[:, 0, :], ALU.mult))
            else:
                ch.link(nc.vector.tensor_reduce(lead[:, :], e_sm[:, :, :], AXX, ALU.add))
                ch.link(nc.vector.reciprocal(lead[:, :], lead[:, :]))
                ch.link(nc.vector.tensor_tensor(sc8[:, :, 0:E1], e_sm[:, :, :],
                                                lead[:, :, None].broadcast_to([P, TPC, E1]), ALU.mult), apart)
                dve_best(ch)
                ch.link(nc.vector.tensor_copy(p12[:, :, :], mx8[:, :, 0:2].rearrange("p t k -> p k t")))
            for t in range(TPC):
                for k in range(2):
                    ins = nc.vector.tensor_scalar(gts[:, k, t, :], iota8[:, :], ixf[:, t, k:k + 1],
                                                  p12[:, k, t:t + 1], ALU.is_equal, ALU.mult)
            ch.link(ins)
            ch.link(nc.vector.tensor_tensor(gts[:, 0, :, :], gts[:, 0, :, :], gts[:, 1, :, :], ALU.add))
            ch.link(nc.vector.tensor_copy(g_halves[:, :, 0:E0].bitcast(F32R), gts[:, 0, :, :]))
            nc.vector.tensor_tensor(g_halves[:, :, E0:2 * E0].bitcast(F32R), gts[:, 0, :, :], g_halves[:, :, 0:E0],
                                    ALU.subtract).then_inc(st.gates, 1)

        def dve_beside(dve, st, n, back, front, par, layer):
            pl = plan[layer]
            fc, bc = dve_front[0], dve_back[0]
            if back is not None:
                if n == pl.y_turn:
                    bc.at(back * BACK_LINKS)
                    dve.wait_ge(st.y_turned, back + 1)
                    bc.link(nc.vector.tensor_tensor(res[1][:, :, :], xs[par][:, :, :],
                                                    bank[3][:, :].rearrange("p (t c) -> p t c", c=D), ALU.add))
                    dve_stats(bc, res[1], 1, st.stats2)
                    assert bc.n == BACK_LINKS
                if n == pl.norm2:
                    dve.wait_ge(st.rstd2, back + 1)
                    if layer == 1:
                        dve.wait_ge(st.done, back + 1)
                    dve.sem_inc(apart, 1)
                    dve_normalise(res[1], x_out, 1).then_inc(st.norm2, 1)
                    if layer == 0:
                        dve.wait_ge(st.norm2, back + 1)
                        dve.sem_inc(apart, 1)
                        nc.vector.tensor_copy(x_tm[:, bass.ds(back * TPC, TPC), :],
                                              x_out[:, :, :]).then_inc(st.x_kept, 1)
                for a, at in enumerate((pl.q, pl.k)):
                    if n == at:
                        dve.wait_ge(st.qk_ready, 2 * back + a + 1)
                        half = slice(par * CH, (par + 1) * CH)
                        nc.vector.tensor_tensor(rot[2 * a][:, :], bank[2][:, :], rope_a[:, half], ALU.mult)
                        nc.vector.tensor_tensor(rot[2 * a + 1][:, :], bank[3][:, :], rope_b[:, half],
                                                ALU.mult).then_inc(st.rot_done, 1)
                if n == pl.v:
                    dve.wait_ge(st.v_ready, back + 1)
                    dve.sem_inc(apart, 1)
                    nc.vector.tensor_copy(v_all[:, bass.ds(back * TPC, TPC), :],
                                          bank[2][:, :].rearrange("p (t c) -> p t c", c=D)).then_inc(st.v_saved, 1)
                    for a in range(2):
                        dve.wait_ge(st.halves_hi, 2 * back + a + 1)
                        nc.vector.tensor_tensor(qk_lo[a][:, :].bitcast(F32R), rot[2 * a][:, :], qk_hi[a][:, :],
                                                ALU.subtract).then_inc(st.halves_lo, 1)
            if front is not None:
                if n == pl.o_turn - 1:
                    nc.vector.tensor_copy(os_[:, :, :], o_tm[:, bass.ds(front * TPC, TPC), :]).then_inc(st.o_in, 1)
                if n == pl.o_proj:
                    fc.at(front * FRONT_LINKS[layer] + layer)
                    dve.wait_ge(st.o_proj, front + 1)
                    dve.sem_inc(apart, 1)
                    fc.link(nc.vector.tensor_tensor(res[0][:, :, :], x_tm[:, bass.ds(front * TPC, TPC), :],
                                                    bank[2][:, :].rearrange("p (t c) -> p t c", c=D), ALU.add))
                    if layer == 1:
                        fc.link(nc.vector.tensor_tensor(res[0][:, :, :], res[0][:, :, :],
                                                        b_o1[:, None, :].broadcast_to([P, TPC, D]), ALU.add))
                    dve_stats(fc, res[0], 0, st.stats)
                if n == pl.norm:
                    dve.wait_ge(st.rstd, front + 1)
                    dve_normalise(res[0], xs[par], 0).then_inc(st.norm, 1)
                if n == pl.x_turn:
                    dve.wait_ge(st.x_upper, front + 1)
                    nc.vector.tensor_tensor(x_lo[par][:, :], xt[0][:, :], x_hi[par][:, :].bitcast(F32),
                                            ALU.subtract).then_inc(st.x_lower, 1)
                if n == pl.router:
                    dve_top2(dve, fc, st, front, layer)
                if n == pl.weigh:
                    dve_weigh(dve, fc, st, front, layer)
                    assert fc.n == FRONT_LINKS[layer], fc.n

        BACK_LINKS = 2
        FRONT_LINKS = [12, 15]
        dve_front, dve_back = [None], [None]

        def dve_chunk(dve, st, c, par, back, front, layer):
            per = SPC // n_exp[layer]
            for n in range(SPC):
                e = n // per
                if n % per == 0:
                    dve.wait_ge(st.gbc_saved, 1 + c * n_exp[layer] + e + 1)
                wait_used(dve, st.y_done, c * SPC + n - 1)
                if layer == 0:
                    dve.wait_ge(st.h_ready, c * SPC + n + 1)
                    nc.vector.tensor_tensor(lin_u[n % 2][:, :], hbank[2 + n % 2], gate_bc[e % 2][:, :],
                                            ALU.mult).then_inc(st.u_done, 1)
                    dve.wait_ge(st.u_done, NS + c * SPC + n + 1)
                    dve.wait_ge(st.s_done, NS + c * SPC + n + 1)
                    nc.vector.tensor_tensor(hid[n % 2][:, :], act_s[n % 2][:, :], lin_u[n % 2][:, :],
                                            ALU.mult).then_inc(st.hid_ready, 1)
                else:
                    dve.wait_ge(st.s_done, NS + c * SPC + n + 1)
                    nc.vector.tensor_tensor(hid[n % 2][:, :], act_s[n % 2][:, :], gate_bc[e % 2][:, :],
                                            ALU.mult).then_inc(st.hid_ready, 1)
                dve_beside(dve, st, n, back, front, 1 - par, layer)

        def dve_end(dve, st, layer):
            dve_front[0], dve_back[0] = Chain(dve, st.chain), Chain(dve, st.back_chain)
            if layer == 1:
                dve_front[0].link(nc.vector.memset(sc8[:, :, E1:8], -1.0))
            for n in range(SPC):
                dve_beside(dve, st, n, None, 0, 0, layer)
                if n == plan[layer].o_proj:
                    for k in range(2 if layer == 0 else 1):
                        dve.wait_ge(w_upper, 2 * layer + k + 1)
                        nc.vector.tensor_tensor(w_lo[k][:, :], w_raw[k][:, :], w_hi[k][:, :].bitcast(F32),
                                                ALU.subtract).then_inc(w_lower, 1)
            dve_chunk(dve, st, 0, 0, None, 1, layer)
            with dve.Fori(0, B - 1) as u:
                dve_chunk(dve, st, 2 * u + 1, 1, 2 * u, 2 * u + 2, layer)
                dve_chunk(dve, st, 2 * u + 2, 0, 2 * u + 1, 2 * u + 3, layer)
            dve_chunk(dve, st, 2 * B - 1, 1, 2 * B - 2, None, layer)
            for n in range(SPC):
                dve_beside(dve, st, n, 2 * B - 1, None, 1, layer)

        def pool_rstd(pool, pc, wait, sig, k, val):
            pool.wait_ge(wait, val)
            pool.sem_inc(apart_pool, 1)
            pc.link(nc.gpsimd.tensor_scalar(rstd[:, k, :], mv[:, k, :, 1], EPS, None, ALU.add))
            nc.gpsimd.tensor_tensor(rstd[:, k, :], rstd[:, k, :], mhalf[:, :], ALU.pow).then_inc(sig, 1)

        def pool_back(pool, pc, st, c, layer):
            pool_rstd(pool, pc, st.stats2, st.rstd2, 1, c + 1)
            if layer == 0:
                for a in range(2):
                    pool.wait_ge(st.rot_done, 2 * c + a + 1)
                    nc.gpsimd.tensor_tensor(rot[2 * a][:, :], rot[2 * a][:, :], rot[2 * a + 1][:, :],
                                            ALU.add).then_inc(st.rot_sum, 1)

        def pool_end(pool, st, layer):
            pc = Chain(pool, st.pool_chain)
            for c in range(2):
                pool_rstd(pool, pc, st.stats, st.rstd, 0, c + 1)
            with pool.Fori(0, 2 * B - 2) as c:
                pc.at(2 + 2 * c)
                pool_back(pool, pc, st, c, layer)
                pool_rstd(pool, pc, st.stats, st.rstd, 0, c + 3)
            for c in (2 * B - 2, 2 * B - 1):
                pc.at(2 + 2 * (2 * B - 2) + c - (2 * B - 2))
                pool_back(pool, pc, st, c, layer)

        @block.sync
        def _(sp):
            def load_x(c):
                sp.dma_start(xs[c % 2][:, :, :], x_tiles[:, bass.ds(c * TPC, TPC), :]).then_inc(st.x_in[c % 2], 16)

            st = stages[0]
            for t, name in FIRST:
                sp.dma_start(t[tuple(slice(None) for _ in t.shape)], d[name]).then_inc(first_loaded, 16)
            load_x(0)
            load_x(1)
            for t, name in CONSTS:
                sp.dma_start(t[tuple(slice(None) for _ in t.shape)], d[name]).then_inc(const_loaded, 16)
            with sp.Fori(0, B - 1) as b:
                for hh in range(2):
                    c = 2 * b + hh
                    sp_store_pair(sp, st, c, b, hh)
                    sp.wait_ge(st.x_turned, c + 1)
                    sp.dma_start(xs[hh][:, :, :],
                                 x_tiles[:, bass.ds((c + 2) * TPC, TPC), :]).then_inc(st.x_in[hh], 16)
            for hh in range(2):
                sp_store_pair(sp, st, 2 * (B - 1) + hh, B - 1, hh)
            for hh in range(2):
                sp.wait_ge(st.pair_stored[hh], PAIR * (B + 1))
            sp.sem_inc(st.done, 1)
            sp_attention(sp, layers[0])
            sp.wait_ge(layers[0].normed, CPB * NG)
            for k, name in enumerate(("w1", "w2")):
                sp.dma_start(w_raw[k][:, :], d[name]).then_inc(raw_loaded[k], 16)
            sp.dma_start(rope_a[:, :], d["rope_a"]).then_inc(w_loaded, 16)
            sp.dma_start(rope_b[:, :], d["rope_b"]).then_inc(w_loaded, 16)
            st = stages[1]
            with sp.Fori(0, B) as b:
                for hh in range(2):
                    c = 2 * b + hh
                    sp_store_halves(sp, st, 1, c, b, hh)
                    sp.wait_ge(st.stored, STORES * (c + 1))
                    sp.wait_ge(st.v_saved, c + 1)
                    sp.wait_ge(st.x_kept, c + 1)
                    sp.sem_inc(st.done, 1)
            sp_attention(sp, layers[1])
            sp.wait_ge(layers[1].normed, CPB * NG)
            sp.dma_start(w_raw[0][:, :], d["we1"]).then_inc(raw_loaded[0], 16)
            sp.dma_start(we2[:, :, :], d["we2"]).then_inc(we2_loaded, 16)
            st = stages[2]
            with sp.Fori(0, 2 * B) as c:
                sp.wait_ge(st.norm2, c + 1)
                sp.dma_start(out_tiles[:, bass.ds(c * TPC, TPC), :], x_out[:, :, :]).then_inc(st.stored, 16)
                sp.wait_ge(st.stored, 16 * (c + 1))
                sp.sem_inc(st.done, 1)

        @block.gpsimd
        def _(pool):
            nc.gpsimd.memset(mhalf[:, :], -0.5).then_inc(fills, 1)
            pool.wait_ge(rows_ready, 1)
            pool.wait_ge(stages[0].done, 1)
            pool.wait_ge(stages[0].v_saved, 2 * B + 2)
            pool_attention(pool, layers[0])
            pool_end(pool, stages[1], 0)
            pool.wait_ge(stages[1].done, 2 * B + 1)
            pool_attention(pool, layers[1])
            pool_end(pool, stages[2], 1)

        @block.scalar
        def _(act):
            st = stages[0]
            with act.Fori(0, B) as u:
                for par in range(2):
                    c = 2 * u + par
                    act.wait_ge(st.x_turned, c + 1)
                    nc.scalar.activation(xt[par][:, :], bank[3 - par][:, :], ACT.Copy).then_inc(st.xt_ready, 1)
                    act.wait_ge(st.qkv_ready, c + 1)
                    act.wait_ge(st.pair_stored[par], PAIR * (u + 1))
                    for a in range(2):
                        nc.scalar.activation(qk_hi[2 * par + a][:, :].bitcast(F32R), hbank[2 * par + a],
                                             ACT.Copy).then_inc(st.halves_hi, 1)
            act.wait_ge(const_loaded, ALL_CONSTS)
            nc.scalar.activation(expert_row[:, :, :], expert_raw[:, :, :], ACT.Copy).then_inc(rows_ready, 1)
            act.wait_ge(rows_ready, 1)
            act.wait_ge(stages[0].done, 1)
            act_attention(act, layers[0])
            act.wait_ge(w_loaded, ALL_W)
            act_end(act, stages[1], 0)
            act.wait_ge(stages[1].done, 2 * B + 1)
            act_attention(act, layers[1])
            act_end(act, stages[2], 1)

        @block.vector
        def _(dve):
            for L in layers:
                dve.sem_inc(L.exp_done, NS)
                dve.sem_inc(L.pv_done, NP)
                dve.sem_inc(L.o_free, 2 if L.causal else 1)
                dve.sem_inc(L.spare_free, 1)
            dve.sem_inc(layers[1].smax_free, NS)
            for st in stages[1:]:
                dve.sem_inc(st.s_done, NS)
                dve.sem_inc(st.gbc_saved, 1)
                dve.sem_inc(st.y_saved, 1)
                dve.sem_inc(st.done, 1)
            dve.sem_inc(stages[1].u_done, NS)
            for par in range(2):
                dve.sem_inc(stages[0].pair_stored[par], PAIR)
            dve.sem_inc(stages[0].v_saved, 2)
            dve.wait_ge(fills, FILLS)
            st = stages[0]
            with dve.Fori(0, B) as u:
                for par in range(2):
                    c = 2 * u + par
                    dve.wait_ge(st.qkv_ready, c + 1)
                    for a in range(2):
                        dve.wait_ge(st.halves_hi, 2 * c + a + 1)
                        nc.vector.tensor_tensor(qk_lo[2 * par + a][:, :].bitcast(F32R), hbank[2 * par + a],
                                                qk_hi[2 * par + a][:, :], ALU.subtract).then_inc(st.halves_lo, 1)
                    nc.vector.tensor_copy(v_all[:, bass.ds(c * TPC, TPC), :],
                                          bank[par][:, :].rearrange("p (t c) -> p t c", c=D)).then_inc(st.v_saved, 1)
            dve.wait_ge(const_loaded, ALL_CONSTS)
            dve.wait_ge(rows_ready, 1)
            dve.wait_ge(stages[0].done, 1)
            dve_attention(dve, layers[0])
            dve.wait_ge(w_loaded, ALL_W)
            dve.wait_ge(layers[0].normed, CPB * NG)
            dve_end(dve, stages[1], 0)
            dve.wait_ge(stages[1].done, 2 * B + 1)
            dve_attention(dve, layers[1])
            dve.wait_ge(layers[1].normed, CPB * NG)
            dve_end(dve, stages[2], 1)

        @block.tensor
        def _(pe):
            pe.wait_ge(first_loaded, 16 * len(FIRST))
            st = stages[0]
            with pe.Fori(0, B) as u:
                for par in range(2):
                    c = 2 * u + par
                    pe.wait_ge(st.x_in[par], 16 * (u + 1))
                    pe_turn_tiles(bank[3 - par], xs[par]).then_inc(st.x_turned, 1)
                    pe.wait_ge(st.xt_ready, c + 1)
                    pe.wait_ge(st.v_saved, c + 1)
                    pe_qkv(st, w_qkv0, xt[par], par)
            pe.wait_ge(st.v_saved, 2 * B + 2)
            pe.wait_ge(const_loaded, ALL_CONSTS)
            pe_attention(pe, layers[0])
            pe.wait_ge(w_loaded, ALL_W)
            pe_end(pe, stages[1], 0)
            pe.wait_ge(stages[1].done, 2 * B + 1)
            pe_attention(pe, layers[1])
            pe_end(pe, stages[2], 1)


_IN_NAMES = ["x", "ident", "tri", "expert_row", "iota8", "w_qkv0", "w_qkv1", "w_o0", "w_o1", "rope_a",
             "rope_b", "b_o1", "wg", "w1", "w2", "w3", "rw1", "rb1", "rw2", "rb2", "we1", "be1", "we2", "be2"]


def _layout(i):
    f = np.float32
    a = {k: np.asarray(v) for k, v in i.items()}
    c = np.ascontiguousarray
    o = {"x": a["L0_attn_x"].reshape(NTOK, D), "ident": np.eye(P, dtype=f)}
    o["tri"] = np.triu(np.ones((P, P), f))
    er = np.zeros((2 * E0, E0, P), f)
    for e in range(E0):
        er[e, e] = er[E0 + e, e] = 1
    o["expert_row"] = er
    o["iota8"] = np.tile(np.arange(E0, dtype=f), (P, 1))
    w = a["L0_attn_Wqkv"].reshape(3, P, D)
    o["w_qkv0"] = c(w.transpose(2, 0, 1))
    w = a["L1_attn_w_qkv"].reshape(3, H, DK // 2, 2, D)
    rows = [np.concatenate([w[s, :, :, t], w[s, :, :, t]], axis=1).reshape(P, D) for s in range(2) for t in range(2)]
    rows.append(a["L1_attn_w_qkv"][2 * P:])
    o["w_qkv1"] = c(np.stack(rows).transpose(2, 0, 1))
    inv = (f(1.0) / np.power(f(10000.0), np.arange(0, DK, 2, dtype=f) / f(DK))).astype(f)
    ang = np.outer(np.arange(T, dtype=f), inv).astype(f)
    cos, sin = np.cos(ang).astype(f).T, np.sin(ang).astype(f).T
    o["rope_a"] = c(np.tile(np.concatenate([cos, sin]), (H, 1)))
    o["rope_b"] = c(np.tile(np.concatenate([-sin, cos]), (H, 1)))
    o["w_o0"] = c(a["L0_attn_Wout"].T)
    o["w_o1"] = c(a["L1_attn_w_out"].T)
    o["b_o1"] = a["L1_attn_b_out"].reshape(1, D)
    o["wg"] = c(a["L0_ffn_Wg"].T)
    o["w1"] = c(a["L0_ffn_W1"].transpose(2, 0, 1)).reshape(P, NH * P)
    o["w2"] = c(a["L0_ffn_W2"].transpose(2, 0, 1)).reshape(P, NH * P)
    o["w3"] = c(a["L0_ffn_W3"].transpose(2, 0, 1).reshape(F0 // P, P, E0, D).transpose(1, 2, 0, 3).reshape(P, NH, D))
    o["rw1"] = a["L1_ffn_rW1"]
    o["rb1"] = c(a["L1_ffn_rb1"].reshape(2, P).T)
    o["rw2"] = c(a["L1_ffn_rW2"].reshape(2, P, E1).transpose(1, 0, 2))
    o["rb2"] = a["L1_ffn_rb2"].reshape(1, E1)
    o["we1"] = c(a["L1_ffn_We1"].transpose(1, 0, 2)).reshape(P, NH * P)
    o["be1"] = c(a["L1_ffn_be1"].reshape(NH, P).T)
    o["we2"] = c(a["L1_ffn_We2"].reshape(NH, P, D).transpose(1, 0, 2))
    o["be2"] = np.zeros((2 * E0, D), f)
    o["be2"][0:E1] = o["be2"][E0:E0 + E1] = a["L1_ffn_be2"]
    return {k: c(o[k]) for k in _IN_NAMES}


def kernel(**inputs):
    import concourse.bacc as _bacc
    from concourse.bass_utils import run_bass_kernel_spmd as _run

    nc = _bacc.Bacc("TRN2", target_bir_lowering=False, num_devices=1)
    arrays = {f"in_{k}": v for k, v in _layout(inputs).items()}
    aps = {k: nc.dram_tensor(f"in_{k}", arrays[f"in_{k}"].shape, F32, kind="ExternalInput").ap() for k in _IN_NAMES}
    out = nc.dram_tensor("out_dram", (NTOK, D), F32, kind="ExternalOutput").ap()
    build_program(nc, aps, out)
    r = _run(nc, [arrays], core_ids=[0])
    return np.asarray(r.results[0]["out_dram"]).reshape(B, T, D)
```

```python
from contextlib import ExitStack

import numpy as np

import concourse.bass as bass
from concourse import mybir

ALU = mybir.AluOpType
ACT = mybir.ActivationFunctionType
AXX = mybir.AxisListType.X
F32 = mybir.dt.float32
F32R = mybir.dt.float32r
U32 = mybir.dt.uint32

P = 128
B, T, D, H = 4, 1024, 128, 16
DK = D // H
NTOK = B * T
CH = 512
TPC = CH // P
CPB = T // CH
KT = T // P
NT = NTOK // P
HG = 4
G = H // HG
NG = B * G
SLOT = 32
E0, F0 = 8, 256
E1, F1 = 4, 512
NH = E0 * F0 // P
assert NH == E1 * F1 // P
SCALE = float(DK) ** -0.5
CLIP = 10.0
EPS = 1e-5
NS = 2
NP = 4
AHEAD = 3
VW = P + SLOT
LO = 16


def steps_of(causal):
    out = []
    for qc in range(CPB):
        for kt in range(KT if not causal else (qc + 1) * TPC):
            for hp in range(HG // 2):
                q0 = max(qc * CH, kt * P) if causal else qc * CH
                out.append([qc, kt, hp, q0, (qc + 1) * CH - q0, False])
        out[-1][5] = True
    return out


class Layer:

    def __init__(self, n, sem):
        self.n = n
        self.causal = n == 0
        self.steps = steps_of(self.causal)
        self.S = len(self.steps)
        self.loads = 4 * HG if self.causal else 2 * HG + 2
        assert self.S % NP == 0 and self.S % NS == 0
        self.last = [s for s, x in enumerate(self.steps) if x[5]]
        if self.causal:
            self.hi_on = ["dve" if s % 6 == 2 else "act" for s in range(self.S)]
            self.lo_on = ["pool" if s % 4 == 1 else "dve" for s in range(self.S)]
        else:
            self.hi_on = ["act"] * self.S
            self.lo_on = ["pool" if s % 2 else "dve" for s in range(self.S)]
        self.whole = [s for s in range(self.S) if s % 4 == 0 or self.steps[s][4] <= 2 * P] if self.causal else []
        for s in self.whole:
            self.hi_on[s] = self.lo_on[s] = None
        self.norm_prev, self.norm_0 = 2, self.last[0] + 3
        self.max_jobs = 0 if self.causal else KT * HG * 2
        self.max_step = 8
        self.turn_here = None if self.causal else 9
        self.turn_next = None if self.causal else 25
        self.jobs = 2 if self.causal else 4
        self.v_used = [max(s for s, x in enumerate(self.steps) if x[1] == kt) for kt in range(KT)]
        self.stacks_loaded = [sem(f"l{n}_stacks_loaded{p}") for p in range(2)]
        self.zeroed = sem(f"l{n}_zeroed")
        self.v_staged = sem(f"l{n}_v_staged")
        self.scores_ready = sem(f"l{n}_scores_ready")
        self.exp_done = sem(f"l{n}_exp_done")
        self.act_hi = sem(f"l{n}_act_hi")
        self.dve_hi = sem(f"l{n}_dve_hi")
        self.dve_lo = sem(f"l{n}_dve_lo")
        self.pool_lo = sem(f"l{n}_pool_lo")
        self.pv_done = sem(f"l{n}_pv_done")
        self.o_free = sem(f"l{n}_o_free")
        self.o_saved = sem(f"l{n}_o_saved")
        self.spare_ready = sem(f"l{n}_spare_ready")
        self.spare_free = sem(f"l{n}_spare_free")
        self.chain = sem(f"l{n}_chain")
        self.normed = sem(f"l{n}_normed")
        if self.causal:
            self.clip_done = sem(f"l{n}_clip_done")
        else:
            self.aug_loaded = [[sem(f"l{n}_aug_loaded{p}{h}") for h in range(CPB)] for p in range(2)]
            self.smax_ready = sem(f"l{n}_smax_ready")
            self.smax_free = sem(f"l{n}_smax_free")
            self.negmax_ready = sem(f"l{n}_negmax_ready")

    def job_norm_prev(self, i):
        return self.jobs * i - (1 if self.causal else 0)

    def job_turn_here(self, i):
        return self.jobs * i + 1

    def job_norm_0(self, i):
        return self.jobs * i + (0 if self.causal else 2)

    def job_turn_next(self, i):
        return self.jobs * i + 3

    def max_jobs_at(self, s, nxt):
        if self.causal:
            return []
        first = 2 * (s - self.max_step)
        if first < 0:
            return [(0, first + k + 2 * self.S) for k in range(2)]
        return [(1, first + k) for k in range(2)] if nxt else []

    def count(self, on, who, i, s):
        return i * on.count(who) + on[:s + 1].count(who)

    def around(self, i, s, prev, nxt):
        if s < 0:
            return (i - 1, s + self.S) if prev else None
        if s >= self.S:
            return (i + 1, s - self.S) if nxt else None
        return i, s


class Chain:

    def __init__(self, eng, sem):
        self.eng, self.sem, self.base, self.n = eng, sem, 0, 0

    def at(self, base):
        self.base, self.n = base, 0

    def link(self, ins, apart=None):
        self.n += 1
        ins.then_inc(self.sem, 1)
        self.eng.wait_ge(self.sem, self.base + self.n)
        if apart is not None:
            self.eng.sem_inc(apart, 1)


def build_program(nc, d, out):
    with ExitStack() as ctx:
        def sb(name, shape, dt=F32):
            return ctx.enter_context(nc.sbuf_tensor(name, shape, dt))

        def sem(name):
            return ctx.enter_context(nc.semaphore(name))

        bank = [ctx.enter_context(nc.psum_tensor(f"bank{i}", [P, CH], F32)) for i in range(4)]
        score = [ctx.enter_context(nc.psum_tensor(f"score{i}", [P, 2, CH], F32)) for i in range(NS)]
        hbank = [score[0][:, 0, :], score[0][:, 1, :], score[1][:, 0, :], score[1][:, 1, :]]

        ident = sb("ident", [P, P])
        tri = sb("tri", [P, P])
        expert_row = sb("expert_row", [2 * E0, E0, P], F32R)
        iota8 = sb("iota8", [P, E0])
        w_qkv0 = sb("w_qkv0", [P, 3, P])
        w_qkv1 = sb("w_qkv1", [P, 5, P])
        w_o = [sb(f"w_o{n}", [P, D]) for n in range(2)]
        b_o1 = sb("b_o1", [P, D])
        wg = sb("wg", [P, E0])
        w3 = sb("w3", [P, NH, P])
        rw1 = sb("rw1", [P, F0])
        rb1 = sb("rb1", [P, 2])
        rw2 = sb("rw2", [P, 2, E1])
        rb2 = sb("rb2", [P, E1])
        be1 = sb("be1", [P, NH])
        be2 = sb("be2", [2 * E0, D])

        x_tm = sb("x_tm", [P, NT, D])
        v_all = sb("v_all", [P, NT, D])
        o_tm = sb("o_tm", [P, NT, D])
        st6 = sb("st6", [P, 2, TPC, 6])
        mv = sb("mv", [P, 2, TPC, 2])
        rstd = sb("rstd", [P, 2, TPC])
        mhalf = sb("mhalf", [P, TPC])
        sc8 = sb("sc8", [P, TPC, 8])
        mx8 = sb("mx8", [P, TPC, 8])
        ix8 = sb("ix8", [P, TPC, 8], U32)
        ixf = sb("ixf", [P, TPC, 8])
        lead = sb("lead", [P, TPC])
        e_sm = sb("e_sm", [P, TPC, E1])
        p12 = sb("p12", [P, 2, TPC])
        gts = sb("gts", [P, 2, TPC, 8])
        g_halves = sb("g_halves", [P, TPC, 2 * E0])
        v_st_shape = [P, KT, HG * VW]
        with ExitStack() as overlay:
            def osb(name, shape, dt=F32):
                return overlay.enter_context(nc.sbuf_tensor(name, shape, dt))

            k_st = [osb(f"k_st{p}", [P, HG, T], F32R) for p in range(2)]
            q_st = [osb(f"q_st{p}", [P, T], F32R) for p in range(2)]
            v_st = osb("v_st", v_st_shape, F32R)
            probs = [osb(f"probs{p}", [P, 2, CH]) for p in range(NP)]
            p_hi = [osb(f"p_hi{p}", [P, 2, CH], F32R) for p in range(NP)]
            p_lo = [osb(f"p_lo{p}", [P, 2, CH], F32R) for p in range(NP)]
            o_sb = osb("o_sb", [P, CH])
            o_lo = osb("o_lo", [P, TPC, HG, DK])
            o_sum = osb("o_sum", [P, TPC, HG, DK])
            o_rcp = osb("o_rcp", [P, TPC, HG])
            negmax_h = osb("negmax_h", [P, KT, HG, 2])
            negmax = osb("negmax", [P, KT, HG])
            negmax2 = osb("negmax2", [P, KT, 2 * HG])
            negmax_t = osb("negmax_t", [2 * HG, T], F32R)
            ones_t = osb("ones_t", [HG, T])
            zeros_t = osb("zeros_t", [HG, T])
        with ExitStack() as overlay:
            xs = [osb(f"xs{i}", [P, TPC, D]) for i in range(2)]
            x_out = osb("x_out", [P, TPC, D])
            xt = [osb(f"xt{i}", [P, CH]) for i in range(2)]
            xt2 = xt[1]
            x_hi = [osb(f"x_hi{i}", [P, CH], F32R) for i in range(2)]
            x_lo = [osb(f"x_lo{i}", [P, CH], F32R) for i in range(2)]
            os_ = osb("os_", [P, TPC, D])
            ot = osb("ot", [P, CH])
            gate_bc = [osb(f"gate_bc{i}", [P, CH]) for i in range(2)]
            act_s = [osb(f"act_s{i}", [P, CH]) for i in range(2)]
            lin_u = [osb(f"lin_u{i}", [P, CH]) for i in range(2)]
            hid = [osb(f"hid{i}", [P, CH]) for i in range(2)]
            y_sb = osb("y_sb", [P, CH])
            res = [osb(f"res{i}", [P, TPC, D]) for i in range(2)]
            qk_hi = [osb(f"qk_hi{i}", [P, CH]) for i in range(4)]
            qk_lo = [osb(f"qk_lo{i}", [P, CH]) for i in range(4)]
            expert_raw = osb("expert_raw", [2 * E0, E0, P])
            gate_t = osb("gate_t", [2 * E0, CH], F32R)
            w_raw = [osb(f"w_raw{k}", [P, NH * P]) for k in range(2)]
            w_hi = [osb(f"w_hi{k}", [P, NH * P], F32R) for k in range(2)]
            w_lo = [osb(f"w_lo{k}", [P, NH * P], F32R) for k in range(2)]
            with ExitStack() as layer_only:
                rope_a = layer_only.enter_context(nc.sbuf_tensor("rope_a", [P, T], F32))
                rope_b = layer_only.enter_context(nc.sbuf_tensor("rope_b", [P, T], F32))
                rot = [layer_only.enter_context(nc.sbuf_tensor(f"rot{i}", [P, CH], F32)) for i in range(4)]
            with ExitStack() as layer_only:
                rh = layer_only.enter_context(nc.sbuf_tensor("rh", [P, 2, CH], F32))
                we2 = layer_only.enter_context(nc.sbuf_tensor("we2", [P, NH, P], F32))

        q_scr = [nc.dram_tensor(f"q_scr{n}", [B, 2 + n, P, T], F32, kind="Internal").ap() for n in range(2)]
        k_scr = [nc.dram_tensor(f"k_scr{n}", [B, 2 + n, P, T], F32, kind="Internal").ap() for n in range(2)]

        const_loaded = sem("const_loaded")
        w_loaded = sem("w_loaded")
        raw_loaded = [sem(f"raw_loaded{k}") for k in range(2)]
        we2_loaded = sem("we2_loaded")
        rope_loaded = sem("rope_loaded")
        rows_ready = sem("rows_ready")
        w_upper = sem("w_upper")
        w_lower = sem("w_lower")
        fills = sem("fills")
        apart = sem("apart")
        v_upper = sem("v_upper")
        FILLS = 1
        apart_pool = sem("apart_pool")
        first_loaded = sem("first_loaded")
        ones_loaded = sem("ones_loaded")
        layers = [Layer(n, sem) for n in range(2)]

        class Stage:

            def __init__(self, n):
                self.x_turned = sem(f"st{n}_x_turned")
                self.xt_ready = sem(f"st{n}_xt_ready")
                self.qkv_ready = sem(f"st{n}_qkv_ready")
                self.halves_hi = sem(f"st{n}_halves_hi")
                self.halves_lo = sem(f"st{n}_halves_lo")
                self.v_saved = sem(f"st{n}_v_saved")
                self.stored = sem(f"st{n}_stored")
                self.done = sem(f"st{n}_done")
                if n == 0:
                    self.x_in = [sem(f"st0_x_in{p}") for p in range(2)]
                    self.pair_stored = [sem(f"st0_pair_stored{p}") for p in range(2)]
                    return
                self.norm = sem(f"st{n}_norm")
                self.o_in = sem(f"st{n}_o_in")
                self.o_turned = sem(f"st{n}_o_turned")
                self.ot_ready = sem(f"st{n}_ot_ready")
                self.o_proj = sem(f"st{n}_o_proj")
                self.router_in = sem(f"st{n}_router_in")
                self.gate_pre = sem(f"st{n}_gate_pre")
                self.gate_exp = sem(f"st{n}_gate_exp")
                self.gates = sem(f"st{n}_gates")
                self.gates_turned = sem(f"st{n}_gates_turned")
                self.gate_t = sem(f"st{n}_gate_t")
                self.gbc_ready = sem(f"st{n}_gbc_ready")
                self.gbc_saved = sem(f"st{n}_gbc_saved")
                self.h_ready = sem(f"st{n}_h_ready")
                self.x_upper = sem(f"st{n}_x_upper")
                self.x_lower = sem(f"st{n}_x_lower")
                self.router_h = sem(f"st{n}_router_h")
                self.s_done = sem(f"st{n}_s_done")
                self.hid_ready = sem(f"st{n}_hid_ready")
                self.y_done = sem(f"st{n}_y_done")
                self.y_saved = sem(f"st{n}_y_saved")
                self.y_turned = sem(f"st{n}_y_turned")
                self.stats = sem(f"st{n}_stats")
                self.rstd = sem(f"st{n}_rstd")
                self.stats2 = sem(f"st{n}_stats2")
                self.rstd2 = sem(f"st{n}_rstd2")
                self.norm2 = sem(f"st{n}_norm2")
                self.chain = sem(f"st{n}_chain")
                self.back_chain = sem(f"st{n}_back_chain")
                self.pool_chain = sem(f"st{n}_pool_chain")
                if n == 1:
                    self.u_done = sem("st1_u_done")
                    self.x_kept = sem("st1_x_kept")
                    self.rot_done = sem("st1_rot_done")
                    self.rot_sum = sem("st1_rot_sum")
                    self.qk_ready = sem("st1_qk_ready")
                    self.v_ready = sem("st1_v_ready")
                    self.xt2_turned = sem("st1_xt2_turned")
                    self.xt2_ready = sem("st1_xt2_ready")
                else:
                    self.rh_ready = sem("st2_rh_ready")

        stages = [Stage(n) for n in range(3)]

        block = ctx.enter_context(nc.Block())

        FIRST = [(ident, "ident"), (w_qkv0, "w_qkv0")]
        CONSTS = [(tri, "tri"), (iota8, "iota8"), (w_o[0], "w_o0"), (w_o[1], "w_o1"), (expert_raw, "expert_row")]
        WEIGHTS = [(w_qkv1, "w_qkv1"), (wg, "wg"), (w3, "w3"), (rw1, "rw1"), (rb1, "rb1"), (rw2, "rw2"),
                   (be1, "be1"), (be2, "be2")]
        ALL_CONSTS = 16 * len(CONSTS)
        ALL_W = 16 * (len(WEIGHTS) + 3)
        x_tiles = d["x"].rearrange("(t p) c -> p t c", p=P)
        out_tiles = out.rearrange("(t p) c -> p t c", p=P)

        def bg(i):
            return i // G, i % G

        def o_bank(L, qc):
            return bank[qc] if L.causal else bank[3 * qc]

        def spare_bank(L, qc):
            return bank[3] if L.causal else bank[3 - 3 * qc]

        def pe_max_job(pe, L, i, p, m):
            qt, j, half = m // (HG * 2), m // 2 % HG, m % 2
            pe.wait_ge(L.smax_free, i * L.max_jobs + m + 1)
            nc.tensor.matmul(bank[1 + m % 2][:, :], q_st[p][:, qt * P:(qt + 1) * P],
                             k_st[p][:, j, half * CH:(half + 1) * CH],
                             start=True, stop=True).then_inc(L.smax_ready, 1)

        def pe_turn(pe, L, i, half, job):
            pe.wait_ge(L.negmax_ready, CPB * i + half + 1)
            pe.wait_ge(L.spare_free, job + 1)
            for t in range(TPC):
                last = nc.tensor.transpose(spare_bank(L, 1 - half)[0:2 * HG, t * P:(t + 1) * P],
                                           negmax2[:, half * TPC + t, :], ident[:, :])
            last.then_inc(L.spare_ready, 1)

        def pe_norm(pe, L, chunk, qc, job):
            pe.wait_ge(L.o_saved, chunk + 1)
            pe.wait_ge(L.spare_free, job + 1)
            for t in range(TPC):
                last = nc.tensor.transpose(spare_bank(L, 1 - qc)[:, t * P:(t + 1) * P],
                                           o_sb[:, t * P:(t + 1) * P], ident[:, :])
            last.then_inc(L.spare_ready, 1)

        def pe_scores(pe, L, i, p, s):
            qc, kt, hp, q0, w, _ = L.steps[s]
            pe.wait_ge(L.exp_done, i * L.S + s + 1)
            for a in range(2):
                j = 2 * hp + a
                last = nc.tensor.matmul(score[s % NS][:, a, 0:w], k_st[p][:, j, kt * P:(kt + 1) * P],
                                        q_st[p][:, q0:q0 + w], start=True, stop=True)
            last.then_inc(L.scores_ready, 1)

        def pe_loaded(pe, L, i, p, s):
            if L.causal and s == 0:
                pe.wait_ge(L.stacks_loaded[p], 16 * L.loads * (i // 2 + 1))
            if not L.causal and s in (0, L.S // CPB):
                pe.wait_ge(L.aug_loaded[p][s // (L.S // CPB)], 16 * 2 * (i // 2 + 1))

        def pe_values(pe, L, i, s):
            qc, kt, hp, q0, w, last_step = L.steps[s]
            if s in L.whole:
                wait_probs(pe, L, i, s)
            else:
                if L.hi_on[s] == "act":
                    pe.wait_ge(L.act_hi, L.count(L.hi_on, "act", i, s))
                lo = L.dve_lo if L.lo_on[s] == "dve" else L.pool_lo
                pe.wait_ge(lo, L.count(L.lo_on, L.lo_on[s], i, s))
            if hp == 0 and L.steps.index([x for x in L.steps if x[1] == kt][0]) == s:
                pe.wait_ge(L.v_staged, KT * i + kt + 1)
            if kt == 0 and hp == 0:
                pe.wait_ge(L.o_free, CPB * i + qc + 1)
                if not L.causal:
                    pe.wait_ge(L.spare_free, 1 + turn_job(L, i, qc) + 1)
            for a in range(2):
                j = 2 * hp + a
                v = v_st[:, kt, j * P:(j + 1) * P]
                parts = [(v.bitcast(F32), probs)] if s in L.whole else [(v, p_hi), (v, p_lo)]
                for k, (v, part) in enumerate(parts):
                    last = nc.tensor.matmul(o_bank(L, qc)[:, q0 - qc * CH:q0 - qc * CH + w],
                                            v, part[s % NP][:, a, 0:w],
                                            start=(kt == 0 and j == 0 and k == 0),
                                            stop=(last_step and a == 1 and part is parts[-1][1]))
            last.then_inc(L.pv_done, 1)

        def pe_round(pe, L, i, p, prev, nxt):
            for s in range(L.S):
                ahead = L.around(i, s + AHEAD, prev, nxt)
                if ahead:
                    ap = p if s + AHEAD < L.S else 1 - p
                    pe_loaded(pe, L, ahead[0], ap, ahead[1])
                    pe_scores(pe, L, ahead[0], ap, ahead[1])
                jobs = L.max_jobs_at(s, nxt)
                for k, m in jobs[:1]:
                    if m == 0:
                        pe.wait_ge(L.stacks_loaded[1 - p], 16 * L.loads * ((i + 1) // 2 + 1))
                    pe_max_job(pe, L, i + k, (1 - p) if k else p, m)
                pe_values(pe, L, i, s)
                for k, m in jobs[1:]:
                    pe_max_job(pe, L, i + k, (1 - p) if k else p, m)
                if prev and s == L.norm_prev:
                    pe_norm(pe, L, CPB * i - 1, 1, L.job_norm_prev(i))
                if s == L.turn_here:
                    pe_turn(pe, L, i, 1, L.job_turn_here(i))
                if s == L.norm_0:
                    pe_norm(pe, L, CPB * i, 0, L.job_norm_0(i))
                if nxt and s == L.turn_next:
                    pe_turn(pe, L, i + 1, 0, L.job_turn_next(i))

        def pe_attention(pe, L):
            pe.wait_ge(L.stacks_loaded[0], 16 * L.loads)
            if not L.causal:
                pe.wait_ge(ones_loaded, 16 * 2 * HG)
                for m in range(first_max_jobs(L)):
                    pe_max_job(pe, L, 0, 0, m)
                    if m == L.max_jobs // CPB + 1:
                        pe_turn(pe, L, 0, 0, 0)
            pe_loaded(pe, L, 0, 0, 0)
            for s in range(AHEAD):
                pe_scores(pe, L, 0, 0, s)
            pe_round(pe, L, 0, 0, False, True)
            with pe.Fori(0, NG // 2 - 1) as u:
                pe_round(pe, L, 2 * u + 1, 1, True, True)
                pe_round(pe, L, 2 * u + 2, 0, True, True)
            pe_round(pe, L, NG - 1, 1, True, False)
            pe_norm(pe, L, CPB * NG - 1, 1, L.jobs * NG - 1)

        def first_max_jobs(L):
            return 2 * (L.S - L.max_step)

        def act_exp(act, L, i, s):
            w = L.steps[s][4]
            act.wait_ge(L.scores_ready, i * L.S + s + 1)
            act.wait_ge(L.pv_done, i * L.S + s + 1)
            nc.scalar.activation(probs[s % NP][:, :, 0:w], score[s % NS][:, :, 0:w], ACT.Exp,
                                 scale=SCALE).then_inc(L.exp_done, 1)

        def wait_probs(eng, L, i, s):
            if L.causal:
                eng.wait_ge(L.clip_done, i * L.S + s + 1)
            else:
                eng.wait_ge(L.exp_done, NS + i * L.S + s + 1)

        def act_hi(act, L, i, s):
            if L.hi_on[s] != "act":
                return
            w = L.steps[s][4]
            wait_probs(act, L, i, s)
            nc.scalar.activation(p_hi[s % NP][:, :, 0:w], probs[s % NP][:, :, 0:w],
                                 ACT.Copy).then_inc(L.act_hi, 1)

        def turn_job(L, i, half):
            if half == 1:
                return L.job_turn_here(i)
            return 0 if isinstance(i, int) and i == 0 else L.job_turn_next(i - 1)

        def act_turn(act, L, i, p, half, job):
            if not isinstance(i, int) or i > 0:
                act.wait_ge(L.aug_loaded[1 - p][half], 32 * ((i - 1) // 2 + 1))
            act.wait_ge(L.spare_ready, job + 1)
            nc.scalar.activation(negmax_t[:, half * CH:(half + 1) * CH], spare_bank(L, 1 - half)[0:2 * HG, :],
                                 ACT.Copy).then_inc(L.spare_free, 1)

        def act_round(act, L, i, p, prev, nxt):
            for s in range(L.S):
                ahead = L.around(i, s + AHEAD, prev, nxt)
                if ahead:
                    act_exp(act, L, *ahead)
                ahead = L.around(i, s + AHEAD - (1 if L.causal else 0), prev, nxt)
                if ahead:
                    act_hi(act, L, *ahead)
                if s == L.turn_here:
                    act_turn(act, L, i, p, 1, L.job_turn_here(i))
                if nxt and s == L.turn_next:
                    act_turn(act, L, i + 1, 1 - p, 0, L.job_turn_next(i))

        def act_attention(act, L):
            if not L.causal:
                act_turn(act, L, 0, 0, 0, 0)
            for s in range(AHEAD):
                act_exp(act, L, 0, s)
                if not L.causal or s < AHEAD - 1:
                    act_hi(act, L, 0, s)
            act_round(act, L, 0, 0, False, True)
            with act.Fori(0, NG // 2 - 1) as u:
                act_round(act, L, 2 * u + 1, 1, True, True)
                act_round(act, L, 2 * u + 2, 0, True, True)
            act_round(act, L, NG - 1, 1, True, False)

        dve_chain = [None]

        def dve_clip(dve, L, i, s):
            qc, kt, hp, q0, w, _ = L.steps[s]
            dve.wait_ge(L.exp_done, NS + i * L.S + s + 1)
            e = probs[s % NP]
            ins = nc.vector.tensor_scalar(e[:, :, 0:w], e[:, :, 0:w], float(np.exp(-CLIP)),
                                          float(np.exp(CLIP)), ALU.max, ALU.min)
            if q0 == kt * P:
                dve_chain[0].link(ins)
                ins = nc.vector.tensor_tensor(e[:, :, 0:P], e[:, :, 0:P],
                                              tri[:, None, :].broadcast_to([P, 2, P]), ALU.mult)
            ins.then_inc(L.clip_done, 1)

        def dve_hi(dve, L, i, s):
            if L.hi_on[s] != "dve":
                return
            w = L.steps[s][4]
            wait_probs(dve, L, i, s)
            nc.vector.tensor_copy(p_hi[s % NP][:, :, 0:w], probs[s % NP][:, :, 0:w]).then_inc(L.dve_hi, 1)

        def lower_half(eng, engine, L, i, s, who, done):
            if L.lo_on[s] != who:
                return
            w = L.steps[s][4]
            hi_done = L.act_hi if L.hi_on[s] == "act" else L.dve_hi
            eng.wait_ge(hi_done, L.count(L.hi_on, L.hi_on[s], i, s))
            engine.tensor_tensor(p_lo[s % NP][:, :, 0:w], probs[s % NP][:, :, 0:w],
                                 p_hi[s % NP][:, :, 0:w].bitcast(F32), ALU.subtract).then_inc(done, 1)

        def dve_norm(dve, L, job, tile, qc, g):
            c = dve_chain[0]
            turned = spare_bank(L, 1 - qc)[:, :].rearrange("p (t j c) -> p t j c", t=TPC, j=HG)
            dve.wait_ge(L.spare_ready, job + 1)
            nc.vector.reciprocal(o_rcp[:, :, :], turned[:, :, :, DK])
            c.link(nc.vector.tensor_copy(o_lo[:, :, :, :], turned[:, :, :, LO:LO + DK]))
            c.link(nc.vector.tensor_tensor(o_sum[:, :, :, :], turned[:, :, :, 0:DK], o_lo[:, :, :, :], ALU.add))
            dve.sem_inc(L.spare_free, 1)
            dst = o_tm[:, bass.ds(tile, TPC), bass.ds(g * HG * DK, HG * DK)].rearrange("p t (j c) -> p t j c", c=DK)
            nc.vector.tensor_tensor(dst, o_sum[:, :, :, :],
                                    o_rcp[:, :, :, None].broadcast_to([P, TPC, HG, DK]),
                                    ALU.mult).then_inc(L.normed, 1)

        def dve_max_job(dve, L, i, m):
            qt, j, half = m // (HG * 2), m // 2 % HG, m % 2
            dve.wait_ge(L.smax_ready, i * L.max_jobs + m + 1)
            nc.vector.tensor_reduce(negmax_h[:, qt, j, half:half + 1], bank[1 + m % 2][:, :], AXX, ALU.max,
                                    negate=True).then_inc(L.smax_free, 1)

        def dve_negmax(dve, L, i, half):
            q = slice(half * TPC, (half + 1) * TPC)
            dve.wait_ge(L.smax_free, NS + i * L.max_jobs + (half + 1) * (L.max_jobs // CPB))
            c = dve_chain[0]
            c.link(nc.vector.tensor_tensor(negmax[:, q, :], negmax_h[:, q, :, 0], negmax_h[:, q, :, 1], ALU.min))
            c.link(nc.vector.tensor_copy(negmax2[:, q, 0:HG].bitcast(F32R), negmax[:, q, :]))
            nc.vector.tensor_tensor(negmax2[:, q, HG:2 * HG].bitcast(F32R), negmax[:, q, :],
                                    negmax2[:, q, 0:HG], ALU.subtract).then_inc(L.negmax_ready, 1)

        def dve_max_step(dve, L, i, jobs):
            for k, m in jobs:
                dve_max_job(dve, L, i + k, m)
                if (m + 1) % (L.max_jobs // CPB) == 0:
                    dve_negmax(dve, L, i + k, (m + 1) // (L.max_jobs // CPB) - 1)

        def clips(L, steps):
            return sum(L.causal and L.steps[s][3] == L.steps[s][1] * P for s in steps)

        def links(L, prev, nxt):
            n = 2 * (1 + prev) + (0 if L.causal else 2 * (1 + nxt))
            return n + clips(L, range(0 if nxt else AHEAD, L.S))

        def dve_round(dve, L, i, prev, nxt):
            b, g = bg(i)
            for s, (qc, kt, hp, q0, w, last_step) in enumerate(L.steps):
                if last_step:
                    dve.wait_ge(L.pv_done, NP + i * L.S + s + 1)
                    nc.vector.tensor_copy(o_sb[:, :], o_bank(L, qc)[:, :]).then_inc(L.o_saved, 1)
                    dve.wait_ge(L.o_saved, CPB * i + qc + 1)
                    dve.sem_inc(L.o_free, 1)
                ahead = L.around(i, s + AHEAD, prev, nxt)
                if ahead:
                    if L.causal:
                        dve_clip(dve, L, *ahead)
                    dve_hi(dve, L, *ahead)
                dve_max_step(dve, L, i, L.max_jobs_at(s, nxt)[:1])
                ahead = L.around(i, s + AHEAD - 1, prev, nxt)
                if ahead:
                    lower_half(dve, nc.vector, L, *ahead, "dve", L.dve_lo)
                dve_max_step(dve, L, i, L.max_jobs_at(s, nxt)[1:])
                if prev and s == L.norm_prev:
                    pb, pg = bg(i - 1)
                    dve_norm(dve, L, L.job_norm_prev(i), pb * KT + TPC, 1, pg)
                if s == L.norm_0:
                    dve_norm(dve, L, L.job_norm_0(i), b * KT, 0, g)

        def dve_attention(dve, L):
            c = dve_chain[0] = Chain(dve, L.chain)
            places = v_st[:, :, :].bitcast(F32)
            nc.vector.memset(places, 0.0).then_inc(fills, 1)
            dve.wait_ge(fills, FILLS + 2 * L.n + 1)
            nc.vector.memset(places.rearrange("p t (j c) -> p t j c", c=VW)[:, :, :, DK:DK + 1],
                             1.0).then_inc(fills, 1)
            if not L.causal:
                dve_max_step(dve, L, 0, [(0, m) for m in range(first_max_jobs(L))])
            for s in range(AHEAD):
                if L.causal:
                    dve_clip(dve, L, 0, s)
                dve_hi(dve, L, 0, s)
                if s < AHEAD - 1:
                    lower_half(dve, nc.vector, L, 0, s, "dve", L.dve_lo)
            dve_round(dve, L, 0, False, True)
            total = c.n
            per = links(L, True, True)
            with dve.Fori(0, NG // 2 - 1) as u:
                for k in range(2):
                    c.at(total + (2 * u + k) * per)
                    dve_round(dve, L, 2 * u + 1 + k, True, True)
                    assert c.n == per
            total += (NG - 2) * per
            c.at(total)
            dve_round(dve, L, NG - 1, True, False)
            dve_norm(dve, L, L.jobs * NG - 1, (B - 1) * KT + TPC, 1, G - 1)

        def pool_stage_v(pool, L, i, kt):
            b, g = bg(i)
            src = v_all[:, bass.ds(b * KT + kt, 1), bass.ds(g * HG * DK, HG * DK)].rearrange(
                "p t (j c) -> p (t j) c", c=DK)
            dst = v_st[:, kt, :].rearrange("p (j c) -> p j c", c=VW)
            nc.gpsimd.tensor_copy(dst[:, :, 0:DK], src).then_inc(v_upper, 1)
            pool.wait_ge(v_upper, L.n * NG * KT + KT * i + kt + 1)
            pool.sem_inc(apart_pool, 1)
            nc.gpsimd.tensor_tensor(dst[:, :, LO:LO + DK], src, dst[:, :, 0:DK].bitcast(F32),
                                    ALU.subtract).then_inc(L.v_staged, 1)

        def pool_round(pool, L, i, prev, nxt):
            for s in range(L.S):
                ahead = L.around(i, s + AHEAD - 1, prev, nxt)
                if ahead:
                    lower_half(pool, nc.gpsimd, L, *ahead, "pool", L.pool_lo)
                if nxt:
                    for kt in range(KT):
                        if L.v_used[kt] == s - 1 or (s == L.S - 1 and L.v_used[kt] == s):
                            pool.wait_ge(L.pv_done, NP + i * L.S + L.v_used[kt] + 1)
                            pool_stage_v(pool, L, i + 1, kt)

        def pool_attention(pool, L):
            if not L.causal:
                nc.gpsimd.memset(ones_t[:, :], 1.0)
                nc.gpsimd.memset(zeros_t[:, :], 0.0)
            for p in range(2):
                if not L.causal:
                    nc.gpsimd.memset(q_st[p][:, :].bitcast(F32), 0.0)
                nc.gpsimd.memset(k_st[p][:, :, :].bitcast(F32), 0.0).then_inc(L.zeroed, 1)
            pool.wait_ge(fills, FILLS + 2 * (L.n + 1))
            for kt in range(KT):
                pool_stage_v(pool, L, 0, kt)
            for s in range(AHEAD - 1):
                lower_half(pool, nc.gpsimd, L, 0, s, "pool", L.pool_lo)
            pool_round(pool, L, 0, False, True)
            with pool.Fori(0, NG // 2 - 1) as u:
                pool_round(pool, L, 2 * u + 1, True, True)
                pool_round(pool, L, 2 * u + 2, True, True)
            pool_round(pool, L, NG - 1, True, False)

        def sp_load_stacks(sp, L, i, p):
            b, g = bg(i)
            for j in range(HG):
                def halves(scr, first, n):
                    return scr[L.n][bass.ds(b, 1), first:first + n, bass.ds(g * HG * DK + j * DK, DK), :].rearrange(
                        "b t c n -> (b t) c n")
                r = SLOT * j
                if L.causal:
                    for t in range(2):
                        rt = slice(r + 2 * DK * t, r + 2 * DK * (t + 1))
                        sp.dma_start(k_st[p][rt, j, :].bitcast(F32), halves(k_scr, 0, 2)).then_inc(L.stacks_loaded[p], 16)
                        sp.dma_start(q_st[p][rt, :].bitcast(F32),
                                     halves(q_scr, t, 1).broadcast_to([2, DK, T])).then_inc(L.stacks_loaded[p], 16)
                else:
                    rt = slice(r, r + 3 * DK)
                    sp.dma_start(k_st[p][rt, j, :].bitcast(F32), halves(k_scr, 0, 3)).then_inc(L.stacks_loaded[p], 16)
                    sp.dma_start(q_st[p][rt, :].bitcast(F32), halves(q_scr, 0, 3)).then_inc(L.stacks_loaded[p], 16)
            if not L.causal:
                for k in range(2):
                    sp.dma_start(aug_rows(p, k), zeros_t[:, :]).then_inc(L.stacks_loaded[p], 16)

        def aug_rows(p, k):
            r = 3 * DK + k
            return q_st[p][r:r + SLOT * (HG - 1) + 1:SLOT, :].bitcast(F32)

        def sp_load_aug(sp, L, i, p, half):
            sp.wait_ge(L.spare_free, 1 + turn_job(L, i, half) + 1)
            q = slice(half * CH, (half + 1) * CH)
            for k in range(2):
                sp.dma_start(aug_rows(p, k)[:, q],
                             negmax_t[k * HG:(k + 1) * HG, q].bitcast(F32)).then_inc(L.aug_loaded[p][half], 16)

        def sp_attention(sp, L):
            for p in range(2):
                sp.wait_ge(L.zeroed, p + 1)
                if not L.causal:
                    for j in range(HG):
                        r = SLOT * j + 3 * DK
                        sp.dma_start(k_st[p][r:r + 2, j, :].bitcast(F32), ones_t[0:2, :]).then_inc(ones_loaded, 16)
                sp_load_stacks(sp, L, p, p)
            if L.causal:
                for t, name in WEIGHTS:
                    sp.dma_start(t[tuple(slice(None) for _ in t.shape)], d[name]).then_inc(w_loaded, 16)
                sp.dma_start(x_tm[:, :, :], x_tiles).then_inc(w_loaded, 16)
                sp.dma_start(b_o1[:, :], d["b_o1"].broadcast_to([P, D])).then_inc(w_loaded, 16)
                sp.dma_start(rb2[:, :], d["rb2"].broadcast_to([P, E1])).then_inc(w_loaded, 16)
            else:
                sp_load_aug(sp, L, 0, 0, 0)
                sp_load_aug(sp, L, 0, 0, 1)
                sp_load_aug(sp, L, 1, 1, 0)
            with sp.Fori(0, NG // 2 - 1) as u:
                for k in range(2):
                    i = 2 * u + 2 + k
                    sp.wait_ge(L.scores_ready, (i - 1) * L.S)
                    sp_load_stacks(sp, L, i, k)
                    if not L.causal:
                        sp_load_aug(sp, L, i - 1, 1 - k, 1)
                        sp_load_aug(sp, L, i, k, 0)
            if not L.causal:
                sp_load_aug(sp, L, NG - 1, 1, 1)

        def pe_turn_tiles(dst, src):
            for t in range(TPC):
                last = nc.tensor.transpose(dst[:, t * P:(t + 1) * P], src[:, t, :], ident[:, :])
            return last

        def pe_qkv(st, w, x, par):
            for a in range(2):
                nc.tensor.matmul(hbank[2 * par + a], w[:, a, :], x[:, :], start=True, stop=True)
            for t in range(TPC):
                last = nc.tensor.matmul(bank[par][:, t * P:(t + 1) * P], x[:, t * P:(t + 1) * P], w[:, 2, :],
                                        start=True, stop=True)
            last.then_inc(st.qkv_ready, 1)

        def sp_store_halves(sp, st, n, c, b, hh):
            sp.wait_ge(st.halves_lo, 2 * (c + 1))
            sp.wait_ge(st.halves_hi, 2 * (c + 1))
            for a, scr, order in ((0, q_scr, "hhl"), (1, k_scr, "hlh")):
                for t, what in enumerate(order):
                    src = qk_hi[a] if what == "h" else qk_lo[a]
                    dst = scr[n][bass.ds(b, 1), t, :, hh * CH:(hh + 1) * CH].rearrange("b c n -> (b c) n")
                    sp.dma_start(dst, src[:, :]).then_inc(st.stored, 16)
        STORES = 6 * 16

        def sp_store_pair(sp, st, c, b, hh):
            sp.wait_ge(st.halves_lo, 2 * (c + 1))
            sp.wait_ge(st.halves_hi, 2 * (c + 1))
            for a, scr in ((0, q_scr), (1, k_scr)):
                for t, half in enumerate((qk_hi, qk_lo)):
                    dst = scr[0][bass.ds(b, 1), t, :, hh * CH:(hh + 1) * CH].rearrange("b c n -> (b c) n")
                    sp.dma_start(dst, half[2 * hh + a][:, :]).then_inc(st.pair_stored[hh], 16)
        PAIR = 4 * 16

        class Beside:
            pass

        plan = [Beside(), Beside()]
        for pl, steps in ((plan[0], (1, 3, 4, 5, 6, 7, 8, 9, 10, 11, None, 12, 13, 14)),
                          (plan[1], (1, 2, None, None, None, None, 2, 4, 6, 8, 10, 11, 12, 14))):
            (pl.y_turn, pl.norm2, pl.x2_turn, pl.q, pl.k, pl.v,
             pl.o_turn, pl.o_proj, pl.norm, pl.x_turn, pl.hidden, pl.router, pl.weigh, pl.g_turn) = steps

        SPC = NH
        n_exp = [E0, E1]
        h_banks, h_lead = [2, 4], [1, 2]

        def wait_used(eng, signal, count):
            if not isinstance(count, int) or count > 0:
                eng.wait_ge(signal, count)

        def slice_of(n):
            return slice(n * P, (n + 1) * P)

        def pe_hidden(pe, st, c, par, n, layer):
            pe.wait_ge(st.s_done, c * SPC + n + 1)
            if n == 0:
                pe.wait_ge(st.x_lower, c + 1)
            if layer == 0:
                pe.wait_ge(st.u_done, c * SPC + n + 1)
            for k in range(2 if layer == 0 else 1):
                for a, (w, x) in enumerate(((w_hi[k], x_hi[par]), (w_lo[k], x_hi[par]), (w_hi[k], x_lo[par]))):
                    last = nc.tensor.matmul(hbank[2 * k + n % h_banks[layer]], w[:, slice_of(n)], x[:, :], start=(a == 0),
                                            stop=(a == 2))
            last.then_inc(st.h_ready, 1)

        def pe_gate_rows(pe, st, c, e, layer):
            if e == 0:
                pe.wait_ge(st.gate_t, c + 1)
            pe.wait_ge(st.gbc_saved, c * n_exp[layer] + e + 1)
            nc.tensor.matmul(bank[1][:, :], expert_row[:, e, :], gate_t[:, :], start=True,
                             stop=True).then_inc(st.gbc_ready, 1)

        def pe_beside(pe, st, n, back, front, par, layer):
            pl = plan[layer]
            if back is not None:
                if n == pl.y_turn:
                    pe.wait_ge(st.y_saved, back + 2)
                    for t in range(TPC):
                        last = nc.tensor.transpose(bank[3][:, slice_of(t)], y_sb[:, slice_of(t)], ident[:, :])
                    last.then_inc(st.y_turned, 1)
                if n == pl.x2_turn:
                    pe.wait_ge(st.norm2, back + 1)
                    pe_turn_tiles(bank[2], x_out).then_inc(st.xt2_turned, 1)
                for k, at in enumerate((pl.q, pl.k)):
                    if n == at:
                        pe.wait_ge(st.xt2_ready, back + 1)
                        if k == 1:
                            pe.wait_ge(st.rot_done, 2 * back + 1)
                        for a in range(2):
                            last = nc.tensor.matmul(bank[2 + a][:, :], w_qkv1[:, 2 * k + a, :], xt2[:, :],
                                                    start=True, stop=True)
                        last.then_inc(st.qk_ready, 1)
                if n == pl.v:
                    pe.wait_ge(st.rot_done, 2 * back + 2)
                    for t in range(TPC):
                        last = nc.tensor.matmul(bank[2][:, slice_of(t)], xt2[:, slice_of(t)], w_qkv1[:, 4, :],
                                                start=True, stop=True)
                    last.then_inc(st.v_ready, 1)
            if front is not None:
                if n == pl.o_turn:
                    pe.wait_ge(st.o_in, front + 1)
                    pe_turn_tiles(bank[3], os_).then_inc(st.o_turned, 1)
                if n == pl.o_proj:
                    pe.wait_ge(st.ot_ready, front + 1)
                    if layer == 0 and back is not None:
                        pe.wait_ge(st.v_saved, back + 1)
                    for t in range(TPC):
                        last = nc.tensor.matmul(bank[2][:, slice_of(t)], ot[:, slice_of(t)], w_o[layer][:, :],
                                                start=True, stop=True)
                    last.then_inc(st.o_proj, 1)
                if n == pl.x_turn:
                    pe.wait_ge(st.norm, front + 1)
                    pe_turn_tiles(bank[3], xs[par]).then_inc(st.x_turned, 1)
                if n == pl.hidden:
                    pe.wait_ge(st.xt_ready, front + 1)
                    pe.wait_ge(st.x_upper, front + 1)
                    for f in range(2):
                        last = nc.tensor.matmul(bank[2 + f][:, :], rw1[:, slice_of(f)], xt[0][:, :], start=True,
                                                stop=True)
                    last.then_inc(st.router_h, 1)
                if n == pl.router:
                    if layer == 0:
                        pe.wait_ge(st.xt_ready, front + 1)
                        for t in range(TPC):
                            last = nc.tensor.matmul(bank[2][:, t * 8:t * 8 + 8], xt[0][:, slice_of(t)], wg[:, :],
                                                    start=True, stop=True)
                    else:
                        pe.wait_ge(st.rh_ready, front + 1)
                        for t in range(TPC):
                            for f in range(2):
                                last = nc.tensor.matmul(bank[2][:, t * E1:(t + 1) * E1], rh[:, f, slice_of(t)],
                                                        rw2[:, f, :], start=(f == 0), stop=(f == 1))
                    last.then_inc(st.router_in, 1)
                if n == pl.g_turn:
                    pe.wait_ge(st.gates, front + 1)
                    for t in range(TPC):
                        last = nc.tensor.transpose(bank[3][0:2 * E0, slice_of(t)], g_halves[:, t, :], ident[:, :])
                    last.then_inc(st.gates_turned, 1)
                if n == SPC - 1:
                    pe_gate_rows(pe, st, front, 0, layer)

        def pe_chunk(pe, st, c, par, back, front, layer):
            per = SPC // n_exp[layer]
            w = w3 if layer == 0 else we2
            for n in range(SPC):
                pe_beside(pe, st, n, back, front, 1 - par, layer)
                e = n // per + 1
                if n % per == per - 2 and e < n_exp[layer]:
                    pe_gate_rows(pe, st, c, e, layer)
                lead = n + h_lead[layer]
                if lead < SPC:
                    pe_hidden(pe, st, c, par, lead, layer)
                elif front is not None:
                    pe_hidden(pe, st, front, 1 - par, lead - SPC, layer)
                if n == 0:
                    pe.wait_ge(st.y_saved, c + 1)
                    if layer == 1:
                        nc.tensor.matmul(bank[0][:, :], be2[:, :], gate_t[:, :].bitcast(F32), start=True, stop=False)
                pe.wait_ge(st.hid_ready, c * SPC + n + 1)
                nc.tensor.matmul(bank[0][:, :], w[:, n, :], hid[n % 2][:, :], start=(layer == 0 and n == 0),
                                 stop=(n == SPC - 1)).then_inc(st.y_done, 1)

        def pe_end(pe, st, layer):
            pe.wait_ge(rows_ready, 1)
            for n in range(SPC):
                pe_beside(pe, st, n, None, 0, 0, layer)
            pe.wait_ge(w_lower, 2 if layer == 0 else 3)
            if layer == 1:
                pe.wait_ge(we2_loaded, 16)
            for n in range(h_lead[layer]):
                pe_hidden(pe, st, 0, 0, n, layer)
            pe_chunk(pe, st, 0, 0, None, 1, layer)
            with pe.Fori(0, B - 1) as u:
                pe_chunk(pe, st, 2 * u + 1, 1, 2 * u, 2 * u + 2, layer)
                pe_chunk(pe, st, 2 * u + 2, 0, 2 * u + 1, 2 * u + 3, layer)
            pe_chunk(pe, st, 2 * B - 1, 1, 2 * B - 2, None, layer)
            for n in range(SPC):
                pe_beside(pe, st, n, 2 * B - 1, None, 0, layer)

        def act_beside(act, st, n, back, front, par, layer):
            pl = plan[layer]
            if back is not None:
                if n == pl.x2_turn:
                    act.wait_ge(st.xt2_turned, back + 1)
                    nc.scalar.activation(xt2[:, :], bank[2][:, :], ACT.Copy).then_inc(st.xt2_ready, 1)
                if layer == 0 and n in (pl.k, pl.v):
                    a = 0 if n == pl.k else 1
                    act.wait_ge(st.rot_sum, 2 * back + a + 1)
                    act.wait_ge(st.done, back + 1)
                    nc.scalar.activation(qk_hi[a][:, :].bitcast(F32R), rot[2 * a][:, :],
                                         ACT.Copy).then_inc(st.halves_hi, 1)
            if front is not None:
                if n == pl.o_turn:
                    act.wait_ge(st.o_turned, front + 1)
                    nc.scalar.activation(ot[:, :], bank[3][:, :], ACT.Copy).then_inc(st.ot_ready, 1)
                if n == pl.x_turn:
                    act.wait_ge(st.x_turned, front + 1)
                    nc.scalar.activation(xt[0][:, :], bank[3][:, :], ACT.Copy).then_inc(st.xt_ready, 1)
                    nc.scalar.activation(x_hi[par][:, :], bank[3][:, :], ACT.Copy).then_inc(st.x_upper, 1)
                if n == pl.hidden:
                    act.wait_ge(st.router_h, front + 1)
                    for f in range(2):
                        last = nc.scalar.activation(rh[:, f, :], bank[2 + f][:, :], ACT.Gelu, bias=rb1[:, f:f + 1])
                    last.then_inc(st.rh_ready, 1)
                if n == pl.router + 1:
                    act.wait_ge(st.gate_pre, front + 1)
                    if layer == 0:
                        nc.scalar.activation(p12[:, 1, :], lead[:, :], ACT.Exp).then_inc(st.gate_exp, 1)
                    else:
                        nc.scalar.activation(e_sm[:, :, :], sc8[:, :, 0:E1], ACT.Exp).then_inc(st.gate_exp, 1)
                if n == pl.g_turn:
                    act.wait_ge(st.gates_turned, front + 1)
                    nc.scalar.activation(gate_t[:, :], bank[3][0:2 * E0, :], ACT.Copy).then_inc(st.gate_t, 1)
                if n == SPC - 1:
                    act_gate_rows(act, st, front, 0, layer)

        def act_gate_rows(act, st, c, e, layer):
            act.wait_ge(st.gbc_ready, c * n_exp[layer] + e + 1)
            wait_used(act, st.hid_ready, c * SPC + (e - 1) * (SPC // n_exp[layer]))
            nc.scalar.activation(gate_bc[e % 2][:, :], bank[1][:, :], ACT.Copy).then_inc(st.gbc_saved, 1)

        def act_chunk(act, st, c, par, back, front, layer):
            per = SPC // n_exp[layer]
            for n in range(SPC):
                act.wait_ge(st.h_ready, c * SPC + n + 1)
                wait_used(act, st.hid_ready, c * SPC + n - 1)
                if layer == 0:
                    nc.scalar.activation(act_s[n % 2][:, :], hbank[n % 2], ACT.Silu).then_inc(st.s_done, 1)
                else:
                    nc.scalar.activation(act_s[n % 2][:, :], hbank[n % h_banks[1]], ACT.Gelu,
                                         bias=be1[:, n:n + 1]).then_inc(st.s_done, 1)
                act_beside(act, st, n, back, front, 1 - par, layer)
                e = n // per + 1
                if n % per == per - 2 and e < n_exp[layer]:
                    act_gate_rows(act, st, c, e, layer)
            act.wait_ge(st.y_done, (c + 1) * SPC)
            nc.scalar.activation(y_sb[:, :], bank[0][:, :], ACT.Copy).then_inc(st.y_saved, 1)

        def act_end(act, st, layer):
            for n in range(SPC):
                act_beside(act, st, n, None, 0, 0, layer)
                if n == plan[layer].o_turn:
                    for k in range(2 if layer == 0 else 1):
                        act.wait_ge(raw_loaded[k], 16 * (layer + 1) if k == 0 else 16)
                        nc.scalar.activation(w_hi[k][:, :], w_raw[k][:, :], ACT.Copy).then_inc(w_upper, 1)
            act_chunk(act, st, 0, 0, None, 1, layer)
            with act.Fori(0, B - 1) as u:
                act_chunk(act, st, 2 * u + 1, 1, 2 * u, 2 * u + 2, layer)
                act_chunk(act, st, 2 * u + 2, 0, 2 * u + 1, 2 * u + 3, layer)
            act_chunk(act, st, 2 * B - 1, 1, 2 * B - 2, None, layer)
            for n in range(SPC):
                act_beside(act, st, n, 2 * B - 1, None, 0, layer)

        def dve_stats(c_, x, k, signal):
            for t in range(TPC):
                ins = nc.vector.bn_stats(st6[:, k, t, :], x[:, t, :])
            c_.link(ins, apart)
            for t in range(TPC):
                ins = nc.vector.bn_aggr(mv[:, k, t, :], st6[:, k, t, :])
            ins.then_inc(signal, 1)

        def dve_normalise(x, o, k):
            for t in range(TPC):
                ins = nc.vector.tensor_scalar(o[:, t, :], x[:, t, :], mv[:, k, t, 0:1], rstd[:, k, t:t + 1],
                                              ALU.subtract, ALU.mult)
            return ins

        def dve_top2(dve, ch, st, c, layer):
            dve.wait_ge(st.router_in, c + 1)
            if layer == 0:
                ch.link(nc.vector.tensor_copy(sc8[:, :, :], bank[2][:, 0:TPC * 8].rearrange("p (t e) -> p t e", e=8)),
                        apart)
                dve_best(ch)
                nc.vector.tensor_tensor(lead[:, :], mx8[:, :, 1], mx8[:, :, 0], ALU.subtract).then_inc(st.gate_pre, 1)
            else:
                lg = bank[2][:, 0:TPC * E1].rearrange("p (t e) -> p t e", e=E1)
                ch.link(nc.vector.tensor_tensor(sc8[:, :, 0:E1], lg, rb2[:, None, :].broadcast_to([P, TPC, E1]), ALU.add))
                ch.link(nc.vector.tensor_reduce(lead[:, :], sc8[:, :, 0:E1], AXX, ALU.max))
                nc.vector.tensor_tensor(sc8[:, :, 0:E1], sc8[:, :, 0:E1],
                                        lead[:, :, None].broadcast_to([P, TPC, E1]),
                                        ALU.subtract).then_inc(st.gate_pre, 1)

        def dve_best(ch):
            for t in range(TPC):
                ins = nc.vector.max(mx8[:, t, :], sc8[:, t, :])
            ch.link(ins, apart)
            for t in range(TPC):
                ins = nc.vector.max_index(ix8[:, t, :], mx8[:, t, :], sc8[:, t, :])
            ch.link(ins)
            ch.link(nc.vector.tensor_copy(ixf[:, :, :], ix8[:, :, :]))

        def dve_weights(dve, ch, st, c, layer):
            dve.wait_ge(st.gate_exp, c + 1)
            if layer == 0:
                ch.link(nc.vector.tensor_scalar(p12[:, 0, :], p12[:, 1, :], 1.0, None, ALU.add))
                ch.link(nc.vector.reciprocal(p12[:, 0, :], p12[:, 0, :]))
                ch.link(nc.vector.tensor_tensor(p12[:, 1, :], p12[:, 1, :], p12[:, 0, :], ALU.mult))
            else:
                ch.link(nc.vector.tensor_reduce(lead[:, :], e_sm[:, :, :], AXX, ALU.add))
                ch.link(nc.vector.reciprocal(lead[:, :], lead[:, :]))
                ch.link(nc.vector.tensor_tensor(sc8[:, :, 0:E1], e_sm[:, :, :],
                                                lead[:, :, None].broadcast_to([P, TPC, E1]), ALU.mult), apart)
                dve_best(ch)
                ch.link(nc.vector.tensor_copy(p12[:, :, :], mx8[:, :, 0:2].rearrange("p t k -> p k t")))

        def dve_spread(ch, st):
            ch.link(nc.vector.tensor_tensor(
                gts[:, :, :, :], iota8[:, None, None, :].broadcast_to([P, 2, TPC, E0]),
                ixf[:, :, 0:2].rearrange("p t k -> p k t")[:, :, :, None].broadcast_to([P, 2, TPC, E0]),
                ALU.is_equal))
            ch.link(nc.vector.tensor_tensor(gts[:, :, :, :], gts[:, :, :, :],
                                            p12[:, :, :, None].broadcast_to([P, 2, TPC, E0]), ALU.mult))
            ch.link(nc.vector.tensor_tensor(gts[:, 0, :, :], gts[:, 0, :, :], gts[:, 1, :, :], ALU.add))
            ch.link(nc.vector.tensor_copy(g_halves[:, :, 0:E0].bitcast(F32R), gts[:, 0, :, :]))
            nc.vector.tensor_tensor(g_halves[:, :, E0:2 * E0].bitcast(F32R), gts[:, 0, :, :], g_halves[:, :, 0:E0],
                                    ALU.subtract).then_inc(st.gates, 1)

        def dve_beside(dve, st, n, back, front, par, layer):
            pl = plan[layer]
            fc, bc = dve_front[0], dve_back[0]
            if back is not None:
                if n == pl.y_turn:
                    bc.at(back * BACK_LINKS)
                    dve.wait_ge(st.y_turned, back + 1)
                    bc.link(nc.vector.tensor_tensor(res[1][:, :, :], xs[par][:, :, :],
                                                    bank[3][:, :].rearrange("p (t c) -> p t c", c=D), ALU.add))
                    dve_stats(bc, res[1], 1, st.stats2)
                    assert bc.n == BACK_LINKS
                if n == pl.norm2:
                    dve.wait_ge(st.rstd2, back + 1)
                    if layer == 1:
                        dve.wait_ge(st.done, back + 1)
                    dve.sem_inc(apart, 1)
                    dve_normalise(res[1], x_out, 1).then_inc(st.norm2, 1)
                    if layer == 0:
                        dve.wait_ge(st.norm2, back + 1)
                        dve.sem_inc(apart, 1)
                        nc.vector.tensor_copy(x_tm[:, bass.ds(back * TPC, TPC), :],
                                              x_out[:, :, :]).then_inc(st.x_kept, 1)
                for a, at in enumerate((pl.q, pl.k)):
                    if n == at:
                        dve.wait_ge(st.qk_ready, 2 * back + a + 1)
                        half = slice(par * CH, (par + 1) * CH)
                        nc.vector.tensor_tensor(rot[2 * a][:, :], bank[2][:, :], rope_a[:, half], ALU.mult)
                        nc.vector.tensor_tensor(rot[2 * a + 1][:, :], bank[3][:, :], rope_b[:, half],
                                                ALU.mult).then_inc(st.rot_done, 1)
                if n == pl.v:
                    dve.wait_ge(st.v_ready, back + 1)
                    dve.sem_inc(apart, 1)
                    nc.vector.tensor_copy(v_all[:, bass.ds(back * TPC, TPC), :],
                                          bank[2][:, :].rearrange("p (t c) -> p t c", c=D)).then_inc(st.v_saved, 1)
                    for a in range(2):
                        dve.wait_ge(st.halves_hi, 2 * back + a + 1)
                        nc.vector.tensor_tensor(qk_lo[a][:, :].bitcast(F32R), rot[2 * a][:, :], qk_hi[a][:, :],
                                                ALU.subtract).then_inc(st.halves_lo, 1)
            if front is not None:
                if n == pl.o_turn - 1:
                    nc.vector.tensor_copy(os_[:, :, :], o_tm[:, bass.ds(front * TPC, TPC), :]).then_inc(st.o_in, 1)
                if n == pl.o_proj:
                    fc.at(front * FRONT_LINKS[layer] + layer)
                    dve.wait_ge(st.o_proj, front + 1)
                    dve.sem_inc(apart, 1)
                    fc.link(nc.vector.tensor_tensor(res[0][:, :, :], x_tm[:, bass.ds(front * TPC, TPC), :],
                                                    bank[2][:, :].rearrange("p (t c) -> p t c", c=D), ALU.add))
                    if layer == 1:
                        fc.link(nc.vector.tensor_tensor(res[0][:, :, :], res[0][:, :, :],
                                                        b_o1[:, None, :].broadcast_to([P, TPC, D]), ALU.add))
                    dve_stats(fc, res[0], 0, st.stats)
                if n == pl.norm:
                    dve.wait_ge(st.rstd, front + 1)
                    dve_normalise(res[0], xs[par], 0).then_inc(st.norm, 1)
                if n == pl.x_turn:
                    dve.wait_ge(st.x_upper, front + 1)
                    nc.vector.tensor_tensor(x_lo[par][:, :], xt[0][:, :], x_hi[par][:, :].bitcast(F32),
                                            ALU.subtract).then_inc(st.x_lower, 1)
                if n == pl.router:
                    dve_top2(dve, fc, st, front, layer)
                if n == pl.weigh:
                    dve_weights(dve, fc, st, front, layer)
                if n == pl.weigh + layer:
                    dve_spread(fc, st)
                    assert fc.n == FRONT_LINKS[layer], fc.n

        BACK_LINKS = 2
        FRONT_LINKS = [13, 16]
        dve_front, dve_back = [None], [None]

        def dve_chunk(dve, st, c, par, back, front, layer):
            per = SPC // n_exp[layer]
            for n in range(SPC):
                e = n // per
                if n % per == 0:
                    dve.wait_ge(st.gbc_saved, 1 + c * n_exp[layer] + e + 1)
                wait_used(dve, st.y_done, c * SPC + n - 1)
                if layer == 0:
                    dve.wait_ge(st.h_ready, c * SPC + n + 1)
                    nc.vector.tensor_tensor(lin_u[n % 2][:, :], hbank[2 + n % 2], gate_bc[e % 2][:, :],
                                            ALU.mult).then_inc(st.u_done, 1)
                    dve.wait_ge(st.u_done, NS + c * SPC + n + 1)
                    dve.wait_ge(st.s_done, h_banks[layer] + c * SPC + n + 1)
                    nc.vector.tensor_tensor(hid[n % 2][:, :], act_s[n % 2][:, :], lin_u[n % 2][:, :],
                                            ALU.mult).then_inc(st.hid_ready, 1)
                else:
                    dve.wait_ge(st.s_done, h_banks[layer] + c * SPC + n + 1)
                    nc.vector.tensor_tensor(hid[n % 2][:, :], act_s[n % 2][:, :], gate_bc[e % 2][:, :],
                                            ALU.mult).then_inc(st.hid_ready, 1)
                dve_beside(dve, st, n, back, front, 1 - par, layer)

        def dve_end(dve, st, layer):
            dve_front[0], dve_back[0] = Chain(dve, st.chain), Chain(dve, st.back_chain)
            if layer == 1:
                dve_front[0].link(nc.vector.memset(sc8[:, :, E1:8], -1.0))
            for n in range(SPC):
                dve_beside(dve, st, n, None, 0, 0, layer)
                if n == plan[layer].norm:
                    for k in range(2 if layer == 0 else 1):
                        dve.wait_ge(w_upper, 2 * layer + k + 1)
                        nc.vector.tensor_tensor(w_lo[k][:, :], w_raw[k][:, :], w_hi[k][:, :].bitcast(F32),
                                                ALU.subtract).then_inc(w_lower, 1)
            if layer == 0:
                dve.wait_ge(rope_loaded, 16 * 2)
            dve_chunk(dve, st, 0, 0, None, 1, layer)
            with dve.Fori(0, B - 1) as u:
                dve_chunk(dve, st, 2 * u + 1, 1, 2 * u, 2 * u + 2, layer)
                dve_chunk(dve, st, 2 * u + 2, 0, 2 * u + 1, 2 * u + 3, layer)
            dve_chunk(dve, st, 2 * B - 1, 1, 2 * B - 2, None, layer)
            for n in range(SPC):
                dve_beside(dve, st, n, 2 * B - 1, None, 1, layer)

        def pool_rstd(pool, pc, wait, sig, k, val):
            pool.wait_ge(wait, val)
            pool.sem_inc(apart_pool, 1)
            pc.link(nc.gpsimd.tensor_scalar(rstd[:, k, :], mv[:, k, :, 1], EPS, None, ALU.add))
            nc.gpsimd.tensor_tensor(rstd[:, k, :], rstd[:, k, :], mhalf[:, :], ALU.pow).then_inc(sig, 1)

        def pool_back(pool, pc, st, c, layer):
            pool_rstd(pool, pc, st.stats2, st.rstd2, 1, c + 1)
            if layer == 0:
                for a in range(2):
                    pool.wait_ge(st.rot_done, 2 * c + a + 1)
                    nc.gpsimd.tensor_tensor(rot[2 * a][:, :], rot[2 * a][:, :], rot[2 * a + 1][:, :],
                                            ALU.add).then_inc(st.rot_sum, 1)

        def pool_end(pool, st, layer):
            pc = Chain(pool, st.pool_chain)
            for c in range(2):
                pool_rstd(pool, pc, st.stats, st.rstd, 0, c + 1)
            with pool.Fori(0, 2 * B - 2) as c:
                pc.at(2 + 2 * c)
                pool_back(pool, pc, st, c, layer)
                pool_rstd(pool, pc, st.stats, st.rstd, 0, c + 3)
            for c in (2 * B - 2, 2 * B - 1):
                pc.at(2 + 2 * (2 * B - 2) + c - (2 * B - 2))
                pool_back(pool, pc, st, c, layer)

        @block.sync
        def _(sp):
            def load_x(c):
                sp.dma_start(xs[c % 2][:, :, :], x_tiles[:, bass.ds(c * TPC, TPC), :]).then_inc(st.x_in[c % 2], 16)

            st = stages[0]
            for t, name in FIRST:
                sp.dma_start(t[tuple(slice(None) for _ in t.shape)], d[name]).then_inc(first_loaded, 16)
            load_x(0)
            load_x(1)
            for t, name in CONSTS:
                sp.dma_start(t[tuple(slice(None) for _ in t.shape)], d[name]).then_inc(const_loaded, 16)
            with sp.Fori(0, B - 1) as b:
                for hh in range(2):
                    c = 2 * b + hh
                    sp_store_pair(sp, st, c, b, hh)
                    sp.wait_ge(st.x_turned, c + 1)
                    sp.dma_start(xs[hh][:, :, :],
                                 x_tiles[:, bass.ds((c + 2) * TPC, TPC), :]).then_inc(st.x_in[hh], 16)
            for hh in range(2):
                sp_store_pair(sp, st, 2 * (B - 1) + hh, B - 1, hh)
            for hh in range(2):
                sp.wait_ge(st.pair_stored[hh], PAIR * (B + 1))
            sp.sem_inc(st.done, 1)
            sp_attention(sp, layers[0])
            sp.wait_ge(layers[0].normed, CPB * NG)
            for k, name in enumerate(("w1", "w2")):
                sp.dma_start(w_raw[k][:, :], d[name]).then_inc(raw_loaded[k], 16)
            sp.dma_start(rope_a[:, :], d["rope_a"]).then_inc(rope_loaded, 16)
            sp.dma_start(rope_b[:, :], d["rope_b"]).then_inc(rope_loaded, 16)
            st = stages[1]
            with sp.Fori(0, B) as b:
                for hh in range(2):
                    c = 2 * b + hh
                    sp_store_halves(sp, st, 1, c, b, hh)
                    sp.wait_ge(st.stored, STORES * (c + 1))
                    sp.wait_ge(st.v_saved, c + 1)
                    sp.wait_ge(st.x_kept, c + 1)
                    sp.sem_inc(st.done, 1)
            sp_attention(sp, layers[1])
            sp.wait_ge(layers[1].normed, CPB * NG)
            sp.dma_start(w_raw[0][:, :], d["we1"]).then_inc(raw_loaded[0], 16)
            sp.dma_start(we2[:, :, :], d["we2"]).then_inc(we2_loaded, 16)
            st = stages[2]
            with sp.Fori(0, 2 * B) as c:
                sp.wait_ge(st.norm2, c + 1)
                sp.dma_start(out_tiles[:, bass.ds(c * TPC, TPC), :], x_out[:, :, :]).then_inc(st.stored, 16)
                sp.wait_ge(st.stored, 16 * (c + 1))
                sp.sem_inc(st.done, 1)

        @block.gpsimd
        def _(pool):
            nc.gpsimd.memset(mhalf[:, :], -0.5).then_inc(fills, 1)
            pool.wait_ge(rows_ready, 1)
            pool.wait_ge(stages[0].done, 1)
            pool.wait_ge(stages[0].v_saved, 2 * B + 2)
            pool_attention(pool, layers[0])
            pool_end(pool, stages[1], 0)
            pool.wait_ge(stages[1].done, 2 * B + 1)
            pool_attention(pool, layers[1])
            pool_end(pool, stages[2], 1)

        @block.scalar
        def _(act):
            st = stages[0]
            with act.Fori(0, B) as u:
                for par in range(2):
                    c = 2 * u + par
                    act.wait_ge(st.x_turned, c + 1)
                    nc.scalar.activation(xt[par][:, :], bank[3 - par][:, :], ACT.Copy).then_inc(st.xt_ready, 1)
                    act.wait_ge(st.qkv_ready, c + 1)
                    act.wait_ge(st.pair_stored[par], PAIR * (u + 1))
                    for a in range(2):
                        nc.scalar.activation(qk_hi[2 * par + a][:, :].bitcast(F32R), hbank[2 * par + a],
                                             ACT.Copy).then_inc(st.halves_hi, 1)
            act.wait_ge(const_loaded, ALL_CONSTS)
            nc.scalar.activation(expert_row[:, :, :], expert_raw[:, :, :], ACT.Copy).then_inc(rows_ready, 1)
            act.wait_ge(rows_ready, 1)
            act.wait_ge(stages[0].done, 1)
            act_attention(act, layers[0])
            act.wait_ge(w_loaded, ALL_W)
            act_end(act, stages[1], 0)
            act.wait_ge(stages[1].done, 2 * B + 1)
            act_attention(act, layers[1])
            act_end(act, stages[2], 1)

        @block.vector
        def _(dve):
            for L in layers:
                dve.sem_inc(L.exp_done, NS)
                dve.sem_inc(L.pv_done, NP)
                dve.sem_inc(L.o_free, 2)
                dve.sem_inc(L.spare_free, 1)
            dve.sem_inc(layers[1].smax_free, NS)
            for layer, st in enumerate(stages[1:]):
                dve.sem_inc(st.s_done, h_banks[layer])
                dve.sem_inc(st.gbc_saved, 1)
                dve.sem_inc(st.y_saved, 1)
                dve.sem_inc(st.done, 1)
            dve.sem_inc(stages[1].u_done, NS)
            for par in range(2):
                dve.sem_inc(stages[0].pair_stored[par], PAIR)
            dve.sem_inc(stages[0].v_saved, 2)
            dve.wait_ge(fills, FILLS)
            st = stages[0]
            with dve.Fori(0, B) as u:
                for par in range(2):
                    c = 2 * u + par
                    dve.wait_ge(st.qkv_ready, c + 1)
                    for a in range(2):
                        dve.wait_ge(st.halves_hi, 2 * c + a + 1)
                        nc.vector.tensor_tensor(qk_lo[2 * par + a][:, :].bitcast(F32R), hbank[2 * par + a],
                                                qk_hi[2 * par + a][:, :], ALU.subtract).then_inc(st.halves_lo, 1)
                    nc.vector.tensor_copy(v_all[:, bass.ds(c * TPC, TPC), :],
                                          bank[par][:, :].rearrange("p (t c) -> p t c", c=D)).then_inc(st.v_saved, 1)
            dve.wait_ge(const_loaded, ALL_CONSTS)
            dve.wait_ge(rows_ready, 1)
            dve.wait_ge(stages[0].done, 1)
            dve_attention(dve, layers[0])
            dve.wait_ge(w_loaded, ALL_W)
            dve.wait_ge(layers[0].normed, CPB * NG)
            dve_end(dve, stages[1], 0)
            dve.wait_ge(stages[1].done, 2 * B + 1)
            dve_attention(dve, layers[1])
            dve.wait_ge(layers[1].normed, CPB * NG)
            dve_end(dve, stages[2], 1)

        @block.tensor
        def _(pe):
            pe.wait_ge(first_loaded, 16 * len(FIRST))
            st = stages[0]
            with pe.Fori(0, B) as u:
                for par in range(2):
                    c = 2 * u + par
                    pe.wait_ge(st.x_in[par], 16 * (u + 1))
                    pe_turn_tiles(bank[3 - par], xs[par]).then_inc(st.x_turned, 1)
                    pe.wait_ge(st.xt_ready, c + 1)
                    pe.wait_ge(st.v_saved, c + 1)
                    pe_qkv(st, w_qkv0, xt[par], par)
            pe.wait_ge(st.v_saved, 2 * B + 2)
            pe.wait_ge(const_loaded, ALL_CONSTS)
            pe_attention(pe, layers[0])
            pe.wait_ge(w_loaded, ALL_W)
            pe_end(pe, stages[1], 0)
            pe.wait_ge(stages[1].done, 2 * B + 1)
            pe_attention(pe, layers[1])
            pe_end(pe, stages[2], 1)


_IN_NAMES = ["x", "ident", "tri", "expert_row", "iota8", "w_qkv0", "w_qkv1", "w_o0", "w_o1", "rope_a",
             "rope_b", "b_o1", "wg", "w1", "w2", "w3", "rw1", "rb1", "rw2", "rb2", "we1", "be1", "we2", "be2"]


def _layout(i):
    f = np.float32
    a = {k: np.asarray(v) for k, v in i.items()}
    c = np.ascontiguousarray
    o = {"x": a["L0_attn_x"].reshape(NTOK, D), "ident": np.eye(P, dtype=f)}
    o["tri"] = np.triu(np.ones((P, P), f))
    er = np.zeros((2 * E0, E0, P), f)
    for e in range(E0):
        er[e, e] = er[E0 + e, e] = 1
    o["expert_row"] = er
    o["iota8"] = np.tile(np.arange(E0, dtype=f), (P, 1))
    w = a["L0_attn_Wqkv"].reshape(3, P, D)
    o["w_qkv0"] = c(w.transpose(2, 0, 1))
    w = a["L1_attn_w_qkv"].reshape(3, H, DK // 2, 2, D)
    rows = [np.concatenate([w[s, :, :, t], w[s, :, :, t]], axis=1).reshape(P, D) for s in range(2) for t in range(2)]
    rows.append(a["L1_attn_w_qkv"][2 * P:])
    o["w_qkv1"] = c(np.stack(rows).transpose(2, 0, 1))
    inv = (f(1.0) / np.power(f(10000.0), np.arange(0, DK, 2, dtype=f) / f(DK))).astype(f)
    ang = np.outer(np.arange(T, dtype=f), inv).astype(f)
    cos, sin = np.cos(ang).astype(f).T, np.sin(ang).astype(f).T
    o["rope_a"] = c(np.tile(np.concatenate([cos, sin]), (H, 1)))
    o["rope_b"] = c(np.tile(np.concatenate([-sin, cos]), (H, 1)))
    o["w_o0"] = c(a["L0_attn_Wout"].T)
    o["w_o1"] = c(a["L1_attn_w_out"].T)
    o["b_o1"] = a["L1_attn_b_out"].reshape(1, D)
    o["wg"] = c(a["L0_ffn_Wg"].T)
    o["w1"] = c(a["L0_ffn_W1"].transpose(2, 0, 1)).reshape(P, NH * P)
    o["w2"] = c(a["L0_ffn_W2"].transpose(2, 0, 1)).reshape(P, NH * P)
    o["w3"] = c(a["L0_ffn_W3"].transpose(2, 0, 1).reshape(F0 // P, P, E0, D).transpose(1, 2, 0, 3).reshape(P, NH, D))
    o["rw1"] = a["L1_ffn_rW1"]
    o["rb1"] = c(a["L1_ffn_rb1"].reshape(2, P).T)
    o["rw2"] = c(a["L1_ffn_rW2"].reshape(2, P, E1).transpose(1, 0, 2))
    o["rb2"] = a["L1_ffn_rb2"].reshape(1, E1)
    o["we1"] = c(a["L1_ffn_We1"].transpose(1, 0, 2)).reshape(P, NH * P)
    o["be1"] = c(a["L1_ffn_be1"].reshape(NH, P).T)
    o["we2"] = c(a["L1_ffn_We2"].reshape(NH, P, D).transpose(1, 0, 2))
    o["be2"] = np.zeros((2 * E0, D), f)
    o["be2"][0:E1] = o["be2"][E0:E0 + E1] = a["L1_ffn_be2"]
    return {k: c(o[k]) for k in _IN_NAMES}


def kernel(**inputs):
    import concourse.bacc as _bacc
    from concourse.bass_utils import run_bass_kernel_spmd as _run

    nc = _bacc.Bacc("TRN2", target_bir_lowering=False, num_devices=1)
    arrays = {f"in_{k}": v for k, v in _layout(inputs).items()}
    aps = {k: nc.dram_tensor(f"in_{k}", arrays[f"in_{k}"].shape, F32, kind="ExternalInput").ap() for k in _IN_NAMES}
    out = nc.dram_tensor("out_dram", (NTOK, D), F32, kind="ExternalOutput").ap()
    build_program(nc, aps, out)
    r = _run(nc, [arrays], core_ids=[0])
    return np.asarray(r.results[0]["out_dram"]).reshape(B, T, D)
```
